# Optimizing a Trainium2 kernel written in Bass

```python
import numpy as np
import jax
import jax.numpy as jnp

def _softmax(x, axis=-1):
    return jax.nn.softmax(x, axis=axis)

def _gelu(x):
    return jax.nn.gelu(x, approximate=True)

def _silu(x):
    return jax.nn.silu(x)

def _sigmoid(x):
    return jax.nn.sigmoid(x)

def _layernorm(x, axis=-1, eps=1e-05):
    m = jnp.mean(x, axis=axis, keepdims=True)
    v = jnp.var(x, axis=axis, keepdims=True)
    return (x - m) / jnp.sqrt(v + eps)

def _scatter_add(tgt, idx, src, axis=0):
    return tgt.at[idx].add(src)

def _segment_sum(src, seg, n):
    return jax.ops.segment_sum(src, seg, n)
kernel_name = 'mk_audio_tower_d1_tok_audfeat512_r4_2c1d9d'

def setup_inputs(seed: int=0):
    np.random.seed(seed)
    _w = jnp.asarray

    def _rec_inputs():
        import jax
        import jax.numpy as jnp
        _rk = jax.random.key(seed)
        x = -0.000520686 + 1.00062 * jax.random.normal(jax.random.fold_in(_rk, 1), (8, 32, 750), jnp.float32)
        return x
    x = _rec_inputs()

    def _L0_tok_setup():
        import jax, jax.numpy as jnp
        import numpy as np
        ALPHA = 0.1

        def ewma(y, alpha=ALPHA):
            y_t = jnp.swapaxes(y, 0, 1)

            def step(carry, xt):
                c = alpha * xt + (1.0 - alpha) * carry
                return (c, c)
            _, out = jax.lax.scan(step, y_t[0], y_t[1:])
            out = jnp.concatenate([y_t[:1], out], axis=0)
            return jnp.swapaxes(out, 0, 1)
        key = jax.random.key(seed)
        k1, k2, k3, k4, k5 = jax.random.split(key, 5)
        B, C, T, D = (32, 32, 512, 128)
        x = jax.random.normal(k1, (B, C, T), dtype=jnp.float32)
        W_ve = jax.random.normal(k2, (D, C), dtype=jnp.float32) * (1.0 / np.sqrt(C))
        b_ve = jax.random.normal(k3, (D,), dtype=jnp.float32) * 0.01
        W_lin = jax.random.normal(k4, (D, D), dtype=jnp.float32) * (1.0 / np.sqrt(D))
        b_lin = jax.random.normal(k5, (D,), dtype=jnp.float32) * 0.01
        return {'x': x, 'W_ve': W_ve, 'b_ve': b_ve, 'W_lin': W_lin, 'b_lin': b_lin}
    _L0_tok_all = _L0_tok_setup()
    _L0_tok_in = {k: v for k, v in _L0_tok_all.items() if k in ('W_ve', 'b_ve', 'W_lin', 'b_lin')}
    del _L0_tok_all

    def _L0_attn_setup():
        import jax, jax.numpy as jnp
        import numpy as np
        DIM = 128
        DIM_HEAD = 64
        HEADS = 8
        SCALE = 8.0
        DIM_INNER = DIM_HEAD * HEADS

        def _l2norm(t, axis=-1, eps=1e-12):
            return t / jnp.maximum(jnp.linalg.norm(t, axis=axis, keepdims=True), eps)
        key = jax.random.key(seed)
        k1, k2, k3, k4 = jax.random.split(key, 4)
        b, n = (8, 1024)
        x = jax.random.normal(k1, (b, n, DIM), dtype=jnp.float32)
        gamma = jnp.ones((DIM,), dtype=jnp.float32)
        w_qkv = jax.random.normal(k2, (DIM, 3 * DIM_INNER), dtype=jnp.float32) * DIM ** (-0.5)
        temperature = jnp.ones((HEADS, 1, 1), dtype=jnp.float32)
        w_out = jax.random.normal(k3, (DIM_INNER, DIM), dtype=jnp.float32) * DIM_INNER ** (-0.5)
        return {'x': x, 'gamma': gamma, 'w_qkv': w_qkv, 'temperature': temperature, 'w_out': w_out}
    _L0_attn_all = _L0_attn_setup()
    _L0_attn_in = {k: v for k, v in _L0_attn_all.items() if k in ('gamma', 'w_qkv', 'temperature', 'w_out')}
    del _L0_attn_all

    def _L0_ffn_setup():
        import jax, jax.numpy as jnp
        import numpy as np
        B, T, D, F, E, K = (8, 256, 128, 512, 8, 2)

        def _moe_forward(x, Wr, br, W1, b1, W2, b2):
            Bx, Tx, Dx = x.shape
            xf = x.reshape(-1, Dx)
            logits = xf @ Wr + br
            probs = jax.nn.softmax(logits, axis=-1)
            vals, idx = jax.lax.top_k(probs, K)
            cw = (jax.nn.one_hot(idx, E, dtype=x.dtype) * vals[..., None]).sum(axis=1)

            def body(acc, params):
                W1e, b1e, W2e, b2e, cwe = params
                h = jax.nn.relu(xf @ W1e + b1e)
                y = h @ W2e + b2e
                return (acc + cwe[:, None] * y, None)
            out, _ = jax.lax.scan(body, jnp.zeros_like(xf), (W1, b1, W2, b2, cw.T))
            return out.reshape(Bx, Tx, Dx)
        key = jax.random.key(seed)
        k0, k1, k2, k3 = jax.random.split(key, 4)
        s_d = 1.0 / np.sqrt(D)
        s_f = 1.0 / np.sqrt(F)
        return {'x': jax.random.normal(k0, (B, T, D), jnp.float32), 'Wr': jax.random.uniform(k1, (D, E), jnp.float32, -s_d, s_d), 'br': jnp.zeros((E,), jnp.float32), 'W1': jax.random.uniform(k2, (E, D, F), jnp.float32, -s_d, s_d), 'b1': jnp.zeros((E, F), jnp.float32), 'W2': jax.random.uniform(k3, (E, F, D), jnp.float32, -s_f, s_f), 'b2': jnp.zeros((E, D), jnp.float32)}
    _L0_ffn_all = _L0_ffn_setup()
    _L0_ffn_in = {k: v for k, v in _L0_ffn_all.items() if k in ('Wr', 'br', 'W1', 'b1', 'W2', 'b2')}
    del _L0_ffn_all
    return {'x': x, 'L0_tok_W_ve': _L0_tok_in['W_ve'], 'L0_tok_b_ve': _L0_tok_in['b_ve'], 'L0_tok_W_lin': _L0_tok_in['W_lin'], 'L0_tok_b_lin': _L0_tok_in['b_lin'], 'L0_attn_gamma': _L0_attn_in['gamma'], 'L0_attn_w_qkv': _L0_attn_in['w_qkv'], 'L0_attn_temperature': _L0_attn_in['temperature'], 'L0_attn_w_out': _L0_attn_in['w_out'], 'L0_ffn_Wr': _L0_ffn_in['Wr'], 'L0_ffn_br': _L0_ffn_in['br'], 'L0_ffn_W1': _L0_ffn_in['W1'], 'L0_ffn_b1': _L0_ffn_in['b1'], 'L0_ffn_W2': _L0_ffn_in['W2'], 'L0_ffn_b2': _L0_ffn_in['b2']}

def reference(x, L0_tok_W_ve, L0_tok_b_ve, L0_tok_W_lin, L0_tok_b_lin, L0_attn_gamma, L0_attn_w_qkv, L0_attn_temperature, L0_attn_w_out, L0_ffn_Wr, L0_ffn_br, L0_ffn_W1, L0_ffn_b1, L0_ffn_W2, L0_ffn_b2):
    import jax
    import jax.numpy as jnp

    def _L0_tok_ref(x, W_ve, b_ve, W_lin, b_lin):
        import jax, jax.numpy as jnp
        import numpy as np
        ALPHA = 0.1

        def ewma(y, alpha=ALPHA):
            y_t = jnp.swapaxes(y, 0, 1)

            def step(carry, xt):
                c = alpha * xt + (1.0 - alpha) * carry
                return (c, c)
            _, out = jax.lax.scan(step, y_t[0], y_t[1:])
            out = jnp.concatenate([y_t[:1], out], axis=0)
            return jnp.swapaxes(out, 0, 1)
        xt = jnp.transpose(x, (0, 2, 1))
        B, T, C = xt.shape
        x_diff = jnp.concatenate([jnp.zeros((B, 1, C), dtype=xt.dtype), xt[:, 1:, :] - xt[:, :-1, :]], axis=1)
        x_emb = jnp.einsum('btc,dc->btd', x_diff, W_ve) + b_ve
        x_lr = ewma(x_emb)
        x_rl = jnp.flip(ewma(jnp.flip(x_emb, axis=1)), axis=1)
        x_smooth = (x_lr + x_rl) * 0.5
        return jnp.einsum('btd,ed->bte', x_smooth, W_lin) + b_lin

    def _L0_attn_ref(x, gamma, w_qkv, temperature, w_out):
        import jax, jax.numpy as jnp
        import numpy as np
        DIM = 128
        DIM_HEAD = 64
        HEADS = 8
        SCALE = 8.0
        DIM_INNER = DIM_HEAD * HEADS

        def _l2norm(t, axis=-1, eps=1e-12):
            return t / jnp.maximum(jnp.linalg.norm(t, axis=axis, keepdims=True), eps)
        b, n, _ = x.shape
        xn = _l2norm(x) * DIM ** 0.5 * gamma
        qkv = xn @ w_qkv
        qkv = qkv.reshape(b, n, 3, HEADS, DIM_HEAD)
        qkv = jnp.transpose(qkv, (2, 0, 3, 4, 1))
        q, k, v = (qkv[0], qkv[1], qkv[2])
        q = _l2norm(q)
        k = _l2norm(k)
        q = q * jnp.exp(temperature)
        sim = jnp.einsum('bhdn,bhen->bhde', q, k) * SCALE
        attn = jax.nn.softmax(sim, axis=-1)
        out = jnp.einsum('bhde,bhen->bhdn', attn, v)
        out = jnp.transpose(out, (0, 3, 1, 2)).reshape(b, n, DIM_INNER)
        return out @ w_out

    def _L0_ffn_ref(x, Wr, br, W1, b1, W2, b2):
        import jax, jax.numpy as jnp
        import numpy as np
        B, T, D, F, E, K = (8, 256, 128, 512, 8, 2)

        def _moe_forward(x, Wr, br, W1, b1, W2, b2):
            Bx, Tx, Dx = x.shape
            xf = x.reshape(-1, Dx)
            logits = xf @ Wr + br
            probs = jax.nn.softmax(logits, axis=-1)
            vals, idx = jax.lax.top_k(probs, K)
            cw = (jax.nn.one_hot(idx, E, dtype=x.dtype) * vals[..., None]).sum(axis=1)

            def body(acc, params):
                W1e, b1e, W2e, b2e, cwe = params
                h = jax.nn.relu(xf @ W1e + b1e)
                y = h @ W2e + b2e
                return (acc + cwe[:, None] * y, None)
            out, _ = jax.lax.scan(body, jnp.zeros_like(xf), (W1, b1, W2, b2, cw.T))
            return out.reshape(Bx, Tx, Dx)
        return _moe_forward(x, Wr, br, W1, b1, W2, b2)
    h = _L0_tok_ref(x, L0_tok_W_ve, L0_tok_b_ve, L0_tok_W_lin, L0_tok_b_lin)
    h = h + _L0_attn_ref(_layernorm(h, axis=-1), L0_attn_gamma, L0_attn_w_qkv, L0_attn_temperature, L0_attn_w_out)
    h = h + _L0_ffn_ref(_layernorm(h, axis=-1), L0_ffn_Wr, L0_ffn_br, L0_ffn_W1, L0_ffn_b1, L0_ffn_W2, L0_ffn_b2)
    return h

_drawn_inputs = setup_inputs


def setup_inputs(seed=0):
    import zlib

    import numpy as np

    out = dict(_drawn_inputs(seed))
    spreads = {'L0_attn_gamma': (1.0, 0.2),
     'L0_attn_temperature': (1.0, 0.2),
     'L0_ffn_br': (0.0, 0.1),
     'L0_ffn_b1': (0.0, 0.469),
     'L0_ffn_b2': (0.0, 0.1)}
    factors = {}
    for name, (base, spread) in spreads.items():
        noise = np.random.default_rng([zlib.crc32(name.encode()), seed]).standard_normal(out[name].shape)
        drawn = base * np.exp(spread * noise) if base else spread * noise
        out[name] = jnp.asarray(drawn.astype(out[name].dtype))
    for name, factor in factors.items():
        out[name] = (out[name] * factor).astype(out[name].dtype)
    return out
```

```python
from contextlib import ExitStack

import concourse.bass as bass
from concourse import mybir

ALU = mybir.AluOpType
ACT = mybir.ActivationFunctionType
AX = mybir.AxisListType.X
F32 = mybir.dt.float32
F16 = mybir.dt.float16
BF16 = mybir.dt.bfloat16
I32 = mybir.dt.int32
U32 = mybir.dt.uint32

B, C, T, D = 8, 32, 750, 128
H, DH = 8, 64
HD = H * DH
HP = H // 2
E, F = 8, 512
FC = F // D
KA = C + 1
KS = 64 + KA
NT, TOK = 6, 125
NTOK = B * T
GB = 128 // C
NC2 = D + 1 + E
DECAY = 0.9
TINY2 = 1e-24
LN2 = 0.6931471805599453
UP_TOKEN, UP_HEAD = 42, 30
EPS = 1e-5

TILE = 256
BLK = TILE // 128
NTILES = (2 * NTOK + E * (TILE - 1)) // TILE
REGION = NTOK + TILE
SPARE = NTILES - 2 * NTOK // TILE + 1
ROWS = E * REGION + SPARE * TILE
TAIL = 6
ROWF = D + TAIL
KT = NTOK // TILE + 1
FAR = float(1 << 14)
WCH = 1024
WS = 16.0

CHUNKS = [(k, n) for k in ("w1", "w2", "b1") for n in range(E * F // WCH)] + [("b2", 0)]

STAGES = [
    ("tokens2", 3), ("tokens", 0), ("square", 3), ("copy_s", 0), ("var2", 3), ("var", 0), ("rho2", 3),
    ("rho", 0), ("union", 2), ("copy_u", 2), ("norm2", 3), ("kappa", 0), ("split_hi", 3), ("gram", 0),
    ("copy_gram", 0), ("pt", 2), ("copy_pt", 2), ("top2", 3), ("turn", 0), ("copy_turn", 0), ("split_lo", 3),
    ("px", 2), ("copy_px", 2), ("qk", 1), ("copy_k", 1), ("rank", 3), ("prods", 1), ("place", 3), ("norms", 1),
    ("sim", 1), ("scatter", 3), ("clamp", 1), ("roots", 1), ("scores", 1), ("exps", 1), ("probs", 1),
]
SCHEDULE = [(name, s - lag) for s in range(B + 3) for name, lag in STAGES if 0 <= s - lag < B]


def emitted_before(name, b, other):
    at = SCHEDULE.index((name, b))
    return sum(n == other for n, _ in SCHEDULE[:at])


def audio_tower(nc, x, w_ve, b_ve, w_lin, b_lin, gamma, w_qkv, temperature, w_out,
                w_r, b_r, w1, b1, w2, b2, out, rows, parts, dbg=None):
    with ExitStack() as ctx:
        def sb(name, shape, dt=F32):
            return ctx.enter_context(nc.sbuf_tensor(name, shape, dt))

        def pb(name, shape, dt=F32):
            return ctx.enter_context(nc.psum_tensor(name, shape, dt))

        def sem(name):
            return ctx.enter_context(nc.semaphore(name))

        wlin_sb = sb("wlin_sb", [D, D])
        vext = sb("vext", [D, KA])
        wve_sb = sb("wve_sb", [D, C])
        blin_sb = sb("blin_sb", [D, 1])
        gamma_sb = sb("gamma_sb", [D, 1])
        wqkv_sb = sb("wqkv_sb", [D, 3 * HD])
        wg_sb = sb("wg_sb", [D, 3 * HD])
        temp_sb = sb("temp_sb", [128, H])
        texp_sb = sb("texp_sb", [128, HP])
        wout_sb = sb("wout_sb", [128, HP, D])
        wr_sb = sb("wr_sb", [D, E])
        br_sb = sb("br_sb", [128, E])
        ident = sb("ident", [128, 128])
        ident16 = sb("ident16", [128, 128], F16)
        ones = sb("ones", [128, 128])
        ones16 = sb("ones16", [128, TILE], F16)
        tri = sb("tri", [128, 128], BF16)
        onesb = sb("onesb", [128, 128], BF16)
        cmat = sb("cmat", [D, NC2])
        wlinT = sb("wlinT", [D, D])
        wc1T = sb("wc1T", [D, KA])
        aT = sb("aT", [D, KA])
        ik = sb("ik", [KA, 2 * KA])
        qk_w = sb("qk_w", [KA, 2 * HD])
        vT = sb("vT", [128, HP, KA])
        em8 = sb("em8", [128, E])
        ebase = sb("ebase", [128, E])
        lift = sb("lift", [128, 2])
        dests = sb("dests", [TOK, B * NT, 2])

        big = sb("big", [128, 8, NT * D])
        x_sb, diff, lr, rl = (big[:, 2 * i:2 * i + 2, 0:T] for i in range(4))
        rl0 = sb("rl0", [128, 2])
        decay = sb("decay", [128, T])
        SR = sb("SR", [KS, B, T])
        R = sb("R", [KS, 2, NC2])

        sT = sb("sT", [TOK, 2, NT, KA])
        quad = sb("quad", [TOK, NT, KA])
        kap = sb("kap", [TOK, 4, NT])
        spT = sb("spT", [TOK, 2, NT, KA])
        g_sb = sb("g_sb", [KA, 2, KA])
        k_sb = sb("k_sb", [KA, 2, HD])
        prod = sb("prod", [KA, 2, 2 * HD])
        norm_c = sb("norm_c", [128, HP * DH + HP])
        norm_r = sb("norm_r", [128, HP * DH + HP])
        norm_t = sb("norm_t", [128, HP * DH + HP])
        z_sb = sb("z_sb", [128, 2, HP * DH])
        zm = sb("zm", [128, HP])
        ez = sb("ez", [128, 2, HP * DH])
        zs = sb("zs", [128, 2, HP])
        attn = sb("attn", [128, 2, HP, 128])
        u_sb = sb("u_sb", [128, 2, HP * D])
        pt_sb = sb("pt_sb", [128, 2, KA])
        sq_sb = sb("sq_sb", [TOK, NT, D])
        mean2 = sb("mean2", [TOK, NT])
        rho2 = sb("rho2", [TOK, 3, NT])
        h2 = sb("h2", [TOK, B * NT, D])
        x2 = sb("x2", [TOK, 2, NT, D])
        lg = sb("lg", [TOK, 2, NT, E])
        m12 = sb("m12", [TOK, 2, NT])
        exl = sb("exl", [TOK, 2, NT, E])
        pick = sb("pick", [TOK, 2, NT, E])
        oh = sb("oh", [TOK, 2, 2, NT, E])
        mask = sb("mask", [TOK, 2, NT, E], BF16)
        msum = sb("msum", [TOK, B + 1, E], BF16)
        mrow = sb("mrow", [TOK, E])
        sums = sb("sums", [TOK, 2, NT])
        rk = sb("rk", [TOK, NT, E])
        rk2 = sb("rk2", [TOK, 2, NT, E])
        posf = sb("posf", [TOK, 2, NT])
        pos = sb("pos", [TOK, 2, 2, NT], U32)
        xrow = sb("xrow", [TOK, 2, NT, ROWF])
        xrow16 = xrow[:, :, :, :].bitcast(F16)

        wraw = sb("wraw", [128, 2, WCH])
        w1h = sb("w1h", [128, E * F], F16)
        w1l = sb("w1l", [128, E * F], F16)
        w2h = sb("w2h", [128, E * F], F16)
        w2l = sb("w2l", [128, E * F], F16)
        b1h = sb("b1h", [128, E * F], F16)
        b2h = sb("b2h", [64, E * D], F16)
        zrow = sb("zrow", [128, BLK * ROWF])
        ksteps = sb("ksteps", [128, KT])
        tindex = sb("tindex", [128, NTILES])
        cnt = sb("cnt", [128, E])
        over = sb("over", [128, E, KT])
        tiles = sb("tiles", [128, E])
        cumend = sb("cumend", [128, E])
        past, past2 = (u_sb[:, i, 0:NTILES * E].rearrange("p (t e) -> p t e", e=E) for i in range(2))
        et = sb("et", [128, NTILES])
        et8 = sb("et8", [128, NTILES])
        cstart = sb("cstart", [128, NTILES])
        rowf = sb("rowf", [128, NTILES])
        padf = sb("padf", [128, E])
        table = sb("table", [128, NTILES, 4], I32)
        pads = sb("pads", [128, E], I32)

        xin = sb("xin", [128, 2, BLK, ROWF])
        xin16 = xin[:, :, :, :].bitcast(F16)
        over1, over2 = wqkv_sb[:, :].bitcast(F16), wg_sb[:, :].bitcast(F16)
        hhi = over1[:, 0:4 * 512].rearrange("p (u f n) -> p u f n", u=2, f=FC)
        xT = over1[:, 4 * 512:6 * 512].rearrange("p (u s n) -> p u s n", u=2, s=2)
        hlo = over2[:, 0:4 * 512].rearrange("p (u f n) -> p u f n", u=2, f=FC)
        ysb = wg_sb[:, 1024:1536].rearrange("p (u r n) -> p u r n", u=2, r=BLK)
        mine = sb("mine", [128, 2, BLK, 2])
        both = sb("both", [128, 2, BLK, 2, 2])
        cwd = sb("cwd", [128, 2, BLK, 2])
        dst = sb("dst", [128, 2, BLK], U32)

        ps_tok = pb("ps_tok", [128, 512])
        ps_small = pb("ps_small", [128, 512])
        ps_qk = pb("ps_qk", [128, 2, 512])
        ps_norm = pb("ps_norm", [128, 512])
        ps_sim = pb("ps_sim", [128, 512])
        ps_tok2 = pb("ps_tok2", [128, 2, 512])
        GRAM = ps_tok[0:KA, 2 * KA * NT:2 * KA * NT + KA]
        TOKS = ps_tok[0:TOK, 0:2 * KA * NT].rearrange("p (j k) -> p j k", k=2 * KA)
        PT = ps_small[:, 0:KA]
        PX = ps_small[0:KA, 64:64 + NC2]
        RANK = ps_small[0:TOK, 256:256 + NT * E].rearrange("p (j e) -> p j e", e=E)
        COUNT = ps_small[:, 320:320 + E]
        NQ = ps_norm[:, HP * DH:HP * DH + HP]
        NK = ps_norm[:, 0:HP * DH]
        SIM = ps_sim[:, 0:HP * DH]
        UNION = ps_qk[:, 0, :]
        TOK2 = ps_tok2[0:TOK, :, 0:3 * NC2].rearrange("p a (j n) -> p a j n", n=NC2)

        XPS = [ps_tok[:, :].bitcast(F16), ps_small[:, :].bitcast(F16)]
        HPS = [ps_qk[:, :, :].rearrange("p a n -> p (a n)"), ps_tok2[:, :, :].rearrange("p a n -> p (a n)")]
        YPS = [ps_norm[:, 0:BLK * D], ps_sim[:, 0:BLK * D]]

        wload = [sem("wload0"), sem("wload1")]
        wscaled = sem("wscaled")
        whigh = sem("whigh")
        wlow = sem("wlow")
        zeroed = sem("zeroed")
        spares = sem("spares")
        padded = sem("padded")
        count_ps = sem("count_ps")
        table_ready = sem("table_ready")
        x_in = [sem("x_in0"), sem("x_in1")]
        x_ps = sem("x_ps")
        x_sbuf = sem("x_sbuf")
        h_ps = sem("h_ps")
        h_high = sem("h_high")
        h_low = sem("h_low")
        y_ps = sem("y_ps")
        y_sbuf = sem("y_sbuf")
        weights = sem("weights")
        y_sent = [sem("y_sent0"), sem("y_sent1")]
        y_in = [sem(f"y_in{i}") for i in range(4)]
        summed = sem("summed")
        stored = [sem(f"stored{i}") for i in range(4)]
        load = {n: sem(f"load_{n}") for n in (
            "x0", "x1", "wlin", "wve", "bve", "blin", "gamma", "wqkv", "temp", "wout", "wr", "br")}
        consts = sem("consts")
        ch_pool = sem("ch_pool")
        ch_dve = sem("ch_dve")
        ch_act = sem("ch_act")
        ch_pe = sem("ch_pe")
        setup_ps = sem("setup_ps")
        setup_sb = sem("setup_sb")
        scans = sem("scans")
        smooth = sem("smooth")
        done = {name: sem(f"done_{name}") for name, _ in STAGES}
        quad_read = sem("quad_read")
        sim_read = sem("sim_read")
        h2_read = sem("h2_read")
        x2_ready = sem("x2_ready")
        lg_ready = sem("lg_ready")
        tail_ready = sem("tail_ready")
        sent = [sem("sent0"), sem("sent1")]
        dbg_sem = sem("dbg_sem")
        done["split_hi_exp"] = sem("done_exp_logits")
        setup_dve = sem("setup_dve")
        counted = sem("counted")
        weighed = sem("weighed")
        weigh1 = sem("weigh1")
        weigh2 = sem("weigh2")
        weigh3 = sem("weigh3")
        rank_read = sem("rank_read")

        def chained(semaphore):
            count = [0]

            def step(eng, ins):
                count[0] += 1
                ins.then_inc(semaphore, 1)
                eng.wait_ge(semaphore, count[0])
            return step

        def split_of(kind, n):
            at = slice(WCH * n, WCH * n + WCH)
            if kind == "w1":
                return w1h[:, at], w1l[:, at], slice(0, 128)
            if kind == "w2":
                return w2h[:, at], w2l[:, at], slice(0, 128)
            to = b1h if kind == "b1" else b2h
            return to[0:1, at], to[32:33, at], None

        block = ctx.enter_context(nc.Block())

        SETUP = ["wlinT", "wc1T", "cr", "aT", "ax", "kk", "q", "k", "v"]

        @block.sync
        def _(sp):
            for g in range(2):
                sp.dma_start(x_sb[:, g, :], x[GB * g:GB * (g + 1)].rearrange("b c t -> (b c) t")).then_inc(load[f"x{g}"], 16)
            sp.dma_start(wlin_sb[:, :], w_lin).then_inc(load["wlin"], 16)
            sp.dma_start(wve_sb[:, :], w_ve).then_inc(load["wve"], 16)
            sp.dma_start(vext[:, C:KA], b_ve.rearrange("(d a) -> d a", a=1)).then_inc(load["bve"], 16)
            sp.dma_start(blin_sb[:, :], b_lin.rearrange("(d a) -> d a", a=1)).then_inc(load["blin"], 16)
            sp.dma_start(wr_sb[:, :], w_r).then_inc(load["wr"], 16)
            sp.dma_start(gamma_sb[:, :], gamma.rearrange("(d a) -> d a", a=1)).then_inc(load["gamma"], 16)
            sp.dma_start(wqkv_sb[:, :], w_qkv).then_inc(load["wqkv"], 16)
            sp.dma_start(temp_sb[:, :], temperature.rearrange("h a b -> (a b) h").to_broadcast((128, H))).then_inc(load["temp"], 16)
            sp.dma_start(wout_sb[:, :, :], w_out.rearrange("(p r) n -> r p n", r=128)).then_inc(load["wout"], 16)
            sp.dma_start(br_sb[:, :], b_r.rearrange("(a e) -> a e", a=1).to_broadcast((128, E))).then_inc(load["br"], 16)
            w1v = w1.rearrange("e d f -> d e f")
            w2v = w2.rearrange("e (c p) n -> p e c n", p=128)
            for k, (kind, n) in enumerate(CHUNKS):
                if k >= 2:
                    sp.wait_ge(wlow, k - 1)
                raw = wraw[:, k % 2, :]
                if kind == "w1":
                    for i in range(2):
                        sp.dma_start(raw[:, F * i:F * i + F], w1v[:, 2 * n + i, :]).then_inc(wload[k % 2], 16)
                elif kind == "w2":
                    for i in range(2):
                        sp.dma_start(raw[:, F * i:F * i + F].rearrange("p (c n) -> p c n", n=D),
                                     w2v[:, 2 * n + i]).then_inc(wload[k % 2], 16)
                else:
                    src = (b1 if kind == "b1" else b2).rearrange("(a e) f -> a (e f)", a=1)[:, WCH * n:WCH * n + WCH]
                    for r in (0, 32):
                        sp.dma_start(raw[r:r + 1, :], src).then_inc(wload[k % 2], 16)
            sp.wait_ge(zeroed, 3)
            sp.dma_start(rows[E * REGION:ROWS, :].rearrange("(s p r) n -> p s (r n)", p=128, r=BLK),
                         zrow[:, :].rearrange("p (a n) -> p a n", a=1).to_broadcast((128, SPARE, BLK * ROWF))
                         ).then_inc(spares, 16)
            sp.wait_ge(table_ready, 2)
            for e in range(E):
                first = sp.value_load(pads[0:1, e:e + 1], min_val=0, max_val=E * REGION - TILE)
                sp.dma_start(rows[bass.ds(first, TILE), :].rearrange("(p r) n -> p (r n)", r=BLK),
                             zrow[:, :]).then_inc(padded, 16)
            for i in range(2):
                sp.wait_ge(sent[i], 16 * NT * B)
            sp.wait_ge(spares, 16)
            sp.wait_ge(padded, 16 * E)

            def load_tile(t, u, reused=True):
                if reused:
                    sp.wait_ge(x_ps, t - 1)
                    sp.wait_ge(weights, t - 1)
                first = sp.value_load(table[0:1, bass.ds(t, 1), 0:1], min_val=0, max_val=ROWS - TILE)
                sp.dma_start(xin[:, u].rearrange("p r n -> p (r n)"),
                             rows[bass.ds(first, TILE), :].rearrange("(p r) n -> p (r n)", r=BLK)).then_inc(x_in[u], 16)

            for u in range(2):
                load_tile(u, u, False)
            with sp.Fori(1, NTILES // 2) as i:
                for u in range(2):
                    load_tile(2 * i + u, u)

            for i in range(2):
                sp.wait_ge(y_sent[i], 16 * BLK * NTILES // 2)
            pv = parts.rearrange("(c b j p) n -> p c b j n", c=2, b=B, p=TOK)
            ov = out.rearrange("b (j p) n -> p b j n", p=TOK)
            for s in range(B + 2):
                if s < B:
                    if s >= 4:
                        sp.wait_ge(stored[s % 4], 16)
                    for c in range(2):
                        sp.dma_start(big[0:TOK, 2 * (s % 4) + c, :].rearrange("p (j n) -> p j n", n=D),
                                     pv[:, c, s]).then_inc(y_in[s % 4], 16)
                if s >= 2:
                    b = s - 2
                    sp.wait_ge(summed, b + 1)
                    sp.dma_start(ov[:, b], big[0:TOK, 2 * (b % 4), :].rearrange("p (j n) -> p j n", n=D)
                                 ).then_inc(stored[b % 4], 16)
            for i in range(4):
                sp.wait_ge(stored[i], 32)
            if dbg is not None:
                sp.wait_ge(sent[0], 16 * 12 * B // 2)
                sp.wait_ge(sent[1], 16 * 12 * B // 2)
                sp.dma_start(dbg["h2"], h2[:, :, :]).then_inc(dbg_sem, 16)
                sp.dma_start(dbg["sr"], SR[:, :, :]).then_inc(dbg_sem, 16)
                sp.dma_start(dbg["msum"], msum[:, :, :]).then_inc(dbg_sem, 16)
                sp.dma_start(dbg["lg"], lg[:, :, :, :]).then_inc(dbg_sem, 16)
                sp.dma_start(dbg["xrow"], xrow[:, :, :, :]).then_inc(dbg_sem, 16)
                sp.dma_start(dbg["pos"], pos[:, :, :, :]).then_inc(dbg_sem, 16)
                sp.wait_ge(dbg_sem, 96)

        @block.gpsimd
        def _(pool):
            step = chained(ch_pool)
            made = [0]

            def const(ins):
                made[0] += 1
                ins.then_inc(consts, 1)
                pool.wait_ge(consts, made[0])

            const(pool.memset(ones[:, :], 1.0))
            const(pool.memset(ones16[:, :], 1.0))
            const(pool.memset(onesb[:, :], 1.0))
            const(pool.memset(decay[:, :], DECAY))
            const(pool.memset(lift[:, 0:1], UP_TOKEN / 2 * LN2))
            const(pool.memset(lift[:, 1:2], UP_HEAD / 2 * LN2))
            const(pool.memset(attn[:, :, :, :], 0.0))
            const(pool.memset(msum[:, 0, :], 0.0))
            const(pool.memset(R[32:64, :, :], 0.0))
            const(pool.affine_select(out=ident[:, :], in_=ones[:, :], compare_op=ALU.is_equal, fill=0.0,
                               base=0, pattern=[[-1, 128]], channel_multiplier=1))
            const(pool.affine_select(out=ident16[:, :], in_=ones16[:, 0:128], compare_op=ALU.is_equal, fill=0.0,
                               base=0, pattern=[[-1, 128]], channel_multiplier=1))
            const(pool.affine_select(out=tri[:, :], in_=onesb[:, :], compare_op=ALU.is_gt, fill=0.0,
                               base=0, pattern=[[1, 128]], channel_multiplier=-1))
            const(pool.iota(ksteps[:, :], [[TILE, KT]], base=0, channel_multiplier=0,
                            allow_small_or_imprecise_dtypes=True))
            const(pool.iota(tindex[:, :], [[1, NTILES]], base=0, channel_multiplier=0,
                            allow_small_or_imprecise_dtypes=True))
            const(pool.iota(em8[:, :], [[1, E]], base=-E, channel_multiplier=0,
                      allow_small_or_imprecise_dtypes=True))
            const(pool.iota(ebase[:, :], [[REGION, E]], base=0, channel_multiplier=0,
                      allow_small_or_imprecise_dtypes=True))
            const(pool.iota(dests[:, :, :], [[TOK, B * NT], [NTOK, 2]], base=-int(FAR), channel_multiplier=1,
                      allow_small_or_imprecise_dtypes=True))
            step(pool, pool.memset(SR[32:64, :, :], 0.0))
            step(pool, pool.memset(SR[32:33, :, :], 1.0))
            pool.memset(zrow[:, :], 0.0).then_inc(zeroed, 1)
            pool.wait_ge(zeroed, 1)
            pool.memset(b1h[:, :], 0.0).then_inc(zeroed, 1)
            pool.wait_ge(zeroed, 2)
            pool.memset(b2h[:, :], 0.0).then_inc(zeroed, 1)
            pool.wait_ge(zeroed, 3)
            for b in range(B):
                g, i = b // GB, b % GB
                pool.wait_ge(scans, 2 * g + 2)
                pool.tensor_tensor(SR[0:C, b, :], lr[C * i:C * i + C, g, :], rl[C * i:C * i + C, g, :],
                                   ALU.add).then_inc(smooth, 1)
                pool.wait_ge(smooth, b + 1)

            for k, (kind, n) in enumerate(CHUNKS):
                pool.wait_ge(whigh, k + 1)
                high, low, r = split_of(kind, n)
                if kind[0] == "b":
                    high, r = low, slice(32, 33)
                pool.tensor_tensor(low, wraw[r, k % 2, :], high, ALU.subtract).then_inc(wlow, 1)
                pool.wait_ge(wlow, k + 1)

            def split_lo(b):
                pool.wait_ge(done["split_hi"], b + 1)
                pool.tensor_tensor(xrow16[:, b % 2, :, D:2 * D], x2[:, b % 2], xrow16[:, b % 2, :, 0:D],
                                   ALU.subtract).then_inc(done["split_lo"], 1)
                pool.wait_ge(done["split_lo"], b + 1)
                tail = xrow[:, b % 2, :, D + 4:D + 6]
                pool.tensor_copy(tail, dests[:, NT * b:NT * b + NT, :]).then_inc(tail_ready, 1)

            def scatter(b):
                pool.wait_ge(done["place"], b + 1)
                pool.wait_ge(done["split_lo"], b + 1)
                pool.wait_ge(tail_ready, b + 1)
                for c in range(2):
                    for j in range(NT):
                        pool.indirect_dma_start(
                            rows, bass.IndirectOffsetOnAxis(ap=pos[:, b % 2, c, j:j + 1], axis=0),
                            xrow[:, b % 2, j, :], None).then_inc(sent[b % 2], 16)

            for name, b in SCHEDULE:
                if name == "split_lo":
                    split_lo(b)
                elif name == "scatter":
                    scatter(b)

            def send(t, u):
                pool.wait_ge(y_sbuf, t + 1)
                pool.reg_alu(bound, pool.to_reg(t + 2 * NTOK), 2 * NTOK - 1, op=ALU.min)
                for r in range(BLK):
                    pool.indirect_dma_start(
                        parts, bass.IndirectOffsetOnAxis(ap=dst[:, u, r:r + 1], axis=0), ysb[:, u, r, :], None,
                        bounds_check=bound, oob_is_err=False).then_inc(y_sent[u], 16)

            bound = pool.alloc_register("bound")
            with pool.Fori(0, NTILES // 2) as i:
                for u in range(2):
                    send(2 * i + u, u)

        @block.scalar
        def _(act):
            step = chained(ch_act)

            def copied(n, dst, src, scale=1.0):
                act.wait_ge(setup_ps, n + 1)
                act.activation(dst, src, ACT.Copy, scale=scale).then_inc(setup_sb, 1)

            act.preload_act_table_set("natural_log_exp_and_others")
            act.wait_ge(load["temp"], 16)
            for i in range(2):
                step(act, act.activation(texp_sb[64 * i:64 * i + 64, :], temp_sb[64 * i:64 * i + 64, i::2], ACT.Exp))
            copied(0, wlinT[:, :], ps_qk[:, 0, 0:D])
            copied(1, wc1T[:, :], ps_qk[:, 1, 0:KA])
            copied(2, cmat[:, D + 1:NC2], ps_norm[:, 0:E])
            copied(3, aT[:, :], ps_sim[:, 0:KA])
            act.wait_ge(consts, 9)
            act.wait_ge(setup_ps, 5)
            act.activation(R[0:KA, 0, :], ps_tok[0:KA, 0:NC2], ACT.Copy).then_inc(setup_sb, 1)
            act.activation(R[0:KA, 1, :], ps_tok[0:KA, 0:NC2], ACT.Copy).then_inc(setup_sb, 1)
            copied(5, ik[:, KA:2 * KA], ps_small[0:KA, 0:KA], 1.0 / D)
            copied(6, qk_w[:, 0:HD], ps_qk[0:KA, 0, :])
            copied(7, qk_w[:, HD:2 * HD], ps_qk[0:KA, 1, :])
            copied(8, vT[:, :, :], ps_tok2[:, 0, 0:HP * KA].rearrange("p (h k) -> p h k", k=KA))

            act.wait_ge(zeroed, 3)
            for k, (kind, n) in enumerate(CHUNKS):
                act.wait_ge(wload[k % 2], 32 * (k // 2 + 1))
                high, low, r = split_of(kind, n)
                for r, to in ([(r, high)] if r else [(slice(0, 1), high), (slice(32, 33), low)]):
                    step(act, act.activation(wraw[r, k % 2, :], wraw[r, k % 2, :], ACT.Copy,
                                             scale=WS * WS if kind == "b2" else WS))
                    last = act.activation(to, wraw[r, k % 2, :], ACT.Copy)
                last.then_inc(whigh, 1)

            def copy_s(b):
                act.wait_ge(done["tokens"], b + 1)
                if b >= 2:
                    act.wait_ge(done["kappa"], b - 1)
                act.activation(sT[:, b % 2], TOKS[:, :, 0:KA], ACT.Copy).then_inc(done["copy_s"], 1)

            def root(dst, src, up):
                step(act, act.activation(dst, src, ACT.Ln, scale=2.0 ** up))
                n = dst.shape[0]
                bias = {0: 0.0, UP_TOKEN: lift[0:n, 0:1], UP_HEAD: lift[0:n, 1:2]}[up]
                return act.activation(dst, dst, ACT.Exp, bias=bias, scale=-0.5)

            def rho(b):
                act.wait_ge(done["var"], b + 1)
                root(kap[:, 3, :], kap[:, 2, :], UP_TOKEN).then_inc(done["rho"], 1)

            def rho2_(b):
                act.wait_ge(done["var2"], b + 1)
                root(rho2[:, 2, :], rho2[:, 1, :], 0).then_inc(done["rho2"], 1)

            def roots(b):
                act.wait_ge(done["clamp"], b + 1)
                if b >= 1:
                    act.wait_ge(sim_read, b)
                root(norm_r[:, :], norm_c[:, :], UP_HEAD).then_inc(done["roots"], 1)

            def copy_gram(b):
                act.wait_ge(done["gram"], b + 1)
                if b >= 2:
                    act.wait_ge(done["qk"], b - 1)
                act.activation(g_sb[:, b % 2, :], GRAM, ACT.Copy).then_inc(done["copy_gram"], 1)

            def copy_turn(b):
                act.wait_ge(done["turn"], b + 1)
                act.activation(SR[64:KS, b, :].rearrange("p (a t) -> p a t", a=2),
                               ps_tok2[0:KA, :, 0:3 * TOK], ACT.Copy).then_inc(done["copy_turn"], 1)

            def copy_k(b):
                act.wait_ge(done["qk"], b + 1)
                if b >= 2:
                    act.wait_ge(done["sim"], b - 1)
                    act.wait_ge(done["prods"], 2 * (b - 1))
                act.activation(k_sb[:, b % 2, :], ps_qk[0:KA, 1, :], ACT.Copy).then_inc(done["copy_k"], 1)

            def exps(b):
                act.wait_ge(done["scores"], b + 1)
                if b >= 2:
                    act.wait_ge(done["probs"], b - 1)
                act.activation(ez[:, b % 2, :], z_sb[:, b % 2, :], ACT.Exp).then_inc(done["exps"], 1)

            def copy_u(b):
                act.wait_ge(done["union"], b + 1)
                if b >= 2:
                    act.wait_ge(done["pt"], b - 1)
                act.activation(u_sb[:, b % 2, :], UNION, ACT.Copy).then_inc(done["copy_u"], 1)

            def copy_pt(b):
                act.wait_ge(done["pt"], b + 1)
                if b >= 2:
                    act.wait_ge(done["px"], b - 1)
                act.activation(pt_sb[:, b % 2, :], PT, ACT.Copy).then_inc(done["copy_pt"], 1)

            def copy_px(b):
                act.wait_ge(done["px"], b + 1)
                if b >= 2:
                    act.wait_ge(done["tokens2"], b - 1)
                act.activation(R[64:KS, b % 2, :], PX, ACT.Copy).then_inc(done["copy_px"], 1)

            def square(b):
                act.wait_ge(done["tokens2"], b + 1)
                if b >= 1:
                    act.wait_ge(h2_read, b)
                act.activation(sq_sb[:, :, :].rearrange("p (a j) n -> p a j n", a=2), TOK2[:, :, :, 0:D],
                               ACT.Square).then_inc(done["square"], 1)

            def split_hi(b):
                act.wait_ge(x2_ready, b + 1)
                if b >= 2:
                    act.wait_ge(sent[b % 2], 16 * 2 * NT * (b // 2))
                act.activation(xrow16[:, b % 2, :, 0:D], x2[:, b % 2], ACT.Copy).then_inc(done["split_hi"], 1)
                act.wait_ge(lg_ready, b + 1)
                if b >= 2:
                    act.wait_ge(done["top2"], b - 1)
                act.activation(exl[:, b % 2], lg[:, b % 2], ACT.Exp).then_inc(done["split_hi_exp"], 1)

            here = dict(copy_s=copy_s, rho=rho, rho2=rho2_, roots=roots, copy_gram=copy_gram, copy_turn=copy_turn, copy_k=copy_k, exps=exps,
                        copy_u=copy_u, copy_pt=copy_pt, copy_px=copy_px, square=square, split_hi=split_hi)
            for name, b in SCHEDULE:
                if name in here:
                    here[name](b)

            def copy_x(t, u, reused=True):
                act.wait_ge(x_ps, t + 1)
                if reused:
                    act.wait_ge(h_ps, t - 1)
                act.activation(xT[:, u].rearrange("p s n -> p (s n)"), XPS[u][:, 0:2 * TILE], ACT.Copy).then_inc(x_sbuf, 1)

            def high(t, u, reused=True):
                act.wait_ge(h_ps, t + 1)
                if reused:
                    act.wait_ge(y_ps, t - 1)
                act.activation(hhi[:, u].rearrange("p f n -> p (f n)"), HPS[u], ACT.Relu).then_inc(h_high, 1)

            for u in range(2):
                copy_x(u, u, False)
            for u in range(2):
                high(u, u, False)
                copy_x(u + 2, u)
            with act.Fori(1, NTILES // 2 - 1) as i:
                for u in range(2):
                    high(2 * i + u, u)
                    copy_x(2 * i + u + 2, u)
            for u in range(2):
                high(NTILES - 2 + u, u)

        @block.vector
        def _(dve):
            step = chained(ch_dve)
            for g in range(2):
                step(dve, dve.memset(diff[:, g, 0:1], 0.0))
                dve.wait_ge(load[f"x{g}"], 16)
                step(dve, dve.tensor_tensor(diff[:, g, 1:T], x_sb[:, g, 1:T], x_sb[:, g, 0:T - 1], ALU.subtract))
                step(dve, dve.tensor_scalar(rl0[:, g:g + 1], diff[:, g, T - 1:T], 10.0, None, ALU.mult))
                dve.wait_ge(consts, 9)
                dve.tensor_tensor_scan(lr[:, g, :], decay[:, :], diff[:, g, :], 0.0, ALU.mult,
                                       ALU.add).then_inc(scans, 1)
                dve.tensor_tensor_scan(rl[:, g, ::-1], decay[:, :], diff[:, g, ::-1], rl0[:, g:g + 1],
                                       ALU.mult, ALU.add).then_inc(scans, 1)
                if g == 0:
                    dve.wait_ge(load["wve"], 16)
                    dve.wait_ge(load["bve"], 16)
                    dve.tensor_scalar(vext[:, 0:C], wve_sb[:, :], 0.05, None, ALU.mult).then_inc(setup_dve, 1)
                    dve.wait_ge(consts, 12)
                    dve.tensor_scalar(cmat[:, 0:D], ident[:, :], 1.0 / D, None, ALU.subtract).then_inc(setup_dve, 1)
                    dve.tensor_scalar(cmat[:, D:D + 1], ones[:, 0:1], 1.0 / D, None, ALU.mult).then_inc(setup_dve, 1)
                    dve.tensor_copy(ik[:, 0:KA], ident[0:KA, 0:KA]).then_inc(setup_dve, 1)
                    dve.wait_ge(load["gamma"], 16)
                    dve.wait_ge(load["wqkv"], 16)
                    dve.tensor_scalar(wg_sb[:, :], wqkv_sb[:, :], gamma_sb[:, :], None, ALU.mult).then_inc(setup_dve, 1)
                    dve.wait_ge(load["blin"], 16)
                    dve.wait_ge(setup_sb, 2)
                    dve.tensor_tensor(wc1T[:, C:KA], wc1T[:, C:KA], blin_sb[:, :], ALU.add).then_inc(setup_dve, 1)

            def var(b):
                dve.wait_ge(done["copy_s"], b + 1)
                if b >= 1:
                    dve.wait_ge(done["kappa"], b)
                dve.tensor_tensor(quad[:, :, :], TOKS[:, :, KA:2 * KA], sT[:, b % 2], ALU.mult).then_inc(quad_read, 1)
                dve.wait_ge(quad_read, b + 1)
                step(dve, dve.tensor_reduce(kap[:, 0, :], quad[:, :, :], AX, ALU.add))
                step(dve, dve.tensor_scalar(kap[:, 1, :], kap[:, 0, :], EPS, TINY2 / D, ALU.add, ALU.mult))
                dve.tensor_tensor(kap[:, 2, :], kap[:, 0, :], kap[:, 1, :], ALU.max).then_inc(done["var"], 1)

            def polish(y, square, t):
                step(dve, dve.tensor_tensor(t, y, y, ALU.mult))
                step(dve, dve.scalar_tensor_tensor(t, t, -0.5, square, ALU.mult, ALU.mult))
                step(dve, dve.scalar_tensor_tensor(y, t, 1.5, y, ALU.add, ALU.mult))

            def kappa(b):
                dve.wait_ge(done["rho"], b + 1)
                polish(kap[:, 3, :], kap[:, 2, :], kap[:, 1, :])
                if b >= 2:
                    dve.wait_ge(done["turn"], b - 1)
                dve.tensor_tensor(spT[:, b % 2], sT[:, b % 2],
                                  kap[:, 3, :].rearrange("p (j a) -> p j a", a=1).to_broadcast((TOK, NT, KA)),
                                  ALU.mult).then_inc(done["kappa"], 1)

            def prods(b):
                dve.wait_ge(done["qk"], b + 1)
                if b >= 2:
                    dve.wait_ge(done["norms"], b - 1)
                dve.tensor_tensor(prod[:, b % 2, 0:HD], ps_qk[0:KA, 0, :], qk_w[:, 0:HD],
                                  ALU.mult).then_inc(done["prods"], 1)
                dve.wait_ge(done["copy_k"], b + 1)
                dve.tensor_tensor(prod[:, b % 2, HD:2 * HD], k_sb[:, b % 2, :], qk_w[:, HD:2 * HD],
                                  ALU.mult).then_inc(done["prods"], 1)

            def clamp(b):
                dve.wait_ge(done["norms"], b + 1)
                dve.tensor_scalar(norm_c[:, :], ps_norm[:, 0:HP * DH + HP], TINY2, None,
                                  ALU.max).then_inc(done["clamp"], 1)

            def scores(b):
                dve.wait_ge(done["roots"], b + 1)
                nk, nq, z = norm_r[:, 0:HP * DH], norm_r[:, HP * DH:HP * DH + HP], z_sb[:, b % 2, :]
                z3 = z.rearrange("p (h e) -> p h e", h=HP)
                wide = lambda a: a.rearrange("p (h e) -> p h e", e=1).to_broadcast((128, HP, DH))
                polish(norm_r[:, :], norm_c[:, :], norm_t[:, :])
                if b == 0:
                    dve.wait_ge(ch_act, 2)
                step(dve, dve.scalar_tensor_tensor(nq, nq, 8.0, texp_sb[:, :], ALU.mult, ALU.mult))
                dve.wait_ge(done["sim"], b + 1)
                if b >= 2:
                    dve.wait_ge(done["exps"], b - 1)
                dve.tensor_tensor(z, SIM, nk, ALU.mult).then_inc(sim_read, 1)
                dve.wait_ge(sim_read, b + 1)
                step(dve, dve.tensor_tensor(z3, z3, wide(nq), ALU.mult))
                step(dve, dve.tensor_reduce(zm[:, :], z3, AX, ALU.max))
                dve.tensor_tensor(z3, z3, wide(zm[:, :]), ALU.subtract).then_inc(done["scores"], 1)

            def probs(b):
                dve.wait_ge(done["exps"], b + 1)
                e3 = ez[:, b % 2, :].rearrange("p (h e) -> p h e", h=HP)
                step(dve, dve.tensor_reduce(zs[:, b % 2, :], e3, AX, ALU.add))
                step(dve, dve.reciprocal(zs[:, b % 2, :], zs[:, b % 2, :]))
                if b >= 2:
                    dve.wait_ge(done["union"], b - 1)
                for i in range(2):
                    r = slice(64 * i, 64 * i + 64)
                    dve.tensor_tensor(attn[r, b % 2, :, r], e3[r], zs[r, b % 2, :].rearrange(
                        "p (h e) -> p h e", e=1).to_broadcast((64, HP, DH)), ALU.mult).then_inc(done["probs"], 1)

            def var2(b):
                dve.wait_ge(done["square"], b + 1)
                wide = lambda a, n: a.rearrange("p (a j k) -> p a j k", a=2, k=1).to_broadcast((TOK, 2, 3, n))
                four = lambda t: t.rearrange("p (a j) n -> p a j n", a=2)
                step(dve, dve.tensor_copy(mean2[:, :].rearrange("p (a j) -> p a j", a=2), TOK2[:, :, :, D]))
                step(dve, dve.tensor_tensor(four(h2[:, NT * b:NT * b + NT, :]), TOK2[:, :, :, 0:D],
                                            wide(mean2[:, :], D), ALU.add))
                dve.tensor_reduce(rho2[:, 0, :], sq_sb[:, :, :], AX, ALU.add).then_inc(h2_read, 1)
                dve.wait_ge(h2_read, b + 1)
                dve.tensor_scalar(rho2[:, 1, :], rho2[:, 0, :], 1.0 / D, EPS, ALU.mult,
                                  ALU.add).then_inc(done["var2"], 1)

            def norm2(b):
                wide = lambda a, n: a.rearrange("p (a j k) -> p a j k", a=2, k=1).to_broadcast((TOK, 2, 3, n))
                four = lambda t: t.rearrange("p (a j) n -> p a j n", a=2)
                dve.wait_ge(done["rho2"], b + 1)
                polish(rho2[:, 2, :], rho2[:, 1, :], rho2[:, 0, :])
                if b >= 2:
                    dve.wait_ge(done["split_lo"], b - 1)
                dve.tensor_tensor(four(x2[:, b % 2]), TOK2[:, :, :, 0:D], wide(rho2[:, 2, :], D),
                                  ALU.mult).then_inc(x2_ready, 1)
                if b >= 2:
                    dve.wait_ge(done["split_hi_exp"], b - 1)
                dve.tensor_tensor(four(lg[:, b % 2]), TOK2[:, :, :, D + 1:NC2], wide(rho2[:, 2, :], E),
                                  ALU.mult).then_inc(done["norm2"], 1)
                dve.wait_ge(done["norm2"], b + 1)
                if b == 0:
                    dve.wait_ge(load["br"], 16)
                bias = br_sb[0:TOK, :].rearrange("p (j e) -> p j e", j=1).to_broadcast((TOK, NT, E))
                step(dve, dve.tensor_tensor(lg[:, b % 2], lg[:, b % 2], bias, ALU.add))
                step(dve, dve.tensor_reduce(m12[:, 0, :], lg[:, b % 2], AX, ALU.max))
                wide8 = m12[:, 0, :].rearrange("p (j a) -> p j a", a=1).to_broadcast((TOK, NT, E))
                dve.tensor_tensor(lg[:, b % 2], lg[:, b % 2], wide8, ALU.subtract).then_inc(lg_ready, 1)
                dve.wait_ge(lg_ready, b + 1)

            def top2(b):
                l, o, tail = lg[:, b % 2], oh[:, b % 2], xrow[:, b % 2, :, D:ROWF]
                wide = lambda a: a.to_broadcast((TOK, NT, E))
                ids = em8[0:TOK, :].rearrange("p (j e) -> p j e", j=1).to_broadcast((TOK, NT, E))
                if b >= 2:
                    dve.wait_ge(sent[b % 2], 16 * 2 * NT * (b // 2))
                if b >= 1:
                    dve.wait_ge(done["top2"], b)
                step(dve, dve.scalar_tensor_tensor(pick[:, 0], l, 0.0, ids, ALU.is_ge, ALU.mult))
                step(dve, dve.tensor_reduce(tail[:, :, 0:1], pick[:, 0], AX, ALU.min))
                step(dve, dve.tensor_tensor(o[:, 0], ids, wide(tail[:, :, 0:1]), ALU.is_equal))
                step(dve, dve.scalar_tensor_tensor(pick[:, 0], o[:, 0], -1e30, l, ALU.mult, ALU.add))
                step(dve, dve.tensor_reduce(m12[:, 1, :], pick[:, 0], AX, ALU.max))
                step(dve, dve.tensor_tensor(pick[:, 1], pick[:, 0], wide(m12[:, 1, :].rearrange(
                    "p (j a) -> p j a", a=1)), ALU.is_equal))
                step(dve, dve.tensor_tensor(pick[:, 1], pick[:, 1], ids, ALU.mult))
                step(dve, dve.tensor_reduce(tail[:, :, 1:2], pick[:, 1], AX, ALU.min))
                step(dve, dve.tensor_tensor(o[:, 1], ids, wide(tail[:, :, 1:2]), ALU.is_equal))
                dve.tensor_tensor(mask[:, b % 2], o[:, 0], o[:, 1], ALU.add).then_inc(done["top2"], 1)
                dve.wait_ge(done["top2"], b + 1)
                step(dve, dve.tensor_reduce(mrow[:, :], mask[:, b % 2].rearrange("p j e -> p e j"), AX, ALU.add))
                dve.tensor_tensor(msum[:, b + 1, :], mrow[:, :], msum[:, b, :], ALU.add).then_inc(counted, 1)
                dve.wait_ge(done["split_hi_exp"], b + 1)
                step(dve, dve.tensor_reduce(sums[:, 0, :], exl[:, b % 2], AX, ALU.add))
                step(dve, dve.tensor_tensor(pick[:, 0], exl[:, b % 2], o[:, 1], ALU.mult))
                step(dve, dve.tensor_reduce(sums[:, 1, :], pick[:, 0], AX, ALU.add))
                step(dve, dve.tensor_scalar(sums[:, 0, :], sums[:, 0, :], WS * WS, None, ALU.mult))
                step(dve, dve.reciprocal(tail[:, :, 2], sums[:, 0, :]))
                dve.tensor_tensor(tail[:, :, 3], sums[:, 1, :], tail[:, :, 2], ALU.mult).then_inc(weighed, 1)

            def place(b):
                dve.wait_ge(done["rank"], b + 1)
                base = ebase[0:TOK, :].rearrange("p (j e) -> p j e", j=1).to_broadcast((TOK, NT, E))
                dve.tensor_tensor(rk[:, :, :], RANK, base, ALU.add).then_inc(rank_read, 1)
                dve.wait_ge(rank_read, b + 1)
                for c in range(2):
                    step(dve, dve.tensor_tensor(rk2[:, c], oh[:, b % 2, c], rk[:, :, :], ALU.mult))
                step(dve, dve.tensor_reduce(posf[:, :, :], rk2[:, :, :, :], AX, ALU.add))
                if b >= 2:
                    dve.wait_ge(sent[b % 2], 16 * 2 * NT * (b // 2))
                dve.wait_ge(weighed, b + 1)
                dve.tensor_copy(pos[:, b % 2], posf[:, :, :]).then_inc(done["place"], 1)

            here = dict(var=var, kappa=kappa, prods=prods, clamp=clamp, var2=var2, scores=scores, probs=probs, norm2=norm2, top2=top2, place=place)
            for name, b in SCHEDULE:
                if name in here:
                    here[name](b)

            dve.wait_ge(count_ps, 1)
            mid = lambda a, n: a.rearrange("p (e k) -> p e k", k=1).to_broadcast((128, a.shape[1], n))
            last = lambda a, n: a.rearrange("p (e k) -> p e k", e=1).to_broadcast((128, n, a.shape[1]))
            step(dve, dve.tensor_copy(cnt[:, :], COUNT))
            step(dve, dve.tensor_tensor(over[:, :, :], mid(cnt[:, :], KT), last(ksteps[:, :], E), ALU.is_gt))
            step(dve, dve.tensor_reduce(tiles[:, :], over[:, :, :], AX, ALU.add))
            step(dve, dve.tensor_tensor(padf[:, :], cnt[:, :], ebase[:, :], ALU.add))
            dve.tensor_copy(pads[:, :], padf[:, :]).then_inc(table_ready, 1)
            step(dve, dve.tensor_tensor_scan(cumend[:, :], ones[:, 0:E], tiles[:, :], 0.0, ALU.mult, ALU.add))
            step(dve, dve.tensor_tensor(past[:, :, :], mid(tindex[:, :], E), last(cumend[:, :], NTILES), ALU.is_ge))
            step(dve, dve.tensor_reduce(et[:, :], past[:, :, :], AX, ALU.add))
            step(dve, dve.tensor_tensor(past2[:, :, :], past[:, :, :], last(tiles[:, :], NTILES), ALU.mult))
            step(dve, dve.tensor_reduce(cstart[:, :], past2[:, :, :], AX, ALU.add))
            step(dve, dve.tensor_tensor(cstart[:, :], tindex[:, :], cstart[:, :], ALU.subtract))
            step(dve, dve.tensor_scalar(rowf[:, :], et[:, :], float(REGION), None, ALU.mult))
            step(dve, dve.scalar_tensor_tensor(rowf[:, :], cstart[:, :], float(TILE), rowf[:, :], ALU.mult, ALU.add))
            step(dve, dve.tensor_scalar(et8[:, :], et[:, :], float(E), None, ALU.subtract))
            step(dve, dve.tensor_copy(table[:, :, 0], rowf[:, :]))
            step(dve, dve.tensor_scalar(rowf[:, :], et[:, :], float(E - 1), float(F), ALU.min, ALU.mult))
            step(dve, dve.tensor_copy(table[:, :, 1], rowf[:, :]))
            step(dve, dve.tensor_scalar(rowf[:, :], et[:, :], float(E - 1), float(D), ALU.min, ALU.mult))
            dve.tensor_copy(table[:, :, 2], rowf[:, :]).then_inc(table_ready, 1)

            def weigh(t, i, u, reused=True):
                dve.wait_ge(x_in[u], 16 * i + 16)
                if reused:
                    dve.wait_ge(y_sent[u], 16 * BLK * i)
                tail = xin[:, u, :, D:ROWF]
                dve.tensor_scalar(mine[:, u], tail[:, :, 0:2], et8[:, bass.ds(t, 1)], None,
                                  ALU.is_equal).then_inc(weigh1, 1)
                dve.wait_ge(weigh1, t + 1)
                for q in range(2):
                    ins = dve.tensor_tensor(both[:, u, :, q], tail[:, :, 2 + 2 * q:4 + 2 * q], mine[:, u], ALU.mult)
                ins.then_inc(weigh2, 1)
                dve.wait_ge(weigh2, t + 1)
                dve.tensor_reduce(cwd[:, u], both[:, u], AX, ALU.add).then_inc(weigh3, 1)
                dve.wait_ge(weigh3, t + 1)
                dve.tensor_scalar(dst[:, u], cwd[:, u, :, 1], FAR, None, ALU.add).then_inc(weights, 1)

            def low(t, u, reused=True):
                dve.wait_ge(h_high, t + 1)
                if reused:
                    dve.wait_ge(y_ps, t - 1)
                dve.scalar_tensor_tensor(hlo[:, u].rearrange("p f n -> p (f n)"), HPS[u], 0.0,
                                         hhi[:, u].rearrange("p f n -> p (f n)"), ALU.max,
                                         ALU.subtract).then_inc(h_low, 1)

            def scale_y(t, u):
                dve.wait_ge(y_ps, t + 1)
                dve.tensor_tensor(ysb[:, u], YPS[u].rearrange("p (r n) -> p r n", n=D),
                                  cwd[:, u, :, 0:1].to_broadcast((128, BLK, D)), ALU.mult).then_inc(y_sbuf, 1)

            weigh(0, 0, 0, False)
            low(0, 0, False)
            weigh(1, 0, 1, False)
            low(1, 1, False)
            scale_y(0, 0)
            with dve.Fori(1, NTILES // 2) as i:
                weigh(2 * i, i, 0)
                low(2 * i, 0)
                scale_y(2 * i - 1, 1)
                weigh(2 * i + 1, i, 1)
                low(2 * i + 1, 1)
                scale_y(2 * i, 0)
            scale_y(NTILES - 1, 1)

            for b in range(B):
                dve.wait_ge(y_in[b % 4], 32 * (b // 4 + 1))
                y1, y2 = big[0:TOK, 2 * (b % 4), :], big[0:TOK, 2 * (b % 4) + 1, :]
                h = h2[:, NT * b:NT * b + NT, :].rearrange("p j n -> p (j n)")
                step(dve, dve.tensor_tensor(y1, y1, y2, ALU.add))
                dve.tensor_tensor(y1, y1, h, ALU.add).then_inc(summed, 1)

        @block.tensor
        def _(pe):
            def made(ins):
                ins.then_inc(setup_ps, 1)

            pe.wait_ge(consts, 17)
            pe.wait_ge(load["wlin"], 16)
            made(pe.transpose(ps_qk[:, 0, 0:D], wlin_sb[:, :], ident[:, :]))
            pe.wait_ge(setup_sb, 1)
            pe.wait_ge(setup_dve, 4)
            made(pe.matmul(ps_qk[:, 1, 0:KA], lhsT=wlinT[:, :], rhs=vext[:, :], start=True, stop=True))
            pe.wait_ge(load["wr"], 16)
            made(pe.matmul(ps_norm[:, 0:E], lhsT=cmat[:, 0:D], rhs=wr_sb[:, :], start=True, stop=True))
            pe.wait_ge(setup_dve, 6)
            made(pe.matmul(ps_sim[:, 0:KA], lhsT=cmat[:, 0:D], rhs=wc1T[:, :], start=True, stop=True))
            pe.wait_ge(setup_sb, 4)
            made(pe.matmul(ps_tok[0:KA, 0:NC2], lhsT=wc1T[:, :], rhs=cmat[:, :], start=True, stop=True))
            made(pe.matmul(ps_small[0:KA, 0:KA], lhsT=aT[:, :], rhs=aT[:, :], start=True, stop=True))
            for i in range(2):
                made(pe.matmul(ps_qk[0:KA, i, :], lhsT=aT[:, :], rhs=wg_sb[:, HD * i:HD * i + HD], start=True, stop=True))
            for p in range(HP):
                last = pe.matmul(ps_tok2[:, 0, KA * p:KA * p + KA], lhsT=wg_sb[:, 2 * HD + 128 * p:2 * HD + 128 * p + 128],
                                 rhs=aT[:, :], start=True, stop=True)
            made(last)
            pe.wait_ge(setup_sb, 10)
            pe.wait_ge(load["wout"], 16)

            def tokens(b):
                pe.wait_ge(smooth, b + 1)
                if b == 0:
                    pe.wait_ge(ch_pool, 2)
                if b >= 1:
                    pe.wait_ge(done["copy_gram"], b)
                for j in range(NT):
                    last = pe.matmul(TOKS[:, j, :], lhsT=SR[0:KA, b, TOK * j:TOK * j + TOK], rhs=ik[:, :],
                                     start=True, stop=True)
                last.then_inc(done["tokens"], 1)

            def gram(b):
                pe.wait_ge(done["kappa"], b + 1)
                for j in range(NT):
                    last = pe.matmul(GRAM, lhsT=spT[:, b % 2, j, :], rhs=spT[:, b % 2, j, :],
                                     start=(j == 0), stop=(j == NT - 1))
                last.then_inc(done["gram"], 1)

            def turn(b):
                n2 = emitted_before("turn", b, "tokens2")
                if n2:
                    pe.wait_ge(done["norm2"], n2)
                if b >= 1:
                    pe.wait_ge(done["copy_turn"], b)
                for j in range(NT):
                    last = pe.transpose(ps_tok2[0:KA, j // 3, TOK * (j % 3):TOK * (j % 3) + TOK],
                                        spT[:, b % 2, j, :], ident[0:TOK, 0:TOK])
                last.then_inc(done["turn"], 1)

            def qk(b):
                pe.wait_ge(done["copy_gram"], b + 1)
                if b >= 1:
                    pe.wait_ge(done["prods"], 2 * b)
                    pe.wait_ge(done["copy_k"], b)
                nu = emitted_before("qk", b, "union")
                if nu:
                    pe.wait_ge(done["copy_u"], nu)
                for i in range(2):
                    last = pe.matmul(ps_qk[0:KA, i, :], lhsT=g_sb[:, b % 2, :], rhs=qk_w[:, HD * i:HD * i + HD],
                                     start=True, stop=True)
                last.then_inc(done["qk"], 1)

            def norms(b):
                pe.wait_ge(done["prods"], 2 * b + 2)
                if b >= 1:
                    pe.wait_ge(done["clamp"], b)
                for p in range(HP):
                    pe.matmul(NQ[:, p:p + 1], lhsT=prod[:, b % 2, 128 * p:128 * p + 128], rhs=ones[0:KA, 0:1],
                              start=True, stop=True)
                kp = prod[:, b % 2, HD:2 * HD].rearrange("k (p i e) -> k i p e", i=2, e=DH)
                for i in range(2):
                    last = pe.matmul(NK[64 * i:64 * i + 64, :], lhsT=ones[0:KA, 0:64], rhs=kp[:, i], start=True, stop=True)
                last.then_inc(done["norms"], 1)

            def sim(b):
                pe.wait_ge(done["copy_k"], b + 1)
                if b >= 1:
                    pe.wait_ge(sim_read, b)
                for h in range(H):
                    i, p = h % 2, h // 2
                    last = pe.matmul(SIM[64 * i:64 * i + 64, DH * p:DH * p + DH], lhsT=qk_w[:, DH * h:DH * h + DH],
                                     rhs=k_sb[:, b % 2, DH * h:DH * h + DH], start=True, stop=True)
                last.then_inc(done["sim"], 1)

            def union(b):
                pe.wait_ge(done["probs"], 2 * b + 2)
                pe.wait_ge(done["prods"], 2 * emitted_before("union", b, "prods"))
                if b >= 1:
                    pe.wait_ge(done["copy_u"], b)
                for p in range(HP):
                    last = pe.matmul(UNION[:, D * p:D * p + D], lhsT=attn[:, b % 2, p, :], rhs=wout_sb[:, p, :],
                                     start=True, stop=True)
                last.then_inc(done["union"], 1)

            def bank_small(name, b):
                n = emitted_before(name, b, "px")
                if n:
                    pe.wait_ge(done["copy_px"], n)
                n = emitted_before(name, b, "rank")
                if n:
                    pe.wait_ge(rank_read, n)

            def pt(b):
                pe.wait_ge(done["copy_u"], b + 1)
                bank_small("pt", b)
                for p in range(HP):
                    last = pe.matmul(PT, lhsT=u_sb[:, b % 2, D * p:D * p + D], rhs=vT[:, p, :],
                                     start=(p == 0), stop=(p == HP - 1))
                last.then_inc(done["pt"], 1)

            def px(b):
                pe.wait_ge(done["copy_pt"], b + 1)
                pe.matmul(PX, lhsT=pt_sb[:, b % 2, :], rhs=cmat[:, :], start=True, stop=True).then_inc(done["px"], 1)

            def tokens2(b):
                pe.wait_ge(done["copy_px"], b + 1)
                pe.wait_ge(done["copy_turn"], emitted_before("tokens2", b, "turn"))
                if b >= 1:
                    pe.wait_ge(done["norm2"], b)
                    pe.wait_ge(done["square"], b)
                for j in range(NT):
                    last = pe.matmul(TOK2[:, j // 3, j % 3, :], lhsT=SR[:, b, TOK * j:TOK * j + TOK], rhs=R[:, b % 2, :],
                                     start=True, stop=True)
                last.then_inc(done["tokens2"], 1)

            def rank(b):
                pe.wait_ge(done["top2"], b + 1)
                if b >= 1:
                    pe.wait_ge(counted, b)
                bank_small("rank", b)
                pe.matmul(RANK, lhsT=tri[0:TOK, 0:TOK], rhs=mask[:, b % 2], start=True, stop=False)
                for j in range(NT - 1):
                    pe.matmul(RANK[:, j + 1:NT, :], lhsT=onesb[0:TOK, 0:TOK],
                              rhs=mask[:, b % 2, j:j + 1, :].to_broadcast((TOK, NT - 1 - j, E)), start=False, stop=False)
                pe.matmul(RANK, lhsT=onesb[0:TOK, 0:TOK],
                          rhs=msum[:, b:b + 1, :].to_broadcast((TOK, NT, E)), start=False,
                          stop=True).then_inc(done["rank"], 1)

            here = dict(tokens=tokens, gram=gram, turn=turn, qk=qk, norms=norms, sim=sim, union=union, pt=pt,
                        px=px, tokens2=tokens2, rank=rank)
            for name, b in SCHEDULE:
                if name in here:
                    here[name](b)

            pe.wait_ge(counted, B)
            pe.wait_ge(rank_read, B)
            pe.matmul(COUNT, lhsT=onesb[0:TOK, :], rhs=msum[:, B, :], start=True, stop=True).then_inc(count_ps, 1)
            pe.wait_ge(table_ready, 2)
            pe.wait_ge(wlow, len(CHUNKS))

            def turn_x(t, i, u, reused=True):
                pe.wait_ge(x_in[u], 16 * i + 16)
                if reused:
                    pe.wait_ge(x_sbuf, t - 1)
                for s in range(2):
                    for r in range(BLK):
                        last = pe.transpose(XPS[u][:, TILE * s + 128 * r:TILE * s + 128 * r + 128],
                                            xin16[:, u, r, D * s:D * s + D], ident16[:, :])
                last.then_inc(x_ps, 1)

            def hidden(t, u, reused=True):
                at = pe.value_load(table[0:1, bass.ds(t, 1), 1:2], min_val=0, max_val=(E - 1) * F)
                pe.wait_ge(x_sbuf, t + 1)
                if reused:
                    pe.wait_ge(h_low, t - 1)
                for f in range(FC):
                    to = HPS[u][:, TILE * f:TILE * f + TILE]
                    cols = bass.ds(at + 128 * f, 128)
                    pe.matmul(to, lhsT=w1h[:, cols], rhs=xT[:, u, 0, :], start=True, stop=False)
                    pe.matmul(to, lhsT=w1h[:, cols], rhs=xT[:, u, 1, :], start=False, stop=False)
                    pe.matmul(to, lhsT=w1l[:, cols], rhs=xT[:, u, 0, :], start=False, stop=False)
                    last = pe.matmul(to, lhsT=b1h[:, cols], rhs=ones16[:, :], start=False, stop=True)
                last.then_inc(h_ps, 1)

            def result(t, u, reused=True):
                at = pe.value_load(table[0:1, bass.ds(t, 1), 1:2], min_val=0, max_val=(E - 1) * F)
                at2 = pe.value_load(table[0:1, bass.ds(t, 1), 2:3], min_val=0, max_val=(E - 1) * D)
                pe.wait_ge(h_low, t + 1)
                if reused:
                    pe.wait_ge(y_sbuf, t - 1)
                for r in range(BLK):
                    to = YPS[u][:, D * r:D * r + D]
                    for f in range(FC):
                        cols = bass.ds(at + 128 * f, 128)
                        hi, lo = (h[:, u, f, 128 * r:128 * r + 128] for h in (hhi, hlo))
                        pe.matmul(to, lhsT=hi, rhs=w2h[:, cols], start=(f == 0), stop=False)
                        pe.matmul(to, lhsT=hi, rhs=w2l[:, cols], start=False, stop=False)
                        pe.matmul(to, lhsT=lo, rhs=w2h[:, cols], start=False, stop=False)
                    last = pe.matmul(to, lhsT=ones16[0:64, 0:128], rhs=b2h[:, bass.ds(at2, D)], start=False, stop=True)
                last.then_inc(y_ps, 1)

            turn_x(0, 0, 0, False)
            hidden(0, 0, False)
            turn_x(1, 0, 1, False)
            hidden(1, 1, False)
            turn_x(2, 1, 0)
            result(0, 0, False)
            hidden(2, 0)
            turn_x(3, 1, 1)
            result(1, 1, False)
            with pe.Fori(1, NTILES // 2 - 1) as i:
                hidden(2 * i + 1, 1)
                turn_x(2 * i + 2, i + 1, 0)
                result(2 * i, 0)
                hidden(2 * i + 2, 0)
                turn_x(2 * i + 3, i + 1, 1)
                result(2 * i + 1, 1)
            hidden(NTILES - 1, 1)
            result(NTILES - 2, 0)
            result(NTILES - 1, 1)


_INS = ["x", "L0_tok_W_ve", "L0_tok_b_ve", "L0_tok_W_lin", "L0_tok_b_lin", "L0_attn_gamma", "L0_attn_w_qkv",
        "L0_attn_temperature", "L0_attn_w_out", "L0_ffn_Wr", "L0_ffn_br", "L0_ffn_W1", "L0_ffn_b1",
        "L0_ffn_W2", "L0_ffn_b2"]


def kernel(**inputs):
    import numpy as _np
    import concourse.bacc as _bacc
    from concourse import mybir as _mybir
    from concourse.bass_utils import run_bass_kernel_spmd as _run

    nc = _bacc.Bacc("TRN2", target_bir_lowering=False, num_devices=1)
    arrays, args = {}, []
    for name in _INS:
        a = _np.ascontiguousarray(inputs[name])
        arrays[f"in_{name}"] = a
        args.append(nc.dram_tensor(f"in_{name}", a.shape, _mybir.dt.from_np(a.dtype), kind="ExternalInput").ap())
    out = nc.dram_tensor("out", (B, T, D), F32, kind="ExternalOutput").ap()
    rows = nc.dram_tensor("rows", (ROWS, ROWF), F32).ap()
    parts = nc.dram_tensor("parts", (2 * NTOK, D), F32).ap()
    audio_tower(nc, *args, out, rows, parts)
    r = _run(nc, [arrays], core_ids=[0])
    return r.results[0]["out"]
```

```python
from contextlib import ExitStack

import concourse.bass as bass
from concourse import mybir

ALU = mybir.AluOpType
ACT = mybir.ActivationFunctionType
AX = mybir.AxisListType.X
F32 = mybir.dt.float32
F16 = mybir.dt.float16
BF16 = mybir.dt.bfloat16
I32 = mybir.dt.int32
U32 = mybir.dt.uint32

B, C, T, D = 8, 32, 750, 128
H, DH = 8, 64
HD = H * DH
HP = H // 2
E, F = 8, 512
FC = F // D
KA = C + 1
KS = 64 + KA
NT, TOK = 6, 125
NTOK = B * T
GB = 128 // C
NC2 = D + 1 + E
DECAY = 0.9
TINY2 = 1e-24
LN2 = 0.6931471805599453
UP_TOKEN, UP_HEAD = 42, 30
EPS = 1e-5

TILE = 256
BLK = TILE // 128
NTILES = (2 * NTOK + E * (TILE - 1)) // TILE
REGION = NTOK + TILE
SPARE = NTILES - 2 * NTOK // TILE + 1
ROWS = E * REGION + SPARE * TILE
TAIL = 6
ROWF = D + TAIL
KT = NTOK // TILE + 1
EARLY = B - 2
FAR = float(1 << 14)
XB = 4
RSENT = 16 * NT
WCH = 1024
WS = 16.0

CHUNKS = [(k, n) for k in ("w1", "w2") for n in range(E * F // WCH)] + [("b2", 0)]
CHUNK_STEP = 2

STAGES = [
    ("tokens", 0), ("rank", 4), ("split_hi", 4), ("copy_turn", 1), ("shares", 4), ("place", 4),
    ("scores", 2), ("qk", 1), ("copy_k", 1), ("tokens2", 3), ("copy_s", 0), ("exps", 2), ("split_lo", 5),
    ("square", 3), ("prods", 1), ("var", 0), ("sim", 1), ("rho", 0), ("norms", 1), ("probs", 2),
    ("scatter", 5), ("union", 2), ("var2", 3), ("rho2", 3), ("shift_w", 2), ("high_w", 2), ("copy_u", 2),
    ("kappa", 0), ("gram", 0), ("clamp", 1), ("norm2", 3), ("low_w", 2), ("copy_gram", 0), ("gram_rest", 0),
    ("top2", 3), ("roots", 1), ("gram_mid", 0), ("px", 2), ("turn", 0), ("copy_px", 2), ("exp_logits", 3),
    ("gram_low", 0),
]
SCHEDULE = [(name, s - lag) for s in range(B + max(lag for _, lag in STAGES))
            for name, lag in STAGES if 0 <= s - lag < B]


def emitted_before(name, b, other):
    at = SCHEDULE.index((name, b))
    return sum(n == other for n, _ in SCHEDULE[:at])


def audio_tower(nc, x, w_ve, b_ve, w_lin, b_lin, gamma, w_qkv, temperature, w_out,
                w_r, b_r, w1, b1, w2, b2, out, rows, parts, dbg=None):
    with ExitStack() as ctx:
        def sb(name, shape, dt=F32):
            return ctx.enter_context(nc.sbuf_tensor(name, shape, dt))

        def pb(name, shape, dt=F32):
            return ctx.enter_context(nc.psum_tensor(name, shape, dt))

        def sem(name):
            return ctx.enter_context(nc.semaphore(name))

        wlin_sb = sb("wlin_sb", [D, D])
        vext = sb("vext", [D, KA])
        wve_sb = sb("wve_sb", [D, C])
        blin_sb = sb("blin_sb", [D, 1])
        gamma_sb = sb("gamma_sb", [D, 1])
        wqkv_sb = sb("wqkv_sb", [D, 3 * HD])
        wg_sb = sb("wg_sb", [D, 3 * HD])
        temp_sb = sb("temp_sb", [128, H])
        texp_sb = sb("texp_sb", [128, HP])
        wout_sb = sb("wout_sb", [128, HP, D])
        woutT = wqkv_sb[:, 0:HP * D].rearrange("p (h n) -> p h n", h=HP)
        wc_out = sb("wc_out", [128, HP, NC2])
        wr_sb = sb("wr_sb", [D, E])
        br_sb = sb("br_sb", [128, E])
        ident = sb("ident", [128, 128])
        ident16 = sb("ident16", [128, 128], F16)
        ones = sb("ones", [128, 128])
        ones16 = sb("ones16", [128, 128], F16)
        tri = sb("tri", [128, 128], BF16)
        onesb = sb("onesb", [128, 128], BF16)
        cmat = sb("cmat", [D, NC2])
        wlinT = sb("wlinT", [D, D])
        wc1T = sb("wc1T", [D, KA])
        aT = sb("aT", [D, KA])
        ik = sb("ik", [KA, 2 * KA])
        qk_w = sb("qk_w", [KA, 2 * HD])
        vT = sb("vT", [128, HP, KA])
        exp_ids = sb("exp_ids", [128, E])
        ebase = sb("ebase", [128, E])
        lift = sb("lift", [128, 2])
        dests = sb("dests", [TOK, B * NT, 2])

        big = sb("big", [128, 8, NT * D])
        x_sb, diff, lr, rl = (big[:, 2 * i:2 * i + 2, 0:T] for i in range(4))
        rl0 = sb("rl0", [128, 2])
        decay = sb("decay", [128, 1])
        SR = sb("SR", [KS, B, T])
        R = sb("R", [KS, 2, NC2])

        sT = sb("sT", [TOK, 2, NT, KA])
        quad = sb("quad", [TOK, NT, KA])
        kap = sb("kap", [TOK, 4, NT])
        spT = sb("spT", [TOK, 2, NT, KA])
        g_sb = sb("g_sb", [KS, 2, 2, KA], BF16)
        g_rest = sb("g_rest", [KA, 2, KA])
        g_mid = sb("g_mid", [KA, 2, KA], BF16)
        qk_parts = sb("qk_parts", [KS, 3, 2 * HD], BF16)
        k_sb = sb("k_sb", [KA, 2, HD])
        prod = sb("prod", [KA, 2, 2 * HD])
        norm_c = sb("norm_c", [128, HP * DH + HP])
        norm_r = sb("norm_r", [128, HP * DH + HP])
        norm_t = sb("norm_t", [128, HP * DH + HP])
        z_sb = sb("z_sb", [128, 2, HP * DH])
        zm = sb("zm", [128, HP])
        zscale = sb("zscale", [128, 2, HP])
        zshift = sb("zshift", [128, 2, HP])
        ez = sb("ez", [128, 2, HP * DH])
        zs = sb("zs", [128, 2, HP])
        attn = sb("attn", [128, 2, HP, 128])
        u_sb = sb("u_sb", [128, 2, HP, NC2])
        sq_sb = wg_sb[0:TOK, 0:NT * D].rearrange("p (j n) -> p j n", j=NT)
        mean2 = sb("mean2", [TOK, NT])
        rho2 = sb("rho2", [TOK, 3, NT])
        h2 = sb("h2", [TOK, B * NT, D])
        x2 = sb("x2", [TOK, 2, NT, D])
        lg = sb("lg", [TOK, 2, NT, E])
        top = sb("top", [TOK, NT, E])
        tops = sb("tops", [TOK, 2, NT, E])
        topi = sb("topi", [TOK, NT, E], U32)
        exl = sb("exl", [TOK, 2, NT, E])
        oh = sb("oh", [TOK, 2, 2, NT, E])
        mask = sb("mask", [TOK, 2, NT, E], BF16)
        msum = sb("msum", [TOK, B + 1, E], BF16)
        mrow = sb("mrow", [TOK, E])
        sums = sb("sums", [TOK, 1, NT])
        rk = sb("rk", [TOK, NT, E])
        rk2 = sb("rk2", [TOK, 2, NT, E])
        posf = sb("posf", [TOK, 2, NT])
        pos = sb("pos", [TOK, 2, 2, NT], U32)
        xrow = sb("xrow", [TOK, 2, NT, ROWF])
        xrow16 = xrow[:, :, :, :].bitcast(F16)

        wraw = sb("wraw", [128, 2, WCH])
        w1h = sb("w1h", [128, E * F], F16)
        w1l = sb("w1l", [128, E * F], F16)
        w2h = sb("w2h", [128, E * F], F16)
        w2l = sb("w2l", [128, E * F], F16)
        w1row = sb("w1row", [128, 2, WCH])
        b2h = sb("b2h", [64, E * D], F16)
        zrow = sb("zrow", [128, BLK * ROWF])
        ksteps = sb("ksteps", [128, KT])
        tindex = sb("tindex", [128, NTILES])
        cnt = sb("cnt", [128, 2, E])
        over = sb("over", [128, E, KT])
        tiles = sb("tiles", [128, E])
        cumend = sb("cumend", [128, E])
        past, past2 = (u_sb[:, i].rearrange("p h n -> p (h n)")[:, 0:NTILES * E].rearrange("p (t e) -> p t e", e=E)
                       for i in range(2))
        et = sb("et", [128, NTILES])
        cstart = sb("cstart", [128, NTILES])
        rowf = sb("rowf", [128, NTILES])
        padf = sb("padf", [128, E])
        early = sb("early", [128, E])
        late = sb("late", [128, NTILES])
        table = sb("table", [128, NTILES, 4], I32)
        pads = sb("pads", [128, E], I32)

        flat = big[:, :, :].rearrange("p a n -> p (a n)")
        xin_flat, ysb_flat = flat[:, 0:XB * BLK * ROWF], flat[:, 4 * NT * D:4 * NT * D + XB * BLK * D]
        xin = xin_flat.rearrange("p (u r n) -> p u r n", u=XB, r=BLK)
        xin16 = xin_flat.bitcast(F16).rearrange("p (u r n) -> p u r n", u=XB, r=BLK)
        ysb = ysb_flat.rearrange("p (u r n) -> p u r n", u=XB, r=BLK)
        over1, over2 = wqkv_sb[:, :].bitcast(F16), wg_sb[:, :].bitcast(F16)
        hhi = over1[:, 0:4 * 512].rearrange("p (u f n) -> p u f n", u=2, f=FC)
        xT = over1[:, 4 * 512:6 * 512].rearrange("p (u s n) -> p u s n", u=2, s=2)
        hlo = over2[:, 0:4 * 512].rearrange("p (u f n) -> p u f n", u=2, f=FC)
        mine = sb("mine", [128, 2, BLK, 2])
        both = sb("both", [128, 2, BLK, 2, 2])
        cwd = sb("cwd", [128, XB, BLK, 2])
        dst = sb("dst", [128, XB, BLK], U32)

        ps_tok = pb("ps_tok", [128, 512])
        ps_small = pb("ps_small", [128, 512])
        ps_qk = pb("ps_qk", [128, 2, 512])
        ps_norm = pb("ps_norm", [128, 512])
        ps_sim = pb("ps_sim", [128, 512])
        ps_tok2 = pb("ps_tok2", [128, 2, 512])
        GRAM = ps_tok[0:KA, 2 * KA * NT:2 * KA * NT + KA]
        TOKS = ps_tok[0:TOK, 0:2 * KA * NT].rearrange("p (j k) -> p j k", k=2 * KA)
        PX = ps_small[0:KA, 64:64 + NC2]
        RANK = ps_small[0:TOK, 256:256 + NT * E].rearrange("p (j e) -> p j e", e=E)
        COUNT = ps_small[:, 320:320 + 2 * E].rearrange("p (a e) -> p a e", e=E)
        NQ = ps_norm[:, HP * DH:HP * DH + HP]
        NK = ps_norm[:, 0:HP * DH]
        SIM = ps_sim[:, 0:HP * DH]
        UNION = [ps_qk[:, 0, 0:3 * NC2].rearrange("p (h n) -> p h n", n=NC2),
                 ps_qk[:, 1, 0:NC2].rearrange("p (h n) -> p h n", n=NC2)]
        TOK2 = ps_tok2[0:TOK, :, 0:3 * NC2].rearrange("p a (j n) -> p a j n", n=NC2)

        XPS = [ps_tok[:, :].bitcast(F16), ps_small[:, :].bitcast(F16)]
        HPS = [ps_qk[:, :, :].rearrange("p a n -> p (a n)"), ps_tok2[:, :, :].rearrange("p a n -> p (a n)")]
        YPS = [ps_norm[:, 0:BLK * D], ps_sim[:, 0:BLK * D]]

        wload = [sem("wload0"), sem("wload1")]
        wshifted = sem("wshifted")
        whigh = sem("whigh")
        wlow = sem("wlow")
        zeroed = sem("zeroed")
        zeros = sem("zeros")
        count_ps = sem("count_ps")
        table_ready = sem("table_ready")
        x_in = [sem(f"x_in{i}") for i in range(XB)]
        x_ps = sem("x_ps")
        x_sbuf = sem("x_sbuf")
        h_ps = sem("h_ps")
        h_high = sem("h_high")
        h_low = sem("h_low")
        y_ps = sem("y_ps")
        y_sbuf = sem("y_sbuf")
        weights = sem("weights")
        y_sent = [sem(f"y_sent{i}") for i in range(XB)]
        y_in = [sem(f"y_in{i}") for i in range(4)]
        summed = sem("summed")
        stored = [sem(f"stored{i}") for i in range(4)]
        load = {n: sem(f"load_{n}") for n in (
            "x0", "x1", "wlin", "wve", "bve", "blin", "gamma", "wqkv", "temp", "wout", "wr", "br")}
        consts = sem("consts")
        ch_pool = sem("ch_pool")
        ch_dve = sem("ch_dve")
        ch_act = sem("ch_act")
        ch_pe = sem("ch_pe")
        setup_ps = sem("setup_ps")
        setup_sb = sem("setup_sb")
        scans = sem("scans")
        smooth = sem("smooth")
        done = {name: sem(f"done_{name}") for name, _ in STAGES}
        quad_read = sem("quad_read")
        sim_read = sem("sim_read")
        h2_read = sem("h2_read")
        x2_ready = sem("x2_ready")
        lg_ready = sem("lg_ready")
        tail_ready = sem("tail_ready")
        sent = [sem("sent0"), sem("sent1")]
        dbg_sem = sem("dbg_sem")
        setup_dve = sem("setup_dve")
        counted = sem("counted")
        weigh1 = sem("weigh1")
        weigh2 = sem("weigh2")
        weigh3 = sem("weigh3")
        rank_read = sem("rank_read")
        parts_zeroed = sem("parts_zeroed")
        qk_high = sem("qk_high")
        qk_mid = sem("qk_mid")
        qk_low = sem("qk_low")
        qk_rest_ready = sem("qk_rest_ready")
        qk_rest = prod[:, 0, :]

        def chained(semaphore):
            count = [0]

            def step(eng, ins):
                count[0] += 1
                ins.then_inc(semaphore, 1)
                eng.wait_ge(semaphore, count[0])
            return step

        def split_of(kind, n):
            at = slice(WCH * n, WCH * n + WCH)
            if kind == "w1":
                return w1h[:, at], w1l[:, at]
            if kind == "w2":
                return w2h[:, at], w2l[:, at]
            return b2h[0:1, :], b2h[32:33, :]

        def loads_before(k):
            return sum(3 if kind == "w1" else 2 for j, (kind, _) in enumerate(CHUNKS[:k + 1]) if j % 2 == k % 2)

        def over_tiles(eng, body, first, end):
            at = min(-(-max(first, 1) // XB) * XB, end)
            for t in range(first, at):
                body(t, t // XB, t % XB)
            loops = (at // XB, end // XB)
            if loops[0] < loops[1]:
                with eng.Fori(*loops) as i:
                    for v in range(XB):
                        body(XB * i + v, i, v)
                at = XB * loops[1]
            for t in range(at, end):
                body(t, t // XB, t % XB)

        def since(t, n):
            return not isinstance(t, int) or t >= n

        block = ctx.enter_context(nc.Block())

        SETUP = ["wlinT", "wc1T", "cr", "aT", "ax", "kk", "q", "k", "v"]

        @block.sync
        def _(sp):
            for g in range(2):
                sp.dma_start(x_sb[:, g, :], x[GB * g:GB * (g + 1)].rearrange("b c t -> (b c) t")).then_inc(load[f"x{g}"], 16)
            sp.dma_start(wlin_sb[:, :], w_lin).then_inc(load["wlin"], 16)
            sp.dma_start(wve_sb[:, :], w_ve).then_inc(load["wve"], 16)
            sp.dma_start(vext[:, C:KA], b_ve.rearrange("(d a) -> d a", a=1)).then_inc(load["bve"], 16)
            sp.dma_start(blin_sb[:, :], b_lin.rearrange("(d a) -> d a", a=1)).then_inc(load["blin"], 16)
            sp.dma_start(wr_sb[:, :], w_r).then_inc(load["wr"], 16)
            sp.dma_start(gamma_sb[:, :], gamma.rearrange("(d a) -> d a", a=1)).then_inc(load["gamma"], 16)
            sp.dma_start(wqkv_sb[:, :], w_qkv).then_inc(load["wqkv"], 16)
            sp.dma_start(temp_sb[:, :], temperature.rearrange("h a b -> (a b) h").to_broadcast((128, H))).then_inc(load["temp"], 16)
            sp.dma_start(wout_sb[:, :, :], w_out.rearrange("(p r) n -> r p n", r=128)).then_inc(load["wout"], 16)
            sp.dma_start(br_sb[:, :], b_r.rearrange("(a e) -> a e", a=1).to_broadcast((128, E))).then_inc(load["br"], 16)
            w1v = w1.rearrange("e d f -> d e f")
            w2v = w2.rearrange("e (c p) n -> p e c n", p=128)
            for k, (kind, n) in enumerate(CHUNKS):
                if k >= 2:
                    sp.wait_ge(wlow, k - 1)
                raw, row = wraw[:, k % 2, :], w1row[1:128, k % 2, :]
                if kind == "w1":
                    at = slice(2 * n, 2 * n + 2)
                    sp.dma_start(raw[1:128, :].rearrange("p (e f) -> p e f", e=2), w1v[1:D, at, :]).then_inc(wload[k % 2], 16)
                    sp.dma_start(raw[0:1, :].rearrange("p (e f) -> p e f", e=2),
                                 b1[at].rearrange("(a e) f -> a e f", a=1)).then_inc(wload[k % 2], 16)
                    sp.dma_start(row.rearrange("p (e f) -> p e f", e=2),
                                 w1v[0:1, at, :].to_broadcast((D - 1, 2, F))).then_inc(wload[k % 2], 16)
                elif kind == "w2":
                    for i in range(2):
                        sp.dma_start(raw[:, F * i:F * i + F].rearrange("p (c n) -> p c n", n=D),
                                     w2v[:, 2 * n + i]).then_inc(wload[k % 2], 16)
                else:
                    for r in (0, 32):
                        sp.dma_start(raw[r:r + 1, :], b2.rearrange("(a e) f -> a (e f)", a=1)).then_inc(wload[k % 2], 16)
            sp.wait_ge(zeroed, 3)
            sp.dma_start(rows[E * REGION:ROWS, :].rearrange("(s p r) n -> p s (r n)", p=128, r=BLK),
                         zrow[:, :].rearrange("p (a n) -> p a n", a=1).to_broadcast((128, SPARE, BLK * ROWF))
                         ).then_inc(zeros, 16)
            sp.wait_ge(table_ready, 2)

            def load_tile(t, i, v):
                if since(t, XB):
                    sp.wait_ge(x_ps, t - XB + 1)
                    sp.wait_ge(weights, t - XB + 1)
                first = sp.value_load(table[0:1, bass.ds(t, 1), 0:1], min_val=0, max_val=ROWS - TILE)
                full = sp.value_load(table[0:1, bass.ds(t, 1), 2:3], min_val=RSENT * EARLY, max_val=RSENT * B)
                filled = sp.value_load(table[0:1, bass.ds(t, 1), 3:4], min_val=16, max_val=16 + 16 * E)
                sp.wait_ge(sent[0], full)
                sp.wait_ge(sent[1], full)
                sp.wait_ge(zeros, filled)
                sp.dma_start(xin[:, v].rearrange("p r n -> p (r n)"),
                             rows[bass.ds(first, TILE), :].rearrange("(p r) n -> p (r n)", r=BLK)).then_inc(x_in[v], 16)

            for t in range(XB):
                load_tile(t, 0, t)
            over_tiles(sp, load_tile, XB, NTILES)

            for v in range(XB):
                sp.wait_ge(y_sent[v], 16 * BLK * ((NTILES - v + XB - 1) // XB))
            pv = parts.rearrange("(c b j p) n -> p c b j n", c=2, b=B, p=TOK)
            ov = out.rearrange("b (j p) n -> p b j n", p=TOK)
            for s in range(B + 2):
                if s < B:
                    if s >= 4:
                        sp.wait_ge(stored[s % 4], 16)
                    for c in range(2):
                        sp.dma_start(big[0:TOK, 2 * (s % 4) + c, :].rearrange("p (j n) -> p j n", n=D),
                                     pv[:, c, s]).then_inc(y_in[s % 4], 16)
                if s >= 2:
                    b = s - 2
                    sp.wait_ge(summed, b + 1)
                    sp.dma_start(ov[:, b], big[0:TOK, 2 * (b % 4), :].rearrange("p (j n) -> p j n", n=D)
                                 ).then_inc(stored[b % 4], 16)
            for i in range(4):
                sp.wait_ge(stored[i], 32)
            if dbg is not None:
                sp.wait_ge(sent[0], 16 * 12 * B // 2)
                sp.wait_ge(sent[1], 16 * 12 * B // 2)
                sp.dma_start(dbg["h2"], h2[:, :, :]).then_inc(dbg_sem, 16)
                sp.dma_start(dbg["sr"], SR[:, :, :]).then_inc(dbg_sem, 16)
                sp.dma_start(dbg["msum"], msum[:, :, :]).then_inc(dbg_sem, 16)
                sp.dma_start(dbg["lg"], lg[:, :, :, :]).then_inc(dbg_sem, 16)
                sp.dma_start(dbg["xrow"], xrow[:, :, :, :]).then_inc(dbg_sem, 16)
                sp.dma_start(dbg["pos"], pos[:, :, :, :]).then_inc(dbg_sem, 16)
                sp.wait_ge(dbg_sem, 96)

        @block.gpsimd
        def _(pool):
            step = chained(ch_pool)
            made = [0]

            def const(ins):
                made[0] += 1
                ins.then_inc(consts, 1)
                pool.wait_ge(consts, made[0])

            const(pool.memset(ones[:, :], 1.0))
            const(pool.memset(ones16[:, :], 1.0))
            const(pool.memset(onesb[:, :], 1.0))
            const(pool.memset(decay[:, :], DECAY))
            const(pool.memset(lift[:, 0:1], UP_TOKEN / 2 * LN2))
            const(pool.memset(lift[:, 1:2], UP_HEAD / 2 * LN2))
            const(pool.memset(attn[:, :, :, :], 0.0))
            const(pool.memset(msum[:, 0, :], 0.0))
            const(pool.memset(x2[:, :, :, 0:1], 1.0))
            const(pool.memset(R[32:64, :, :], 0.0))
            const(pool.affine_select(out=ident[:, :], in_=ones[:, :], compare_op=ALU.is_equal, fill=0.0,
                               base=0, pattern=[[-1, 128]], channel_multiplier=1))
            const(pool.affine_select(out=ident16[:, :], in_=ones16[:, :], compare_op=ALU.is_equal, fill=0.0,
                               base=0, pattern=[[-1, 128]], channel_multiplier=1))
            const(pool.affine_select(out=tri[:, :], in_=onesb[:, :], compare_op=ALU.is_gt, fill=0.0,
                               base=0, pattern=[[1, 128]], channel_multiplier=-1))
            const(pool.iota(ksteps[:, :], [[TILE, KT]], base=0, channel_multiplier=0,
                            allow_small_or_imprecise_dtypes=True))
            const(pool.iota(tindex[:, :], [[1, NTILES]], base=0, channel_multiplier=0,
                            allow_small_or_imprecise_dtypes=True))
            const(pool.iota(exp_ids[:, :], [[1, E]], base=0, channel_multiplier=0,
                      allow_small_or_imprecise_dtypes=True))
            const(pool.iota(ebase[:, :], [[REGION, E]], base=0, channel_multiplier=0,
                      allow_small_or_imprecise_dtypes=True))
            const(pool.iota(dests[:, :, :], [[TOK, B * NT], [NTOK, 2]], base=-int(FAR), channel_multiplier=1,
                      allow_small_or_imprecise_dtypes=True))
            def zero(semaphore, areas):
                for n, area in enumerate(areas):
                    pool.memset(area, 0.0).then_inc(semaphore, 1)
                    pool.wait_ge(semaphore, n + 1)

            for b in range(B):
                g, i = b // GB, b % GB
                step(pool, pool.memset(SR[32:64, b, :], 1.0))
                pool.wait_ge(scans, 2 * g + 2)
                pool.tensor_tensor(SR[0:C, b, :], lr[C * i:C * i + C, g, :], rl[C * i:C * i + C, g, :],
                                   ALU.add).then_inc(smooth, 1)
                pool.wait_ge(smooth, b + 1)
                if b == 1:
                    zero(parts_zeroed, (g_sb[32:64, :, :, :], qk_parts[32:64, :, :]))
            zero(zeroed, (w1row[0:1, :, :], b2h[:, :], zrow[:, :]))

            def shift_w(s):
                for k in range(CHUNK_STEP * s, min(CHUNK_STEP * (s + 1), len(CHUNKS))):
                    kind, n = CHUNKS[k]
                    if kind == "w1":
                        pool.wait_ge(wload[k % 2], 16 * loads_before(k))
                        pool.wait_ge(zeroed, 1)
                        pool.tensor_tensor(wraw[:, k % 2, :], wraw[:, k % 2, :], w1row[:, k % 2, :],
                                           ALU.subtract).then_inc(wshifted, 1)
                        pool.wait_ge(wshifted, n + 1)

            def split_lo(b):
                pool.wait_ge(done["split_hi"], b + 1)
                pool.tensor_tensor(xrow16[:, b % 2, :, D:2 * D], x2[:, b % 2], xrow16[:, b % 2, :, 0:D],
                                   ALU.subtract).then_inc(done["split_lo"], 1)
                pool.wait_ge(done["split_lo"], b + 1)
                tail = xrow[:, b % 2, :, D + 4:D + 6]
                pool.tensor_copy(tail, dests[:, NT * b:NT * b + NT, :]).then_inc(tail_ready, 1)

            def scatter(b):
                pool.wait_ge(done["place"], b + 1)
                pool.wait_ge(done["split_lo"], b + 1)
                pool.wait_ge(tail_ready, b + 1)
                for c in range(2):
                    for j in range(NT):
                        pool.indirect_dma_start(
                            rows, bass.IndirectOffsetOnAxis(ap=pos[:, b % 2, c, j:j + 1], axis=0),
                            xrow[:, b % 2, j, :], None).then_inc(sent[b % 2], 16)

            for name, b in SCHEDULE:
                if name == "shift_w":
                    shift_w(b)
                elif name == "split_lo":
                    split_lo(b)
                elif name == "scatter":
                    scatter(b)

            bound = pool.alloc_register("bound")

            def send(t, i, v):
                pool.wait_ge(y_sbuf, t + 1)
                pool.reg_alu(bound, pool.to_reg(t + 2 * NTOK), 2 * NTOK - 1, op=ALU.min)
                for r in range(BLK):
                    pool.indirect_dma_start(
                        parts, bass.IndirectOffsetOnAxis(ap=dst[:, v, r:r + 1], axis=0), ysb[:, v, r, :], None,
                        bounds_check=bound, oob_is_err=False).then_inc(y_sent[v], 16)

            over_tiles(pool, send, 0, NTILES)

        @block.scalar
        def _(act):
            step = chained(ch_act)

            def copied(n, dst, src, scale=1.0):
                act.wait_ge(setup_ps, n + 1)
                act.activation(dst, src, ACT.Copy, scale=scale).then_inc(setup_sb, 1)

            act.preload_act_table_set("natural_log_exp_and_others")
            act.wait_ge(load["temp"], 16)
            for i in range(2):
                step(act, act.activation(texp_sb[64 * i:64 * i + 64, :], temp_sb[64 * i:64 * i + 64, i::2], ACT.Exp))
            copied(0, wlinT[:, :], ps_qk[:, 0, 0:D])
            copied(1, wc1T[:, :], ps_qk[:, 1, 0:KA])
            copied(2, cmat[:, D + 1:NC2], ps_norm[:, 0:E])
            copied(3, aT[:, :], ps_sim[:, 0:KA])
            act.wait_ge(consts, 9)
            act.wait_ge(setup_ps, 5)
            act.activation(R[0:KA, 0, :], ps_tok[0:KA, 0:NC2], ACT.Copy).then_inc(setup_sb, 1)
            act.activation(R[0:KA, 1, :], ps_tok[0:KA, 0:NC2], ACT.Copy).then_inc(setup_sb, 1)
            copied(5, ik[:, KA:2 * KA], ps_small[0:KA, 0:KA], 1.0 / D)
            copied(6, qk_w[:, 0:HD], ps_qk[0:KA, 0, :])
            copied(7, qk_w[:, HD:2 * HD], ps_qk[0:KA, 1, :])
            act.wait_ge(setup_dve, 5)
            copied(8, woutT, ps_small[:, :].rearrange("p (h n) -> p h n", h=HP))
            act.wait_ge(setup_ps, 10)
            act.activation(wc_out[:, 0:3, :], UNION[0], ACT.Copy)
            act.activation(wc_out[:, 3:4, :], UNION[1], ACT.Copy).then_inc(setup_sb, 1)
            copied(10, vT[:, :, :], ps_tok2[:, 0, 0:HP * KA].rearrange("p (h k) -> p h k", k=KA))
            act.wait_ge(parts_zeroed, 2)
            act.wait_ge(setup_sb, 9)
            for n in (0, 2):
                last = act.activation(qk_parts[0:KA, n, :], qk_w[:, :], ACT.Copy)
            last.then_inc(qk_high, 1)
            act.wait_ge(qk_rest_ready, 1)
            act.activation(qk_parts[0:KA, 1, :], qk_rest[:, :], ACT.Copy).then_inc(qk_mid, 1)

            def high_w(s):
                for k in range(CHUNK_STEP * s, min(CHUNK_STEP * (s + 1), len(CHUNKS))):
                    kind, n = CHUNKS[k]
                    high, low = split_of(kind, n)
                    if kind == "w1":
                        act.wait_ge(wshifted, n + 1)
                    act.wait_ge(wload[k % 2], 16 * loads_before(k))
                    if kind == "b2":
                        act.wait_ge(zeroed, 2)
                        act.activation(high, wraw[0:1, k % 2, :], ACT.Copy, scale=WS * WS)
                        act.activation(low, wraw[32:33, k % 2, :], ACT.Copy, scale=WS * WS).then_inc(whigh, 1)
                    else:
                        act.activation(high, wraw[:, k % 2, :], ACT.Copy, scale=WS).then_inc(whigh, 1)

            def copy_s(b):
                act.wait_ge(done["tokens"], b + 1)
                if b >= 2:
                    act.wait_ge(done["kappa"], b - 1)
                act.activation(sT[:, b % 2], TOKS[:, :, 0:KA], ACT.Copy).then_inc(done["copy_s"], 1)

            def root(dst, src, up):
                step(act, act.activation(dst, src, ACT.Ln, scale=2.0 ** up))
                n = dst.shape[0]
                bias = {0: 0.0, UP_TOKEN: lift[0:n, 0:1], UP_HEAD: lift[0:n, 1:2]}[up]
                return act.activation(dst, dst, ACT.Exp, bias=bias, scale=-0.5)

            def rho(b):
                act.wait_ge(done["var"], b + 1)
                root(kap[:, 3, :], kap[:, 2, :], UP_TOKEN).then_inc(done["rho"], 1)

            def rho2_(b):
                act.wait_ge(done["var2"], b + 1)
                root(rho2[:, 2, :], rho2[:, 1, :], 0).then_inc(done["rho2"], 1)

            def roots(b):
                act.wait_ge(done["clamp"], b + 1)
                if b >= 1:
                    act.wait_ge(sim_read, b)
                step(act, root(norm_r[:, :], norm_c[:, :], UP_HEAD))
                act.activation(norm_t[:, :], norm_r[:, :], ACT.Square).then_inc(done["roots"], 1)

            def copy_gram(b):
                act.wait_ge(done["gram"], b + 1)
                if b == 0:
                    act.wait_ge(parts_zeroed, 2)
                if b >= 2:
                    act.wait_ge(done["qk"], b - 1)
                act.activation(g_sb[0:KA, b % 2, 0, :], GRAM, ACT.Copy)
                act.activation(g_sb[64:KS, b % 2, 1, :], GRAM, ACT.Copy).then_inc(done["copy_gram"], 1)

            def gram_mid(b):
                act.wait_ge(done["gram_rest"], b + 1)
                act.activation(g_mid[:, b % 2, :], g_rest[:, b % 2, :], ACT.Copy)
                act.activation(g_sb[64:KS, b % 2, 0, :], g_rest[:, b % 2, :], ACT.Copy).then_inc(done["gram_mid"], 1)

            def copy_turn(b):
                act.wait_ge(done["turn"], b + 1)
                act.activation(SR[64:KS, b, :].rearrange("p (a t) -> p a t", a=2),
                               ps_tok2[0:KA, :, 0:3 * TOK], ACT.Copy).then_inc(done["copy_turn"], 1)

            def copy_k(b):
                act.wait_ge(done["qk"], b + 1)
                if b >= 2:
                    act.wait_ge(done["sim"], b - 1)
                    act.wait_ge(done["prods"], 2 * (b - 1))
                act.activation(k_sb[:, b % 2, :], ps_qk[0:KA, 1, :], ACT.Copy).then_inc(done["copy_k"], 1)

            def exps(b):
                act.wait_ge(done["scores"], b + 1)
                if b >= 2:
                    act.wait_ge(done["probs"], b - 1)
                for p in range(HP):
                    at = slice(DH * p, DH * p + DH)
                    last = act.activation(ez[:, b % 2, at], z_sb[:, b % 2, at], ACT.Exp, bias=zshift[:, b % 2, p:p + 1],
                                          scale=zscale[:, b % 2, p:p + 1], accum_out=zs[:, b % 2, p:p + 1])
                last.then_inc(done["exps"], 1)

            def copy_u(b):
                act.wait_ge(done["union"], b + 1)
                if b >= 2:
                    act.wait_ge(done["px"], b - 1)
                act.activation(u_sb[:, b % 2, 0:3, :], UNION[0], ACT.Copy)
                act.activation(u_sb[:, b % 2, 3:4, :], UNION[1], ACT.Copy).then_inc(done["copy_u"], 1)

            def copy_px(b):
                act.wait_ge(done["px"], b + 1)
                if b >= 2:
                    act.wait_ge(done["tokens2"], b - 1)
                act.activation(R[64:KS, b % 2, :], PX, ACT.Copy).then_inc(done["copy_px"], 1)

            def square(b):
                act.wait_ge(done["tokens2"], b + 1)
                if b >= 1:
                    act.wait_ge(done["norm2"], b)
                for j in range(NT):
                    last = act.activation(sq_sb[:, j, :], TOK2[:, j // 3, j % 3, 0:D], ACT.Square,
                                          accum_out=rho2[:, 0, j:j + 1])
                last.then_inc(done["square"], 1)

            def split_hi(b):
                act.wait_ge(x2_ready, b + 1)
                if b >= 2:
                    act.wait_ge(sent[b % 2], 2 * RSENT * (b // 2))
                act.activation(xrow16[:, b % 2, :, 0:D], x2[:, b % 2], ACT.Copy).then_inc(done["split_hi"], 1)

            def exp_logits(b):
                act.wait_ge(lg_ready, b + 1)
                if b >= 2:
                    act.wait_ge(done["shares"], b - 1)
                act.activation(exl[:, b % 2], tops[:, b % 2], ACT.Exp).then_inc(done["exp_logits"], 1)

            here = dict(high_w=high_w, copy_s=copy_s, rho=rho, rho2=rho2_, roots=roots, copy_gram=copy_gram, gram_mid=gram_mid, copy_turn=copy_turn, copy_k=copy_k, exps=exps,
                        copy_u=copy_u, copy_px=copy_px, square=square, split_hi=split_hi, exp_logits=exp_logits)
            for name, b in SCHEDULE:
                if name in here:
                    here[name](b)

            def copy_x(t, u):
                act.wait_ge(x_ps, t + 1)
                if since(t, 2):
                    act.wait_ge(h_ps, t - 1)
                act.activation(xT[:, u].rearrange("p s n -> p (s n)"), XPS[u][:, 0:2 * TILE], ACT.Copy).then_inc(x_sbuf, 1)

            def high(t, u):
                act.wait_ge(h_ps, t + 1)
                if since(t, 2):
                    act.wait_ge(y_ps, t - 1)
                act.activation(hhi[:, u].rearrange("p f n -> p (f n)"), HPS[u], ACT.Relu).then_inc(h_high, 1)

            act.wait_ge(table_ready, 1)
            act.wait_ge(zeroed, 3)
            act.wait_ge(zeros, 16)
            for e in range(E):
                first = act.value_load(pads[0:1, e:e + 1], min_val=0, max_val=E * REGION - TILE)
                act.dma_start(rows[bass.ds(first, TILE), :].rearrange("(p r) n -> p (r n)", r=BLK),
                              zrow[:, :]).then_inc(zeros, 16)

            copy_x(0, 0)
            copy_x(1, 1)

            def tile(t, i, v):
                high(t, v % 2)
                copy_x(t + 2, v % 2)

            over_tiles(act, tile, 0, NTILES - 2)
            for t in range(NTILES - 2, NTILES):
                high(t, t % 2)

        @block.vector
        def _(dve):
            step = chained(ch_dve)
            for g in range(2):
                step(dve, dve.memset(diff[:, g, 0:1], 0.0))
                dve.wait_ge(load[f"x{g}"], 16)
                step(dve, dve.tensor_tensor(diff[:, g, 1:T], x_sb[:, g, 1:T], x_sb[:, g, 0:T - 1], ALU.subtract))
                step(dve, dve.tensor_scalar(rl0[:, g:g + 1], diff[:, g, T - 1:T], 10.0, None, ALU.mult))
                dve.wait_ge(consts, 9)
                dve.tensor_tensor_scan(lr[:, g, :], decay[:, :].to_broadcast((128, T)), diff[:, g, :], 0.0, ALU.mult,
                                       ALU.add).then_inc(scans, 1)
                dve.tensor_tensor_scan(rl[:, g, ::-1], decay[:, :].to_broadcast((128, T)), diff[:, g, ::-1], rl0[:, g:g + 1],
                                       ALU.mult, ALU.add).then_inc(scans, 1)
                if g == 0:
                    dve.wait_ge(load["wve"], 16)
                    dve.wait_ge(load["bve"], 16)
                    dve.tensor_scalar(vext[:, 0:C], wve_sb[:, :], 0.05, None, ALU.mult).then_inc(setup_dve, 1)
                    dve.wait_ge(consts, 13)
                    dve.tensor_scalar(cmat[:, 0:D], ident[:, :], 1.0 / D, None, ALU.subtract).then_inc(setup_dve, 1)
                    dve.tensor_scalar(cmat[:, D:D + 1], ones[:, 0:1], 1.0 / D, None, ALU.mult).then_inc(setup_dve, 1)
                    dve.tensor_copy(ik[:, 0:KA], ident[0:KA, 0:KA]).then_inc(setup_dve, 1)
                    dve.wait_ge(load["gamma"], 16)
                    dve.wait_ge(load["wqkv"], 16)
                    dve.tensor_scalar(wg_sb[:, :], wqkv_sb[:, :], gamma_sb[:, :], None, ALU.mult).then_inc(setup_dve, 1)
                    dve.wait_ge(load["blin"], 16)
                    dve.wait_ge(setup_sb, 2)
                    dve.tensor_tensor(wc1T[:, C:KA], wc1T[:, C:KA], blin_sb[:, :], ALU.add).then_inc(setup_dve, 1)

            dve.wait_ge(parts_zeroed, 2)
            dve.wait_ge(setup_sb, 9)
            dve.tensor_copy(qk_parts[64:KS, 0, :], qk_w[:, :])
            dve.wait_ge(qk_high, 1)
            dve.tensor_tensor(qk_rest[:, :], qk_w[:, :], qk_parts[0:KA, 0, :], ALU.subtract).then_inc(qk_rest_ready, 1)
            dve.wait_ge(qk_rest_ready, 1)
            dve.tensor_copy(qk_parts[64:KS, 1, :], qk_rest[:, :])
            dve.wait_ge(qk_mid, 1)
            dve.tensor_tensor(qk_parts[64:KS, 2, :], qk_rest[:, :], qk_parts[0:KA, 1, :], ALU.subtract).then_inc(qk_low, 1)

            def low_w(s):
                for k in range(CHUNK_STEP * s, min(CHUNK_STEP * (s + 1), len(CHUNKS))):
                    kind, n = CHUNKS[k]
                    high, low = split_of(kind, n)
                    if kind == "b2":
                        high = low
                    r = slice(32, 33) if kind == "b2" else slice(0, 128)
                    dve.wait_ge(whigh, k + 1)
                    dve.scalar_tensor_tensor(low, wraw[r, k % 2, :], WS * WS if kind == "b2" else WS, high,
                                             ALU.mult, ALU.subtract).then_inc(wlow, 1)

            def var(b):
                dve.wait_ge(done["copy_s"], b + 1)
                if b >= 1:
                    dve.wait_ge(done["kappa"], b)
                dve.tensor_tensor(quad[:, :, :], TOKS[:, :, KA:2 * KA], sT[:, b % 2], ALU.mult).then_inc(quad_read, 1)
                dve.wait_ge(quad_read, b + 1)
                step(dve, dve.tensor_reduce(kap[:, 0, :], quad[:, :, :], AX, ALU.add))
                step(dve, dve.tensor_scalar(kap[:, 1, :], kap[:, 0, :], EPS, TINY2 / D, ALU.add, ALU.mult))
                dve.tensor_tensor(kap[:, 2, :], kap[:, 0, :], kap[:, 1, :], ALU.max).then_inc(done["var"], 1)

            def polish(y, square, t):
                step(dve, dve.tensor_tensor(t, y, y, ALU.mult))
                step(dve, dve.scalar_tensor_tensor(t, t, -0.5, square, ALU.mult, ALU.mult))
                step(dve, dve.scalar_tensor_tensor(y, t, 1.5, y, ALU.add, ALU.mult))

            def kappa(b):
                dve.wait_ge(done["rho"], b + 1)
                polish(kap[:, 3, :], kap[:, 2, :], kap[:, 1, :])
                if b >= 2:
                    dve.wait_ge(done["turn"], b - 1)
                dve.tensor_tensor(spT[:, b % 2], sT[:, b % 2],
                                  kap[:, 3, :].rearrange("p (j a) -> p j a", a=1).to_broadcast((TOK, NT, KA)),
                                  ALU.mult).then_inc(done["kappa"], 1)

            def gram_rest(b):
                dve.wait_ge(done["copy_gram"], b + 1)
                dve.tensor_tensor(g_rest[:, b % 2, :], GRAM, g_sb[0:KA, b % 2, 0, :], ALU.subtract).then_inc(done["gram_rest"], 1)

            def gram_low(b):
                dve.wait_ge(done["gram_mid"], b + 1)
                dve.tensor_tensor(g_sb[0:KA, b % 2, 1, :], g_rest[:, b % 2, :], g_mid[:, b % 2, :],
                                  ALU.subtract).then_inc(done["gram_low"], 1)

            def prods(b):
                dve.wait_ge(done["qk"], b + 1)
                if b >= 2:
                    dve.wait_ge(done["norms"], b - 1)
                dve.tensor_tensor(prod[:, b % 2, 0:HD], ps_qk[0:KA, 0, :], qk_w[:, 0:HD],
                                  ALU.mult).then_inc(done["prods"], 1)
                dve.wait_ge(done["copy_k"], b + 1)
                dve.tensor_tensor(prod[:, b % 2, HD:2 * HD], k_sb[:, b % 2, :], qk_w[:, HD:2 * HD],
                                  ALU.mult).then_inc(done["prods"], 1)

            def clamp(b):
                dve.wait_ge(done["norms"], b + 1)
                dve.tensor_scalar(norm_c[:, :], ps_norm[:, 0:HP * DH + HP], TINY2, None,
                                  ALU.max).then_inc(done["clamp"], 1)

            def scores(b):
                dve.wait_ge(done["roots"], b + 1)
                nk, nq = norm_r[:, 0:HP * DH], norm_r[:, HP * DH:HP * DH + HP]
                step(dve, dve.scalar_tensor_tensor(norm_t[:, :], norm_t[:, :], -0.5, norm_c[:, :], ALU.mult, ALU.mult))
                step(dve, dve.scalar_tensor_tensor(norm_r[:, :], norm_t[:, :], 1.5, norm_r[:, :], ALU.add, ALU.mult))
                if b == 0:
                    dve.wait_ge(ch_act, 2)
                if b >= 2:
                    dve.wait_ge(done["exps"], b - 1)
                step(dve, dve.scalar_tensor_tensor(zscale[:, b % 2, :], nq, 8.0, texp_sb[:, :], ALU.mult, ALU.mult))
                dve.wait_ge(done["sim"], b + 1)
                dve.tensor_tensor(z_sb[:, b % 2, :], SIM, nk, ALU.mult).then_inc(sim_read, 1)
                dve.wait_ge(sim_read, b + 1)
                step(dve, dve.tensor_reduce(zm[:, :], z_sb[:, b % 2, :].rearrange("p (h e) -> p h e", h=HP), AX, ALU.max))
                dve.scalar_tensor_tensor(zshift[:, b % 2, :], zm[:, :], -1.0, zscale[:, b % 2, :], ALU.mult,
                                         ALU.mult).then_inc(done["scores"], 1)

            def probs(b):
                dve.wait_ge(done["exps"], b + 1)
                e3 = ez[:, b % 2, :].rearrange("p (h e) -> p h e", h=HP)
                step(dve, dve.reciprocal(zs[:, b % 2, :], zs[:, b % 2, :]))
                if b >= 2:
                    dve.wait_ge(done["union"], b - 1)
                for i in range(2):
                    r = slice(64 * i, 64 * i + 64)
                    dve.tensor_tensor(attn[r, b % 2, :, r], e3[r], zs[r, b % 2, :].rearrange(
                        "p (h e) -> p h e", e=1).to_broadcast((64, HP, DH)), ALU.mult).then_inc(done["probs"], 1)

            def var2(b):
                dve.wait_ge(done["square"], b + 1)
                wide = lambda a, n: a.rearrange("p (a j k) -> p a j k", a=2, k=1).to_broadcast((TOK, 2, 3, n))
                four = lambda t: t.rearrange("p (a j) n -> p a j n", a=2)
                dve.tensor_scalar(rho2[:, 1, :], rho2[:, 0, :], 1.0 / D, EPS, ALU.mult,
                                  ALU.add).then_inc(done["var2"], 1)
                step(dve, dve.tensor_copy(mean2[:, :].rearrange("p (a j) -> p a j", a=2), TOK2[:, :, :, D]))
                dve.tensor_tensor(four(h2[:, NT * b:NT * b + NT, :]), TOK2[:, :, :, 0:D],
                                  wide(mean2[:, :], D), ALU.add).then_inc(h2_read, 1)

            def norm2(b):
                wide = lambda a, n: a.rearrange("p (a j k) -> p a j k", a=2, k=1).to_broadcast((TOK, 2, 3, n))
                four = lambda t: t.rearrange("p (a j) n -> p a j n", a=2)
                dve.wait_ge(done["rho2"], b + 1)
                polish(rho2[:, 2, :], rho2[:, 1, :], rho2[:, 0, :])
                if b >= 2:
                    dve.wait_ge(done["split_lo"], b - 1)
                dve.tensor_tensor(four(x2[:, b % 2])[:, :, :, 1:D], TOK2[:, :, :, 1:D], wide(rho2[:, 2, :], D - 1),
                                  ALU.mult).then_inc(x2_ready, 1)
                dve.tensor_tensor(four(lg[:, b % 2]), TOK2[:, :, :, D + 1:NC2], wide(rho2[:, 2, :], E),
                                  ALU.mult).then_inc(done["norm2"], 1)

            def top2(b):
                l, o, tail = lg[:, b % 2], oh[:, b % 2], xrow[:, b % 2, :, D:ROWF]
                if b == 0:
                    dve.wait_ge(load["br"], 16)
                if b >= 2:
                    dve.wait_ge(sent[b % 2], 2 * RSENT * (b // 2))
                    dve.wait_ge(done["exp_logits"], b - 1)
                if b >= 1:
                    dve.wait_ge(done["shares"], emitted_before("top2", b, "shares"))
                dve.wait_ge(done["norm2"], b + 1)
                bias = br_sb[0:TOK, :].rearrange("p (j e) -> p j e", j=1).to_broadcast((TOK, NT, E))
                step(dve, dve.tensor_tensor(l, l, bias, ALU.add))
                for j in range(NT):
                    last = dve.max(top[:, j, :], l[:, j, :])
                step(dve, last)
                dve.tensor_tensor(tops[:, b % 2], top[:, :, :], top[:, :, 0:1].to_broadcast((TOK, NT, E)),
                                  ALU.subtract).then_inc(lg_ready, 1)
                for j in range(NT):
                    last = dve.max_index(topi[:, j, :], top[:, j, :], l[:, j, :])
                step(dve, last)
                step(dve, dve.tensor_copy(tail[:, :, 0:2], topi[:, :, 0:2]))
                ids = exp_ids[0:TOK, :].rearrange("p (j e) -> p j e", j=1).to_broadcast((TOK, NT, E))
                for c in range(2):
                    last = dve.tensor_tensor(o[:, c], ids, tail[:, :, c:c + 1].to_broadcast((TOK, NT, E)), ALU.is_equal)
                step(dve, last)
                dve.tensor_tensor(mask[:, b % 2], o[:, 0], o[:, 1], ALU.add).then_inc(done["top2"], 1)

            def shares(b):
                tail = xrow[:, b % 2, :, D:ROWF]
                dve.wait_ge(done["exp_logits"], b + 1)
                step(dve, dve.tensor_reduce(sums[:, 0, :], exl[:, b % 2], AX, ALU.add))
                dve.wait_ge(done["top2"], b + 1)
                dve.tensor_reduce(mrow[:, :], mask[:, b % 2].rearrange("p j e -> p e j"), AX, ALU.add)
                step(dve, dve.tensor_scalar(sums[:, 0, :], sums[:, 0, :], WS * WS, None, ALU.mult))
                dve.tensor_tensor(msum[:, b + 1, :], mrow[:, :], msum[:, b, :], ALU.add).then_inc(counted, 1)
                step(dve, dve.reciprocal(tail[:, :, 2], sums[:, 0, :]))
                dve.tensor_tensor(tail[:, :, 3], exl[:, b % 2, :, 1], tail[:, :, 2], ALU.mult).then_inc(done["shares"], 1)

            def place(b):
                dve.wait_ge(done["rank"], b + 1)
                base = ebase[0:TOK, :].rearrange("p (j e) -> p j e", j=1).to_broadcast((TOK, NT, E))
                dve.tensor_tensor(rk[:, :, :], RANK, base, ALU.add).then_inc(rank_read, 1)
                dve.wait_ge(rank_read, b + 1)
                for c in range(2):
                    last = dve.tensor_tensor(rk2[:, c], oh[:, b % 2, c], rk[:, :, :], ALU.mult)
                step(dve, last)
                step(dve, dve.tensor_reduce(posf[:, :, :], rk2[:, :, :, :], AX, ALU.add))
                if b >= 2:
                    dve.wait_ge(sent[b % 2], 2 * RSENT * (b // 2))
                dve.wait_ge(done["shares"], b + 1)
                dve.tensor_copy(pos[:, b % 2], posf[:, :, :]).then_inc(done["place"], 1)

            here = dict(gram_rest=gram_rest, gram_low=gram_low, low_w=low_w, var=var, kappa=kappa, prods=prods, clamp=clamp, var2=var2, scores=scores, probs=probs, norm2=norm2, top2=top2, shares=shares, place=place)
            for name, b in SCHEDULE:
                if name in here:
                    here[name](b)

            dve.wait_ge(count_ps, 1)
            mid = lambda a, n: a.rearrange("p (e k) -> p e k", k=1).to_broadcast((128, a.shape[1], n))
            last = lambda a, n: a.rearrange("p (e k) -> p e k", e=1).to_broadcast((128, n, a.shape[1]))
            step(dve, dve.tensor_copy(cnt[:, :, :], COUNT))
            step(dve, dve.tensor_tensor(over[:, :, :], mid(cnt[:, 0, :], KT), last(ksteps[:, :], E), ALU.is_gt))
            step(dve, dve.tensor_reduce(tiles[:, :], over[:, :, :], AX, ALU.add))
            step(dve, dve.tensor_tensor(padf[:, :], cnt[:, 0, :], ebase[:, :], ALU.add))
            dve.tensor_copy(pads[:, :], padf[:, :]).then_inc(table_ready, 1)
            step(dve, dve.tensor_tensor_scan(cumend[:, :], ones[:, 0:E], tiles[:, :], 0.0, ALU.mult, ALU.add))
            step(dve, dve.tensor_tensor(past[:, :, :], mid(tindex[:, :], E), last(cumend[:, :], NTILES), ALU.is_ge))
            step(dve, dve.tensor_reduce(et[:, :], past[:, :, :], AX, ALU.add))
            step(dve, dve.tensor_tensor(past2[:, :, :], past[:, :, :], last(tiles[:, :], NTILES), ALU.mult))
            step(dve, dve.tensor_reduce(cstart[:, :], past2[:, :, :], AX, ALU.add))
            step(dve, dve.tensor_tensor(cstart[:, :], tindex[:, :], cstart[:, :], ALU.subtract))
            step(dve, dve.tensor_scalar(rowf[:, :], et[:, :], float(REGION), None, ALU.mult))
            step(dve, dve.scalar_tensor_tensor(rowf[:, :], cstart[:, :], float(TILE), rowf[:, :], ALU.mult, ALU.add))
            step(dve, dve.tensor_copy(table[:, :, 0], rowf[:, :]))
            step(dve, dve.tensor_scalar(rowf[:, :], et[:, :], float(E - 1), float(D), ALU.min, ALU.mult))
            step(dve, dve.tensor_copy(table[:, :, 1], rowf[:, :]))
            step(dve, dve.tensor_tensor(over[:, :, :], mid(cnt[:, 1, :], KT), last(ksteps[:, :], E), ALU.is_ge))
            step(dve, dve.tensor_reduce(early[:, :], over[:, :, 1:KT], AX, ALU.add))
            step(dve, dve.tensor_tensor(early[:, :], early[:, :], cumend[:, :], ALU.add))
            step(dve, dve.tensor_tensor(early[:, :], early[:, :], tiles[:, :], ALU.subtract))
            step(dve, dve.tensor_tensor(past[:, :, :], mid(tindex[:, :], E), last(early[:, :], NTILES), ALU.is_ge))
            step(dve, dve.tensor_reduce(late[:, :], past[:, :, :], AX, ALU.add))
            step(dve, dve.tensor_tensor(late[:, :], late[:, :], et[:, :], ALU.subtract))
            dve.tensor_scalar(table[:, :, 2], late[:, :], float(RSENT * (B - EARLY)), float(RSENT * EARLY), ALU.mult, ALU.add)
            dve.tensor_scalar(table[:, :, 3], late[:, :], float(16 * E), 16.0, ALU.mult, ALU.add).then_inc(table_ready, 1)

            def weigh(t, i, v):
                u = v % 2
                dve.wait_ge(x_in[v], 16 * i + 16)
                if since(t, XB):
                    dve.wait_ge(y_sent[v], 16 * BLK * i)
                tail = xin[:, v, :, D:ROWF]
                dve.tensor_scalar(mine[:, u], tail[:, :, 0:2], et[:, bass.ds(t, 1)], None,
                                  ALU.is_equal).then_inc(weigh1, 1)
                dve.wait_ge(weigh1, t + 1)
                for q in range(2):
                    ins = dve.tensor_tensor(both[:, u, :, q], tail[:, :, 2 + 2 * q:4 + 2 * q], mine[:, u], ALU.mult)
                ins.then_inc(weigh2, 1)
                dve.wait_ge(weigh2, t + 1)
                dve.tensor_reduce(cwd[:, v], both[:, u], AX, ALU.add).then_inc(weigh3, 1)
                dve.wait_ge(weigh3, t + 1)
                dve.tensor_scalar(dst[:, v], cwd[:, v, :, 1], FAR, None, ALU.add).then_inc(weights, 1)

            def low(t, u):
                dve.wait_ge(h_high, t + 1)
                if since(t, 2):
                    dve.wait_ge(y_ps, t - 1)
                dve.scalar_tensor_tensor(hlo[:, u].rearrange("p f n -> p (f n)"), HPS[u], 0.0,
                                         hhi[:, u].rearrange("p f n -> p (f n)"), ALU.max,
                                         ALU.subtract).then_inc(h_low, 1)

            def scale_y(t, u, v):
                dve.wait_ge(y_ps, t + 1)
                dve.tensor_tensor(ysb[:, v], YPS[u].rearrange("p (r n) -> p r n", n=D),
                                  cwd[:, v, :, 0:1].to_broadcast((128, BLK, D)), ALU.mult).then_inc(y_sbuf, 1)

            def tile(t, i, v):
                low(t, v % 2)
                if since(t, 1):
                    scale_y(t - 1, (v + 1) % 2, (v - 1) % XB)
                weigh(t + 1, i + (v + 1) // XB, (v + 1) % XB)

            weigh(0, 0, 0)
            over_tiles(dve, tile, 0, NTILES - 1)
            low(NTILES - 1, (NTILES - 1) % 2)
            for t in range(NTILES - 2, NTILES):
                scale_y(t, t % 2, t % XB)

            for b in range(B):
                dve.wait_ge(y_in[b % 4], 32 * (b // 4 + 1))
                y1, y2 = big[0:TOK, 2 * (b % 4), :], big[0:TOK, 2 * (b % 4) + 1, :]
                h = h2[:, NT * b:NT * b + NT, :].rearrange("p j n -> p (j n)")
                step(dve, dve.tensor_tensor(y1, y1, y2, ALU.add))
                dve.tensor_tensor(y1, y1, h, ALU.add).then_inc(summed, 1)

        @block.tensor
        def _(pe):
            def made(ins):
                ins.then_inc(setup_ps, 1)

            pe.wait_ge(consts, 18)
            pe.wait_ge(load["wlin"], 16)
            made(pe.transpose(ps_qk[:, 0, 0:D], wlin_sb[:, :], ident[:, :]))
            pe.wait_ge(setup_sb, 1)
            pe.wait_ge(setup_dve, 4)
            made(pe.matmul(ps_qk[:, 1, 0:KA], lhsT=wlinT[:, :], rhs=vext[:, :], start=True, stop=True))
            pe.wait_ge(load["wr"], 16)
            made(pe.matmul(ps_norm[:, 0:E], lhsT=cmat[:, 0:D], rhs=wr_sb[:, :], start=True, stop=True))
            pe.wait_ge(setup_dve, 6)
            made(pe.matmul(ps_sim[:, 0:KA], lhsT=cmat[:, 0:D], rhs=wc1T[:, :], start=True, stop=True))
            pe.wait_ge(setup_sb, 4)
            made(pe.matmul(ps_tok[0:KA, 0:NC2], lhsT=wc1T[:, :], rhs=cmat[:, :], start=True, stop=True))
            made(pe.matmul(ps_small[0:KA, 0:KA], lhsT=aT[:, :], rhs=aT[:, :], start=True, stop=True))
            for i in range(2):
                made(pe.matmul(ps_qk[0:KA, i, :], lhsT=aT[:, :], rhs=wg_sb[:, HD * i:HD * i + HD], start=True, stop=True))
            pe.wait_ge(load["wout"], 16)
            pe.wait_ge(setup_sb, 7)
            for p in range(HP):
                last = pe.transpose(ps_small[:, D * p:D * p + D], wout_sb[:, p, :], ident[:, :])
            made(last)
            pe.wait_ge(setup_sb, 10)
            for p in range(HP):
                last = pe.matmul(UNION[p // 3][:, p % 3, :], lhsT=woutT[:, p, :], rhs=cmat[:, :], start=True, stop=True)
            made(last)
            for p in range(HP):
                last = pe.matmul(ps_tok2[:, 0, KA * p:KA * p + KA], lhsT=wg_sb[:, 2 * HD + 128 * p:2 * HD + 128 * p + 128],
                                 rhs=aT[:, :], start=True, stop=True)
            made(last)
            pe.wait_ge(setup_sb, 12)

            def tokens(b):
                pe.wait_ge(smooth, b + 1)
                pe.wait_ge(ch_pool, b + 1)
                if b >= 1:
                    pe.wait_ge(done["gram_rest"], b)
                for j in range(NT):
                    last = pe.matmul(TOKS[:, j, :], lhsT=SR[0:KA, b, TOK * j:TOK * j + TOK], rhs=ik[:, :],
                                     start=True, stop=True)
                last.then_inc(done["tokens"], 1)

            def gram(b):
                pe.wait_ge(done["kappa"], b + 1)
                for j in range(NT):
                    last = pe.matmul(GRAM, lhsT=spT[:, b % 2, j, :], rhs=spT[:, b % 2, j, :],
                                     start=(j == 0), stop=(j == NT - 1))
                last.then_inc(done["gram"], 1)

            def turn(b):
                n2 = emitted_before("turn", b, "tokens2")
                if n2:
                    pe.wait_ge(done["norm2"], n2)
                if b >= 1:
                    pe.wait_ge(done["copy_turn"], b)
                for j in range(NT):
                    last = pe.transpose(ps_tok2[0:KA, j // 3, TOK * (j % 3):TOK * (j % 3) + TOK],
                                        spT[:, b % 2, j, :], ident[0:TOK, 0:TOK])
                last.then_inc(done["turn"], 1)

            def qk(b):
                pe.wait_ge(done["gram_low"], b + 1)
                if b == 0:
                    pe.wait_ge(qk_low, 1)
                if b >= 1:
                    pe.wait_ge(done["prods"], 2 * b)
                    pe.wait_ge(done["copy_k"], b)
                nu = emitted_before("qk", b, "union")
                if nu:
                    pe.wait_ge(done["copy_u"], nu)
                for i in range(2):
                    for n, g in enumerate((0, 0, 1)):
                        last = pe.matmul(ps_qk[0:KA, i, :], lhsT=g_sb[:, b % 2, g, :],
                                         rhs=qk_parts[:, n, HD * i:HD * i + HD], start=(n == 0), stop=(n == 2))
                last.then_inc(done["qk"], 1)

            def norms(b):
                pe.wait_ge(done["prods"], 2 * b + 2)
                if b >= 1:
                    pe.wait_ge(done["clamp"], b)
                for p in range(HP):
                    pe.matmul(NQ[:, p:p + 1], lhsT=prod[:, b % 2, 128 * p:128 * p + 128], rhs=ones[0:KA, 0:1],
                              start=True, stop=True)
                kp = prod[:, b % 2, HD:2 * HD].rearrange("k (p i e) -> k i p e", i=2, e=DH)
                for i in range(2):
                    last = pe.matmul(NK[64 * i:64 * i + 64, :], lhsT=ones[0:KA, 0:64], rhs=kp[:, i], start=True, stop=True)
                last.then_inc(done["norms"], 1)

            def sim(b):
                pe.wait_ge(done["copy_k"], b + 1)
                if b >= 1:
                    pe.wait_ge(sim_read, b)
                for h in range(H):
                    i, p = h % 2, h // 2
                    last = pe.matmul(SIM[64 * i:64 * i + 64, DH * p:DH * p + DH], lhsT=qk_w[:, DH * h:DH * h + DH],
                                     rhs=k_sb[:, b % 2, DH * h:DH * h + DH], start=True, stop=True)
                last.then_inc(done["sim"], 1)

            def union(b):
                pe.wait_ge(done["probs"], 2 * b + 2)
                pe.wait_ge(done["prods"], 2 * emitted_before("union", b, "prods"))
                if b >= 1:
                    pe.wait_ge(done["copy_u"], b)
                for p in range(HP):
                    last = pe.matmul(UNION[p // 3][:, p % 3, :], lhsT=attn[:, b % 2, p, :], rhs=wc_out[:, p, :],
                                     start=True, stop=True)
                last.then_inc(done["union"], 1)

            def bank_small(name, b):
                n = emitted_before(name, b, "px")
                if n:
                    pe.wait_ge(done["copy_px"], n)
                n = emitted_before(name, b, "rank")
                if n:
                    pe.wait_ge(rank_read, n)

            def px(b):
                pe.wait_ge(done["copy_u"], b + 1)
                bank_small("px", b)
                for p in range(HP):
                    last = pe.matmul(PX, lhsT=vT[:, p, :], rhs=u_sb[:, b % 2, p, :], start=(p == 0), stop=(p == HP - 1))
                last.then_inc(done["px"], 1)

            def tokens2(b):
                pe.wait_ge(done["copy_px"], b + 1)
                pe.wait_ge(done["copy_turn"], emitted_before("tokens2", b, "turn"))
                if b >= 1:
                    pe.wait_ge(done["norm2"], b)
                    pe.wait_ge(done["square"], b)
                for j in range(NT):
                    last = pe.matmul(TOK2[:, j // 3, j % 3, :], lhsT=SR[:, b, TOK * j:TOK * j + TOK], rhs=R[:, b % 2, :],
                                     start=True, stop=True)
                last.then_inc(done["tokens2"], 1)

            def rank(b):
                pe.wait_ge(done["top2"], b + 1)
                if b >= 1:
                    pe.wait_ge(counted, b)
                bank_small("rank", b)
                pe.matmul(RANK, lhsT=tri[0:TOK, 0:TOK], rhs=mask[:, b % 2], start=True, stop=False)
                for j in range(NT - 1):
                    pe.matmul(RANK[:, j + 1:NT, :], lhsT=onesb[0:TOK, 0:TOK],
                              rhs=mask[:, b % 2, j:j + 1, :].to_broadcast((TOK, NT - 1 - j, E)), start=False, stop=False)
                pe.matmul(RANK, lhsT=onesb[0:TOK, 0:TOK],
                          rhs=msum[:, b:b + 1, :].to_broadcast((TOK, NT, E)), start=False,
                          stop=True).then_inc(done["rank"], 1)

            here = dict(tokens=tokens, gram=gram, turn=turn, qk=qk, norms=norms, sim=sim, union=union,
                        px=px, tokens2=tokens2, rank=rank)
            for name, b in SCHEDULE:
                if name in here:
                    here[name](b)

            pe.wait_ge(counted, B)
            pe.wait_ge(rank_read, B)
            for i, b in enumerate((B, EARLY)):
                last = pe.matmul(COUNT[:, i, :], lhsT=onesb[0:TOK, :], rhs=msum[:, b, :], start=True, stop=True)
            last.then_inc(count_ps, 1)
            pe.wait_ge(table_ready, 2)
            pe.wait_ge(wlow, len(CHUNKS))

            def turn_x(t, i, v):
                u = v % 2
                pe.wait_ge(x_in[v], 16 * i + 16)
                if since(t, 2):
                    pe.wait_ge(x_sbuf, t - 1)
                for s in range(2):
                    for r in range(BLK):
                        last = pe.transpose(XPS[u][:, TILE * s + 128 * r:TILE * s + 128 * r + 128],
                                            xin16[:, v, r, D * s:D * s + D], ident16[:, :])
                last.then_inc(x_ps, 1)

            expert_at = [pe.alloc_register(f"expert_at{u}") for u in range(2)]

            def chunk(weights, f, at):
                return weights[:, 128 * f:E * F - 128 * (FC - 1 - f)][:, bass.ds(at, 128)]

            def hidden(t, u):
                pe.reg_load(expert_at[u], table[0:1, bass.ds(t, 1), 1:2])
                at = pe.snap(expert_at[u], min_val=0, max_val=(E - 1) * D) * FC
                pe.wait_ge(x_sbuf, t + 1)
                if since(t, 2):
                    pe.wait_ge(h_low, t - 1)
                for f in range(FC):
                    to = HPS[u][:, TILE * f:TILE * f + TILE]
                    high = chunk(w1h, f, at)
                    pe.matmul(to, lhsT=high, rhs=xT[:, u, 0, :], start=True, stop=False)
                    pe.matmul(to, lhsT=high, rhs=xT[:, u, 1, :], start=False, stop=False)
                    last = pe.matmul(to, lhsT=chunk(w1l, f, at), rhs=xT[:, u, 0, :], start=False, stop=True)
                last.then_inc(h_ps, 1)

            def result(t, u):
                at = pe.snap(expert_at[u], min_val=0, max_val=(E - 1) * D)
                pe.wait_ge(h_low, t + 1)
                if since(t, 2):
                    pe.wait_ge(y_sbuf, t - 1)
                for r in range(BLK):
                    to = YPS[u][:, D * r:D * r + D]
                    for f in range(FC):
                        hi, lo = (h[:, u, f, 128 * r:128 * r + 128] for h in (hhi, hlo))
                        pe.matmul(to, lhsT=hi, rhs=chunk(w2h, f, at * FC), start=(f == 0), stop=False)
                        pe.matmul(to, lhsT=hi, rhs=chunk(w2l, f, at * FC), start=False, stop=False)
                        pe.matmul(to, lhsT=lo, rhs=chunk(w2h, f, at * FC), start=False, stop=False)
                    last = pe.matmul(to, lhsT=ones16[0:64, 0:128], rhs=b2h[:, bass.ds(at, D)], start=False, stop=True)
                last.then_inc(y_ps, 1)

            turn_x(0, 0, 0)
            turn_x(1, 0, 1)
            hidden(0, 0)

            def tile(t, i, v):
                turn_x(t + 2, i + (v + 2) // XB, (v + 2) % XB)
                hidden(t + 1, (v + 1) % 2)
                result(t, v % 2)

            over_tiles(pe, tile, 0, NTILES - 2)
            hidden(NTILES - 1, (NTILES - 1) % 2)
            result(NTILES - 2, NTILES % 2)
            result(NTILES - 1, (NTILES - 1) % 2)


_INS = ["x", "L0_tok_W_ve", "L0_tok_b_ve", "L0_tok_W_lin", "L0_tok_b_lin", "L0_attn_gamma", "L0_attn_w_qkv",
        "L0_attn_temperature", "L0_attn_w_out", "L0_ffn_Wr", "L0_ffn_br", "L0_ffn_W1", "L0_ffn_b1",
        "L0_ffn_W2", "L0_ffn_b2"]


def kernel(**inputs):
    import numpy as _np
    import concourse.bacc as _bacc
    from concourse import mybir as _mybir
    from concourse.bass_utils import run_bass_kernel_spmd as _run

    nc = _bacc.Bacc("TRN2", target_bir_lowering=False, num_devices=1)
    arrays, args = {}, []
    for name in _INS:
        a = _np.ascontiguousarray(inputs[name])
        arrays[f"in_{name}"] = a
        args.append(nc.dram_tensor(f"in_{name}", a.shape, _mybir.dt.from_np(a.dtype), kind="ExternalInput").ap())
    out = nc.dram_tensor("out", (B, T, D), F32, kind="ExternalOutput").ap()
    rows = nc.dram_tensor("rows", (ROWS, ROWF), F32).ap()
    parts = nc.dram_tensor("parts", (2 * NTOK, D), F32).ap()
    audio_tower(nc, *args, out, rows, parts)
    r = _run(nc, [arrays], core_ids=[0])
    return r.results[0]["out"]
```

```python
from contextlib import ExitStack

import concourse.bass as bass
from concourse import mybir

ALU = mybir.AluOpType
ACT = mybir.ActivationFunctionType
AX = mybir.AxisListType.X
F32 = mybir.dt.float32
F16 = mybir.dt.float16
BF16 = mybir.dt.bfloat16
I32 = mybir.dt.int32
U32 = mybir.dt.uint32

B, C, T, D = 8, 32, 750, 128
H, DH = 8, 64
HD = H * DH
HP = H // 2
E, F = 8, 512
FC = F // D
KA = C + 1
KS = 64 + KA
NT, TOK = 6, 125
NTOK = B * T
GB = 128 // C
NC2 = D + 1 + E
DECAY = 0.9
TINY2 = 1e-24
LN2 = 0.6931471805599453
UP_TOKEN, UP_HEAD = 42, 30
EPS = 1e-5

TILE = 256
BLK = TILE // 128
NTILES = (2 * NTOK + E * (TILE - 1)) // TILE
REGION = NTOK + TILE
SPARE = NTILES - 2 * NTOK // TILE + 1
ROWS = E * REGION + SPARE * TILE
TAIL = 5
ROWF = D + TAIL
KT = NTOK // TILE + 1
XB = 8
EARLY = B - 2
EARLY_TILES = (2 * EARLY * T - E * (TILE - 1)) // TILE // XB * XB
FAR = float(1 << 14)
RSENT = 16 * NT
LANDED = 16 * BLK
WCH = 1024
WS = 16.0

CHUNKS = [(k, n) for k in ("w1", "w2") for n in range(E * F // WCH)] + [("b2", 0)]
CHUNK_STEP = 2

STAGES = [
    ("tokens", 0), ("split_hi", 4), ("rank", 4), ("copy_s", 0), ("qk", 1), ("split_lo", 4), ("shares", 4),
    ("exps", 2), ("place", 4), ("var", 0), ("copy_k", 1), ("tokens2", 3), ("prods", 1), ("rho", 0), ("rest", 0),
    ("kappa", 0), ("square", 3), ("var2", 3), ("probs", 2), ("sim", 1), ("norms", 1), ("rho2", 3),
    ("gram", 0), ("clamp", 1), ("norm2", 3), ("shift_w", 1), ("high_w", 1), ("copy_gram", 0), ("union", 2),
    ("gram_rest", 0), ("qk_split", 0), ("low_w", 1), ("turn", 0), ("top2", 3), ("roots", 1), ("gram_mid", 0), ("copy_u", 2),
    ("gram_low", 0), ("px", 2), ("scatter", 4), ("scores", 1), ("copy_px", 2), ("copy_turn", 0),
    ("exp_logits", 3),
]
SCHEDULE = [(name, s - lag) for s in range(B + max(lag for _, lag in STAGES))
            for name, lag in STAGES if 0 <= s - lag < B]


def emitted_before(name, b, other):
    at = SCHEDULE.index((name, b))
    return sum(n == other for n, _ in SCHEDULE[:at])


def audio_tower(nc, x, w_ve, b_ve, w_lin, b_lin, gamma, w_qkv, temperature, w_out,
                w_r, b_r, w1, b1, w2, b2, out, rows):
    with ExitStack() as ctx:
        def sb(name, shape, dt=F32):
            return ctx.enter_context(nc.sbuf_tensor(name, shape, dt))

        def pb(name, shape, dt=F32):
            return ctx.enter_context(nc.psum_tensor(name, shape, dt))

        def sem(name):
            return ctx.enter_context(nc.semaphore(name))

        wlin_sb = sb("wlin_sb", [D, D])
        vext = sb("vext", [D, KA])
        wve_sb = sb("wve_sb", [D, C])
        blin_sb = sb("blin_sb", [D, 1])
        gamma_sb = sb("gamma_sb", [D, 1])
        wqkv_sb = sb("wqkv_sb", [D, 3 * HD])
        wg_sb = sb("wg_sb", [D, 3 * HD])
        temp_sb = sb("temp_sb", [128, H])
        texp_sb = sb("texp_sb", [128, HP])
        wout_sb = sb("wout_sb", [128, HP, D])
        woutT = wqkv_sb[:, 0:HP * D].rearrange("p (h n) -> p h n", h=HP)
        wc_out = sb("wc_out", [128, HP, NC2])
        wr_sb = sb("wr_sb", [D, E])
        br_sb = sb("br_sb", [128, E])
        ident = sb("ident", [128, 128])
        ident16 = sb("ident16", [128, 128], F16)
        ones = sb("ones", [128, 128])
        ones16 = sb("ones16", [128, 128], F16)
        tri = sb("tri", [128, 128], BF16)
        onesb = sb("onesb", [128, 128], BF16)
        cmat = sb("cmat", [D, NC2])
        wlinT = sb("wlinT", [D, D])
        wc1T = sb("wc1T", [D, KA])
        aT = sb("aT", [D, KA])
        ik = sb("ik", [KA, 2 * KA])
        qk_w = sb("qk_w", [KA, 2 * HD])
        vT = sb("vT", [128, HP, KA])
        exp_ids = sb("exp_ids", [128, E])
        ebase = sb("ebase", [128, E])
        lift = sb("lift", [128, 2])
        dests = sb("dests", [TOK, B * NT, 1])

        big = sb("big", [128, 8, NT * D])
        x_sb, diff, lr, rl = (big[:, 2 * i:2 * i + 2, 0:T] for i in range(4))
        rl0 = sb("rl0", [128, 2])
        decay = sb("decay", [128, 1])
        SR = sb("SR", [KS, B, T])
        R = sb("R", [KS, 2, NC2])

        sT = sb("sT", [TOK, 2, NT, KA])
        quad = sb("quad", [TOK, NT, KA])
        kap = sb("kap", [TOK, 4, NT])
        spT = sb("spT", [TOK, 2, NT, KA])
        g_sb = sb("g_sb", [KS, 2, 2, KA], BF16)
        g_rest = sb("g_rest", [KA, 2, KA])
        g_mid = sb("g_mid", [KA, 2, KA], BF16)
        qk_parts = sb("qk_parts", [KS, 3, 2 * HD], BF16)
        k_sb = sb("k_sb", [KA, 2, HD])
        prod = sb("prod", [KA, 2, 2 * HD])
        norm_c = sb("norm_c", [128, HP * DH + HP])
        norm_r = sb("norm_r", [128, HP * DH + HP])
        norm_t = sb("norm_t", [128, HP * DH + HP])
        z_sb = sb("z_sb", [128, 2, HP * DH])
        zm = sb("zm", [128, HP])
        zscale = sb("zscale", [128, 2, HP])
        zshift = sb("zshift", [128, 2, HP])
        ez = sb("ez", [128, 2, HP * DH])
        zs = sb("zs", [128, 2, HP])
        attn = sb("attn", [128, 2, HP, 128])
        u_sb = sb("u_sb", [128, 2, HP, NC2])
        sq_sb = wg_sb[0:TOK, 0:NT * D].rearrange("p (j n) -> p j n", j=NT)
        mean2 = sb("mean2", [TOK, NT])
        rho2 = sb("rho2", [TOK, 3, NT])
        h2 = sb("h2", [TOK, B * NT, D])
        x2 = sb("x2", [TOK, 2, NT, D])
        lg = sb("lg", [TOK, 2, NT, E])
        top = sb("top", [TOK, NT, E])
        tops = sb("tops", [TOK, 2, NT, E])
        topi = sb("topi", [TOK, NT, E], U32)
        exl = sb("exl", [TOK, 2, NT, E])
        oh = sb("oh", [TOK, 2, 2, NT, E])
        mask = sb("mask", [TOK, 2, NT, E], BF16)
        msum = sb("msum", [TOK, B + 1, E], BF16)
        mrow = sb("mrow", [TOK, E])
        sums = sb("sums", [TOK, 1, NT])
        rk = sb("rk", [TOK, NT, E])
        rk2 = sb("rk2", [TOK, 2, NT, E])
        posf = sb("posf", [TOK, 2, NT])
        pos = sb("pos", [TOK, 2, 2, NT], U32)
        xrow = sb("xrow", [TOK, 2, NT, ROWF])
        xrow16 = xrow[:, :, :, :].bitcast(F16)

        wraw = sb("wraw", [128, 2, WCH])
        w1h = sb("w1h", [128, E * F], F16)
        w1l = sb("w1l", [128, E * F], F16)
        w2h = sb("w2h", [128, E * F], F16)
        w2l = sb("w2l", [128, E * F], F16)
        w1row = sb("w1row", [128, 2, WCH])
        b2h = sb("b2h", [64, E * D], F16)
        zrow = sb("zrow", [128, BLK * ROWF])
        ksteps = sb("ksteps", [128, KT])
        tindex = sb("tindex", [128, NTILES])
        cnt = sb("cnt", [128, E])
        over = sb("over", [128, E, KT])
        tiles = sb("tiles", [128, E])
        groups = sb("groups", [128, 2 * E])
        starts = sb("starts", [128, 2 * E + 1])
        ends = sb("ends", [128, 2 * E])
        skip = sb("skip", [128, 2 * E])
        group = sb("group", [128, NTILES + 1])
        et = sb("et", [128, NTILES])
        changed = sb("changed", [128, NTILES])
        first_row = sb("first_row", [128, NTILES])
        table = sb("table", [128, NTILES, 3], I32)
        pads = sb("pads", [128, E], I32)

        flat = big[:, :, :].rearrange("p a n -> p (a n)")
        rows_end = XB * BLK * ROWF
        results_end = rows_end + XB * BLK * D
        xin_flat, ysb_flat = flat[:, 0:rows_end], flat[:, rows_end:results_end]
        past, past2 = (flat[:, results_end + 512 * i:results_end + 512 * (i + 1)] for i in range(2))
        xin = xin_flat.rearrange("p (u r n) -> p u r n", u=XB, r=BLK)
        xin16 = xin_flat.bitcast(F16).rearrange("p (u r n) -> p u r n", u=XB, r=BLK)
        ysb = ysb_flat.rearrange("p (u r n) -> p u r n", u=XB, r=BLK)
        over1, over2 = wqkv_sb[:, :].bitcast(F16), wg_sb[:, :].bitcast(F16)
        hhi = over1[:, 0:2 * FC * TILE].rearrange("p (u f n) -> p u f n", u=2, f=FC)
        xT = over1[:, 2 * FC * TILE:2 * (FC + 2) * TILE].rearrange("p (u s n) -> p u s n", u=2, s=2)
        hlo = over2[:, 0:2 * FC * TILE].rearrange("p (u f n) -> p u f n", u=2, f=FC)
        mine = sb("mine", [128, 2, BLK, 2])
        cw = sb("cw", [128, XB, BLK, 1])
        dst = sb("dst", [128, XB, BLK], U32)

        ps_tok = pb("ps_tok", [128, 512])
        ps_small = pb("ps_small", [128, 512])
        ps_qk = pb("ps_qk", [128, 2, 512])
        ps_norm = pb("ps_norm", [128, 512])
        ps_sim = pb("ps_sim", [128, 512])
        ps_tok2 = pb("ps_tok2", [128, 2, 512])
        GRAM = ps_tok[0:KA, 2 * KA * NT:2 * KA * NT + KA]
        TOKS = ps_tok[0:TOK, 0:2 * KA * NT].rearrange("p (j k) -> p j k", k=2 * KA)
        PX = ps_small[0:KA, 64:64 + NC2]
        RANK = ps_small[0:TOK, 256:256 + NT * E].rearrange("p (j e) -> p j e", e=E)
        COUNT = ps_small[:, 320:320 + E]
        NQ = ps_norm[:, HP * DH:HP * DH + HP]
        NK = ps_norm[:, 0:HP * DH]
        SIM = ps_sim[:, 0:HP * DH]
        UNION = [ps_qk[:, 0, 0:3 * NC2].rearrange("p (h n) -> p h n", n=NC2),
                 ps_qk[:, 1, 0:NC2].rearrange("p (h n) -> p h n", n=NC2)]
        TOK2 = ps_tok2[0:TOK, :, 0:3 * NC2].rearrange("p a (j n) -> p a j n", n=NC2)

        XPS = [ps_tok[:, :].bitcast(F16), ps_small[:, :].bitcast(F16)]
        HPS = [ps_qk[:, :, :].rearrange("p a n -> p (a n)"), ps_tok2[:, :, :].rearrange("p a n -> p (a n)")]
        YPS = [ps_norm[:, 0:BLK * D], ps_sim[:, 0:BLK * D]]

        wload = [sem("wload0"), sem("wload1")]
        wshifted = sem("wshifted")
        whigh = sem("whigh")
        wlow = sem("wlow")
        zeroed = sem("zeroed")
        zeros = sem("zeros")
        count_ps = sem("count_ps")
        table_ready = sem("table_ready")
        pads_ready = sem("pads_ready")
        count_read = sem("count_read")
        x_in = [sem(f"x_in{i}") for i in range(XB)]
        x_ps = sem("x_ps")
        x_sbuf = sem("x_sbuf")
        h_ps = sem("h_ps")
        h_high = sem("h_high")
        h_low = sem("h_low")
        y_ps = sem("y_ps")
        y_sbuf = sem("y_sbuf")
        weights = sem("weights")
        h2_out = sem("h2_out")
        added = [sem("added0"), sem("added1")]
        load = {n: sem(f"load_{n}") for n in (
            "x0", "x1", "wlin", "wve", "bve", "blin", "gamma", "wqkv", "temp", "wout", "wr", "br")}
        consts = sem("consts")
        ch_pool = sem("ch_pool")
        ch_dve = sem("ch_dve")
        ch_act = sem("ch_act")
        setup_ps = sem("setup_ps")
        setup_sb = sem("setup_sb")
        scans = sem("scans")
        smooth = sem("smooth")
        done = {name: sem(f"done_{name}") for name, _ in STAGES}
        quad_read = sem("quad_read")
        sim_read = sem("sim_read")
        h2_read = sem("h2_read")
        x2_ready = sem("x2_ready")
        lg_ready = sem("lg_ready")
        tail_ready = sem("tail_ready")
        sent = [sem("sent0"), sem("sent1")]
        setup_dve = sem("setup_dve")
        counted = sem("counted")
        weigh1 = sem("weigh1")
        rank_read = sem("rank_read")
        parts_zeroed = sem("parts_zeroed")
        qk_high = sem("qk_high")
        qk_mid = sem("qk_mid")
        qk_low = sem("qk_low")
        qk_rest_ready = sem("qk_rest_ready")
        qk_rest = prod[:, 0, :]

        def chained(semaphore):
            count = [0]

            def step(eng, ins):
                count[0] += 1
                ins.then_inc(semaphore, 1)
                eng.wait_ge(semaphore, count[0])
            return step

        def split_of(kind, n):
            at = slice(WCH * n, WCH * n + WCH)
            if kind == "w1":
                return w1h[:, at], w1l[:, at]
            if kind == "w2":
                return w2h[:, at], w2l[:, at]
            return b2h[0:1, :], b2h[32:33, :]

        def loads_before(k):
            return sum(3 if kind == "w1" else 2 for j, (kind, _) in enumerate(CHUNKS[:k + 1]) if j % 2 == k % 2)

        def over_tiles(eng, body, first, end):
            at = min(-(-max(first, 1) // XB) * XB, end)
            for t in range(first, at):
                body(t, t // XB, t % XB)
            loops = (at // XB, end // XB)
            if loops[0] < loops[1]:
                with eng.Fori(*loops) as i:
                    for v in range(XB):
                        body(XB * i + v, i, v)
                at = XB * loops[1]
            for t in range(at, end):
                body(t, t // XB, t % XB)

        def since(t, n):
            return not isinstance(t, int) or t >= n

        block = ctx.enter_context(nc.Block())

        @block.sync
        def _(sp):
            for g in range(2):
                sp.dma_start(x_sb[:, g, :], x[GB * g:GB * (g + 1)].rearrange("b c t -> (b c) t")).then_inc(load[f"x{g}"], 16)
            sp.dma_start(wlin_sb[:, :], w_lin).then_inc(load["wlin"], 16)
            sp.dma_start(wve_sb[:, :], w_ve).then_inc(load["wve"], 16)
            sp.dma_start(vext[:, C:KA], b_ve.rearrange("(d a) -> d a", a=1)).then_inc(load["bve"], 16)
            sp.dma_start(blin_sb[:, :], b_lin.rearrange("(d a) -> d a", a=1)).then_inc(load["blin"], 16)
            sp.dma_start(wr_sb[:, :], w_r).then_inc(load["wr"], 16)
            sp.dma_start(gamma_sb[:, :], gamma.rearrange("(d a) -> d a", a=1)).then_inc(load["gamma"], 16)
            sp.dma_start(wqkv_sb[:, :], w_qkv).then_inc(load["wqkv"], 16)
            sp.dma_start(temp_sb[:, :], temperature.rearrange("h a b -> (a b) h").to_broadcast((128, H))).then_inc(load["temp"], 16)
            sp.dma_start(wout_sb[:, :, :], w_out.rearrange("(p r) n -> r p n", r=128)).then_inc(load["wout"], 16)
            sp.dma_start(br_sb[:, :], b_r.rearrange("(a e) -> a e", a=1).to_broadcast((128, E))).then_inc(load["br"], 16)
            w1v = w1.rearrange("e d f -> d e f")
            w2v = w2.rearrange("e (c p) n -> p e c n", p=128)
            for k, (kind, n) in enumerate(CHUNKS):
                if k >= 2:
                    sp.wait_ge(wlow, k - 1)
                raw, row = wraw[:, k % 2, :], w1row[1:128, k % 2, :]
                if kind == "w1":
                    at = slice(2 * n, 2 * n + 2)
                    sp.dma_start(raw[1:128, :].rearrange("p (e f) -> p e f", e=2), w1v[1:D, at, :]).then_inc(wload[k % 2], 16)
                    sp.dma_start(raw[0:1, :].rearrange("p (e f) -> p e f", e=2),
                                 b1[at].rearrange("(a e) f -> a e f", a=1)).then_inc(wload[k % 2], 16)
                    sp.dma_start(row.rearrange("p (e f) -> p e f", e=2),
                                 w1v[0:1, at, :].to_broadcast((D - 1, 2, F))).then_inc(wload[k % 2], 16)
                elif kind == "w2":
                    for i in range(2):
                        sp.dma_start(raw[:, F * i:F * i + F].rearrange("p (c n) -> p c n", n=D),
                                     w2v[:, 2 * n + i]).then_inc(wload[k % 2], 16)
                else:
                    for r in (0, 32):
                        sp.dma_start(raw[r:r + 1, :], b2.rearrange("(a e) f -> a (e f)", a=1)).then_inc(wload[k % 2], 16)
            sp.wait_ge(zeroed, 3)
            sp.dma_start(rows[E * REGION:ROWS, :].rearrange("(s p r) n -> p s (r n)", p=128, r=BLK),
                         zrow[:, :].rearrange("p (a n) -> p a n", a=1).to_broadcast((128, SPARE, BLK * ROWF))
                         ).then_inc(zeros, 16)
            for b in range(B):
                sp.wait_ge(h2_read, b + 1)
                sp.dma_start(out[b].rearrange("(j p) n -> p j n", p=TOK), h2[:, NT * b:NT * b + NT, :]).then_inc(h2_out, 16)

            def load_tile(t, i, v):
                if since(t, XB):
                    sp.wait_ge(x_ps, t - XB + 1)
                    sp.wait_ge(weights, t - XB + 1)
                first = sp.value_load(table[0:1, bass.ds(t, 1), 0:1], min_val=0, max_val=ROWS - TILE)
                sp.dma_start(xin[:, v].rearrange("p r n -> p (r n)"),
                             rows[bass.ds(first, TILE), :].rearrange("(p r) n -> p (r n)", r=BLK)).then_inc(x_in[v], 16)

            sp.wait_ge(table_ready, 1)
            for i in range(2):
                sp.wait_ge(sent[i], RSENT * EARLY)
            over_tiles(sp, load_tile, 0, XB)
            sp.wait_ge(pads_ready, 1)
            sp.wait_ge(zeros, 16)
            for e in range(E):
                first = sp.value_load(pads[0:1, e:e + 1], min_val=0, max_val=E * REGION - TILE)
                sp.dma_start(rows[bass.ds(first, TILE), :].rearrange("(p r) n -> p (r n)", r=BLK),
                             zrow[:, :]).then_inc(zeros, 16)
            over_tiles(sp, load_tile, XB, EARLY_TILES)
            sp.wait_ge(table_ready, 2)
            for i in range(2):
                sp.wait_ge(sent[i], RSENT * B)
            sp.wait_ge(zeros, 16 + 16 * E)
            over_tiles(sp, load_tile, EARLY_TILES, NTILES)

            for u in range(2):
                sp.wait_ge(added[u], LANDED * (NTILES // 2))

        @block.gpsimd
        def _(pool):
            step = chained(ch_pool)
            made = [0]

            def const(ins):
                made[0] += 1
                ins.then_inc(consts, 1)
                pool.wait_ge(consts, made[0])

            const(pool.memset(ones[:, :], 1.0))
            const(pool.memset(ones16[:, :], 1.0))
            const(pool.memset(onesb[:, :], 1.0))
            const(pool.memset(decay[:, :], DECAY))
            const(pool.memset(lift[:, 0:1], UP_TOKEN / 2 * LN2))
            const(pool.memset(lift[:, 1:2], UP_HEAD / 2 * LN2))
            const(pool.memset(attn[:, :, :, :], 0.0))
            const(pool.memset(msum[:, 0, :], 0.0))
            const(pool.memset(x2[:, :, :, 0:1], 1.0))
            const(pool.memset(R[32:64, :, :], 0.0))
            const(pool.affine_select(out=ident[:, :], in_=ones[:, :], compare_op=ALU.is_equal, fill=0.0,
                               base=0, pattern=[[-1, 128]], channel_multiplier=1))
            const(pool.affine_select(out=ident16[:, :], in_=ones16[:, :], compare_op=ALU.is_equal, fill=0.0,
                               base=0, pattern=[[-1, 128]], channel_multiplier=1))
            const(pool.affine_select(out=tri[:, :], in_=onesb[:, :], compare_op=ALU.is_gt, fill=0.0,
                               base=0, pattern=[[1, 128]], channel_multiplier=-1))
            const(pool.iota(ksteps[:, :], [[TILE, KT]], base=0, channel_multiplier=0,
                            allow_small_or_imprecise_dtypes=True))
            const(pool.iota(tindex[:, :], [[1, NTILES]], base=0, channel_multiplier=0,
                            allow_small_or_imprecise_dtypes=True))
            const(pool.iota(exp_ids[:, :], [[1, E]], base=0, channel_multiplier=0,
                      allow_small_or_imprecise_dtypes=True))
            const(pool.iota(ebase[:, :], [[REGION, E]], base=0, channel_multiplier=0,
                      allow_small_or_imprecise_dtypes=True))
            const(pool.iota(dests[:, :, 0], [[TOK, B * NT]], base=-int(FAR), channel_multiplier=1,
                      allow_small_or_imprecise_dtypes=True))
            def zero(semaphore, areas):
                for n, area in enumerate(areas):
                    pool.memset(area, 0.0).then_inc(semaphore, 1)
                    pool.wait_ge(semaphore, n + 1)

            for b in range(B):
                g, i = b // GB, b % GB
                step(pool, pool.memset(SR[32:64, b, :], 1.0))
                pool.wait_ge(scans, 2 * g + 2)
                pool.tensor_tensor(SR[0:C, b, :], lr[C * i:C * i + C, g, :], rl[C * i:C * i + C, g, :],
                                   ALU.add).then_inc(smooth, 1)
                pool.wait_ge(smooth, b + 1)
                if b == 1:
                    zero(parts_zeroed, (g_sb[32:64, :, :, :], qk_parts[32:64, :, :]))
            zero(zeroed, (w1row[0:1, :, :], b2h[:, :], zrow[:, :]))

            def shift_w(s):
                for k in range(CHUNK_STEP * s, min(CHUNK_STEP * (s + 1), len(CHUNKS))):
                    kind, n = CHUNKS[k]
                    if kind == "w1":
                        pool.wait_ge(wload[k % 2], 16 * loads_before(k))
                        pool.wait_ge(zeroed, 1)
                        pool.tensor_tensor(wraw[:, k % 2, :], wraw[:, k % 2, :], w1row[:, k % 2, :],
                                           ALU.subtract).then_inc(wshifted, 1)
                        pool.wait_ge(wshifted, n + 1)

            def split_lo(b):
                pool.wait_ge(done["split_hi"], b + 1)
                pool.tensor_tensor(xrow16[:, b % 2, :, D:2 * D], x2[:, b % 2], xrow16[:, b % 2, :, 0:D],
                                   ALU.subtract).then_inc(done["split_lo"], 1)
                pool.wait_ge(done["split_lo"], b + 1)
                tail = xrow[:, b % 2, :, D + 4:D + 5]
                pool.tensor_copy(tail, dests[:, NT * b:NT * b + NT, :]).then_inc(tail_ready, 1)

            def scatter(b):
                pool.wait_ge(done["place"], b + 1)
                pool.wait_ge(done["split_lo"], b + 1)
                pool.wait_ge(tail_ready, b + 1)
                for c in range(2):
                    for j in range(NT):
                        pool.indirect_dma_start(
                            rows, bass.IndirectOffsetOnAxis(ap=pos[:, b % 2, c, j:j + 1], axis=0),
                            xrow[:, b % 2, j, :], None).then_inc(sent[b % 2], 16)

            for name, b in SCHEDULE:
                if name == "shift_w":
                    shift_w(b)
                elif name == "split_lo":
                    split_lo(b)
                elif name == "scatter":
                    scatter(b)

            bound = pool.alloc_register("bound")

            def send(t, i, v):
                u, last = v % 2, NTOK - 1
                mine_before, others_before = XB // 2 * i + v // 2, XB // 2 * i + (v + 1) // 2
                if not since(t, 3):
                    pool.wait_ge(y_sbuf, t + 1)
                    if mine_before:
                        pool.wait_ge(added[u], LANDED * mine_before)
                    if others_before:
                        pool.wait_ge(added[1 - u], LANDED * others_before)
                else:
                    first = pool.value_load(table[0:1, bass.ds(t, 1), 2:3], min_val=0, max_val=LANDED)
                    others = pool.snap(first + LANDED * (others_before - 1), min_val=LANDED, max_val=LANDED * NTILES)
                    number = pool.to_reg(t + NTOK)
                    pool.wait_ge(y_sbuf, t + 1)
                    pool.wait_ge(added[u], LANDED * mine_before)
                    pool.wait_ge(added[1 - u], others)
                    pool.reg_alu(bound, number, NTOK - 1, op=ALU.min)
                    last = bound
                for r in range(BLK):
                    pool.indirect_dma_start(
                        out_rows, bass.IndirectOffsetOnAxis(ap=dst[:, v, r:r + 1], axis=0), ysb[:, v, r, :], None,
                        bounds_check=last, oob_is_err=False, compute_op=ALU.add).then_inc(added[u], 16)

            out_rows = out.rearrange("b t n -> (b t) n")
            pool.wait_ge(h2_out, 16 * B)
            pool.wait_ge(table_ready, 2)
            over_tiles(pool, send, 0, NTILES)

        @block.scalar
        def _(act):
            step = chained(ch_act)

            def copied(n, dst, src, scale=1.0):
                act.wait_ge(setup_ps, n + 1)
                act.activation(dst, src, ACT.Copy, scale=scale).then_inc(setup_sb, 1)

            act.preload_act_table_set("natural_log_exp_and_others")
            act.wait_ge(load["temp"], 16)
            for i in range(2):
                step(act, act.activation(texp_sb[64 * i:64 * i + 64, :], temp_sb[64 * i:64 * i + 64, i::2], ACT.Exp))
            copied(0, wlinT[:, :], ps_qk[:, 0, 0:D])
            copied(1, wc1T[:, :], ps_qk[:, 1, 0:KA])
            copied(2, cmat[:, D + 1:NC2], ps_norm[:, 0:E])
            copied(3, aT[:, :], ps_sim[:, 0:KA])
            act.wait_ge(consts, 9)
            act.wait_ge(setup_ps, 5)
            act.activation(R[0:KA, 0, :], ps_tok[0:KA, 0:NC2], ACT.Copy).then_inc(setup_sb, 1)
            act.activation(R[0:KA, 1, :], ps_tok[0:KA, 0:NC2], ACT.Copy).then_inc(setup_sb, 1)
            copied(5, ik[:, KA:2 * KA], ps_small[0:KA, 0:KA], 1.0 / D)
            copied(6, qk_w[:, 0:HD], ps_qk[0:KA, 0, :])
            copied(7, qk_w[:, HD:2 * HD], ps_qk[0:KA, 1, :])

            def rest(b):
                if b:
                    return
                act.wait_ge(parts_zeroed, 2)
                act.wait_ge(setup_sb, 9)
                for n in (0, 2):
                    last = act.activation(qk_parts[0:KA, n, :], qk_w[:, :], ACT.Copy)
                last.then_inc(qk_high, 1)
                act.wait_ge(setup_dve, 5)
                copied(8, woutT, ps_small[:, :].rearrange("p (h n) -> p h n", h=HP))
                act.wait_ge(setup_ps, 10)
                act.activation(wc_out[:, 0:3, :], UNION[0], ACT.Copy)
                act.activation(wc_out[:, 3:4, :], UNION[1], ACT.Copy).then_inc(setup_sb, 1)
                copied(10, vT[:, :, :], ps_tok2[:, 0, 0:HP * KA].rearrange("p (h k) -> p h k", k=KA))

            def qk_split(b):
                if b:
                    return
                act.wait_ge(qk_rest_ready, 1)
                act.activation(qk_parts[0:KA, 1, :], qk_rest[:, :], ACT.Copy).then_inc(qk_mid, 1)

            def high_w(s):
                for k in range(CHUNK_STEP * s, min(CHUNK_STEP * (s + 1), len(CHUNKS))):
                    kind, n = CHUNKS[k]
                    high, low = split_of(kind, n)
                    if kind == "w1":
                        act.wait_ge(wshifted, n + 1)
                    act.wait_ge(wload[k % 2], 16 * loads_before(k))
                    if kind == "b2":
                        act.wait_ge(zeroed, 2)
                        act.activation(high, wraw[0:1, k % 2, :], ACT.Copy, scale=WS * WS)
                        act.activation(low, wraw[32:33, k % 2, :], ACT.Copy, scale=WS * WS).then_inc(whigh, 1)
                    else:
                        act.activation(high, wraw[:, k % 2, :], ACT.Copy, scale=WS).then_inc(whigh, 1)

            def copy_s(b):
                act.wait_ge(done["tokens"], b + 1)
                if b >= 2:
                    act.wait_ge(done["kappa"], b - 1)
                act.activation(sT[:, b % 2], TOKS[:, :, 0:KA], ACT.Copy).then_inc(done["copy_s"], 1)

            def root(dst, src, up):
                step(act, act.activation(dst, src, ACT.Ln, scale=2.0 ** up))
                n = dst.shape[0]
                bias = {0: 0.0, UP_TOKEN: lift[0:n, 0:1], UP_HEAD: lift[0:n, 1:2]}[up]
                return act.activation(dst, dst, ACT.Exp, bias=bias, scale=-0.5)

            def rho(b):
                act.wait_ge(done["var"], b + 1)
                root(kap[:, 3, :], kap[:, 2, :], UP_TOKEN).then_inc(done["rho"], 1)

            def rho2_(b):
                act.wait_ge(done["var2"], b + 1)
                root(rho2[:, 2, :], rho2[:, 1, :], 0).then_inc(done["rho2"], 1)

            def roots(b):
                act.wait_ge(done["clamp"], b + 1)
                if b >= 1:
                    act.wait_ge(sim_read, b)
                step(act, root(norm_r[:, :], norm_c[:, :], UP_HEAD))
                act.activation(norm_t[:, :], norm_r[:, :], ACT.Square).then_inc(done["roots"], 1)

            def copy_gram(b):
                act.wait_ge(done["gram"], b + 1)
                if b == 0:
                    act.wait_ge(parts_zeroed, 2)
                if b >= 2:
                    act.wait_ge(done["qk"], b - 1)
                act.activation(g_sb[0:KA, b % 2, 0, :], GRAM, ACT.Copy)
                act.activation(g_sb[64:KS, b % 2, 1, :], GRAM, ACT.Copy).then_inc(done["copy_gram"], 1)

            def gram_mid(b):
                act.wait_ge(done["gram_rest"], b + 1)
                act.activation(g_mid[:, b % 2, :], g_rest[:, b % 2, :], ACT.Copy)
                act.activation(g_sb[64:KS, b % 2, 0, :], g_rest[:, b % 2, :], ACT.Copy).then_inc(done["gram_mid"], 1)

            def copy_turn(b):
                act.wait_ge(done["turn"], b + 1)
                act.activation(SR[64:KS, b, :].rearrange("p (a t) -> p a t", a=2),
                               ps_tok2[0:KA, :, 0:3 * TOK], ACT.Copy).then_inc(done["copy_turn"], 1)

            def copy_k(b):
                act.wait_ge(done["qk"], b + 1)
                if b >= 2:
                    act.wait_ge(done["sim"], b - 1)
                    act.wait_ge(done["prods"], 2 * (b - 1))
                act.activation(k_sb[:, b % 2, :], ps_qk[0:KA, 1, :], ACT.Copy).then_inc(done["copy_k"], 1)

            def exps(b):
                act.wait_ge(done["scores"], b + 1)
                if b >= 2:
                    act.wait_ge(done["probs"], b - 1)
                for p in range(HP):
                    at = slice(DH * p, DH * p + DH)
                    last = act.activation(ez[:, b % 2, at], z_sb[:, b % 2, at], ACT.Exp, bias=zshift[:, b % 2, p:p + 1],
                                          scale=zscale[:, b % 2, p:p + 1], accum_out=zs[:, b % 2, p:p + 1])
                last.then_inc(done["exps"], 1)

            def copy_u(b):
                act.wait_ge(done["union"], b + 1)
                if b >= 2:
                    act.wait_ge(done["px"], b - 1)
                act.activation(u_sb[:, b % 2, 0:3, :], UNION[0], ACT.Copy)
                act.activation(u_sb[:, b % 2, 3:4, :], UNION[1], ACT.Copy).then_inc(done["copy_u"], 1)

            def copy_px(b):
                act.wait_ge(done["px"], b + 1)
                if b >= 2:
                    act.wait_ge(done["tokens2"], b - 1)
                act.activation(R[64:KS, b % 2, :], PX, ACT.Copy).then_inc(done["copy_px"], 1)

            def square(b):
                act.wait_ge(done["tokens2"], b + 1)
                if b >= 1:
                    act.wait_ge(done["norm2"], b)
                for j in range(NT):
                    last = act.activation(sq_sb[:, j, :], TOK2[:, j // 3, j % 3, 0:D], ACT.Square,
                                          accum_out=rho2[:, 0, j:j + 1])
                last.then_inc(done["square"], 1)

            def split_hi(b):
                act.wait_ge(x2_ready, b + 1)
                if b >= 2:
                    act.wait_ge(sent[b % 2], 2 * RSENT * (b // 2))
                act.activation(xrow16[:, b % 2, :, 0:D], x2[:, b % 2], ACT.Copy).then_inc(done["split_hi"], 1)

            def exp_logits(b):
                act.wait_ge(lg_ready, b + 1)
                if b >= 2:
                    act.wait_ge(done["shares"], b - 1)
                act.activation(exl[:, b % 2], tops[:, b % 2], ACT.Exp).then_inc(done["exp_logits"], 1)

            here = dict(rest=rest, qk_split=qk_split, high_w=high_w, copy_s=copy_s, rho=rho, rho2=rho2_, roots=roots, copy_gram=copy_gram, gram_mid=gram_mid, copy_turn=copy_turn, copy_k=copy_k, exps=exps,
                        copy_u=copy_u, copy_px=copy_px, square=square, split_hi=split_hi, exp_logits=exp_logits)
            for name, b in SCHEDULE:
                if name in here:
                    here[name](b)

            def copy_x(t, u):
                act.wait_ge(x_ps, t + 1)
                if since(t, 2):
                    act.wait_ge(h_ps, t - 1)
                act.activation(xT[:, u].rearrange("p s n -> p (s n)"), XPS[u][:, 0:2 * TILE], ACT.Copy).then_inc(x_sbuf, 1)

            def high(t, u):
                act.wait_ge(h_ps, t + 1)
                if since(t, 2):
                    act.wait_ge(y_ps, t - 1)
                act.activation(hhi[:, u].rearrange("p f n -> p (f n)"), HPS[u], ACT.Relu).then_inc(h_high, 1)

            copy_x(0, 0)
            copy_x(1, 1)

            def tile(t, i, v):
                high(t, v % 2)
                copy_x(t + 2, v % 2)

            over_tiles(act, tile, 0, NTILES - 2)
            for t in range(NTILES - 2, NTILES):
                high(t, t % 2)

        @block.vector
        def _(dve):
            step = chained(ch_dve)
            for g in range(2):
                step(dve, dve.memset(diff[:, g, 0:1], 0.0))
                dve.wait_ge(load[f"x{g}"], 16)
                step(dve, dve.tensor_tensor(diff[:, g, 1:T], x_sb[:, g, 1:T], x_sb[:, g, 0:T - 1], ALU.subtract))
                step(dve, dve.tensor_scalar(rl0[:, g:g + 1], diff[:, g, T - 1:T], 10.0, None, ALU.mult))
                dve.wait_ge(consts, 9)
                dve.tensor_tensor_scan(lr[:, g, :], decay[:, :].to_broadcast((128, T)), diff[:, g, :], 0.0, ALU.mult,
                                       ALU.add).then_inc(scans, 1)
                dve.tensor_tensor_scan(rl[:, g, ::-1], decay[:, :].to_broadcast((128, T)), diff[:, g, ::-1], rl0[:, g:g + 1],
                                       ALU.mult, ALU.add).then_inc(scans, 1)
                if g == 0:
                    dve.wait_ge(load["wve"], 16)
                    dve.wait_ge(load["bve"], 16)
                    dve.tensor_scalar(vext[:, 0:C], wve_sb[:, :], 0.05, None, ALU.mult).then_inc(setup_dve, 1)
                    dve.wait_ge(consts, 13)
                    dve.tensor_scalar(cmat[:, 0:D], ident[:, :], 1.0 / D, None, ALU.subtract).then_inc(setup_dve, 1)
                    dve.tensor_scalar(cmat[:, D:D + 1], ones[:, 0:1], 1.0 / D, None, ALU.mult).then_inc(setup_dve, 1)
                    dve.tensor_copy(ik[:, 0:KA], ident[0:KA, 0:KA]).then_inc(setup_dve, 1)
                    dve.wait_ge(load["gamma"], 16)
                    dve.wait_ge(load["wqkv"], 16)
                    dve.tensor_scalar(wg_sb[:, :], wqkv_sb[:, :], gamma_sb[:, :], None, ALU.mult).then_inc(setup_dve, 1)
                    dve.wait_ge(load["blin"], 16)
                    dve.wait_ge(setup_sb, 2)
                    dve.tensor_tensor(wc1T[:, C:KA], wc1T[:, C:KA], blin_sb[:, :], ALU.add).then_inc(setup_dve, 1)

            def qk_split(b):
                if b:
                    return
                dve.wait_ge(parts_zeroed, 2)
                dve.wait_ge(setup_sb, 9)
                dve.tensor_copy(qk_parts[64:KS, 0, :], qk_w[:, :])
                dve.wait_ge(qk_high, 1)
                dve.tensor_tensor(qk_rest[:, :], qk_w[:, :], qk_parts[0:KA, 0, :], ALU.subtract).then_inc(qk_rest_ready, 1)
                dve.wait_ge(qk_rest_ready, 1)
                dve.tensor_copy(qk_parts[64:KS, 1, :], qk_rest[:, :])
                dve.wait_ge(qk_mid, 1)
                dve.tensor_tensor(qk_parts[64:KS, 2, :], qk_rest[:, :], qk_parts[0:KA, 1, :],
                                  ALU.subtract).then_inc(qk_low, 1)

            def low_w(s):
                for k in range(CHUNK_STEP * s, min(CHUNK_STEP * (s + 1), len(CHUNKS))):
                    kind, n = CHUNKS[k]
                    high, low = split_of(kind, n)
                    if kind == "b2":
                        high = low
                    r = slice(32, 33) if kind == "b2" else slice(0, 128)
                    dve.wait_ge(whigh, k + 1)
                    dve.scalar_tensor_tensor(low, wraw[r, k % 2, :], WS * WS if kind == "b2" else WS, high,
                                             ALU.mult, ALU.subtract).then_inc(wlow, 1)

            def var(b):
                dve.wait_ge(done["copy_s"], b + 1)
                if b >= 1:
                    dve.wait_ge(done["kappa"], b)
                dve.tensor_tensor(quad[:, :, :], TOKS[:, :, KA:2 * KA], sT[:, b % 2], ALU.mult).then_inc(quad_read, 1)
                dve.wait_ge(quad_read, b + 1)
                step(dve, dve.tensor_reduce(kap[:, 0, :], quad[:, :, :], AX, ALU.add))
                step(dve, dve.tensor_scalar(kap[:, 1, :], kap[:, 0, :], EPS, TINY2 / D, ALU.add, ALU.mult))
                dve.tensor_tensor(kap[:, 2, :], kap[:, 0, :], kap[:, 1, :], ALU.max).then_inc(done["var"], 1)

            def polish(y, square, t):
                step(dve, dve.tensor_tensor(t, y, y, ALU.mult))
                step(dve, dve.scalar_tensor_tensor(t, t, -0.5, square, ALU.mult, ALU.mult))
                step(dve, dve.scalar_tensor_tensor(y, t, 1.5, y, ALU.add, ALU.mult))

            def kappa(b):
                dve.wait_ge(done["rho"], b + 1)
                polish(kap[:, 3, :], kap[:, 2, :], kap[:, 1, :])
                if b >= 2:
                    dve.wait_ge(done["turn"], b - 1)
                dve.tensor_tensor(spT[:, b % 2], sT[:, b % 2],
                                  kap[:, 3, :].rearrange("p (j a) -> p j a", a=1).to_broadcast((TOK, NT, KA)),
                                  ALU.mult).then_inc(done["kappa"], 1)

            def gram_rest(b):
                dve.wait_ge(done["copy_gram"], b + 1)
                dve.tensor_tensor(g_rest[:, b % 2, :], GRAM, g_sb[0:KA, b % 2, 0, :], ALU.subtract).then_inc(done["gram_rest"], 1)

            def gram_low(b):
                dve.wait_ge(done["gram_mid"], b + 1)
                dve.tensor_tensor(g_sb[0:KA, b % 2, 1, :], g_rest[:, b % 2, :], g_mid[:, b % 2, :],
                                  ALU.subtract).then_inc(done["gram_low"], 1)

            def prods(b):
                dve.wait_ge(done["qk"], b + 1)
                if b >= 2:
                    dve.wait_ge(done["norms"], b - 1)
                dve.tensor_tensor(prod[:, b % 2, 0:HD], ps_qk[0:KA, 0, :], qk_w[:, 0:HD],
                                  ALU.mult).then_inc(done["prods"], 1)
                dve.wait_ge(done["copy_k"], b + 1)
                dve.tensor_tensor(prod[:, b % 2, HD:2 * HD], k_sb[:, b % 2, :], qk_w[:, HD:2 * HD],
                                  ALU.mult).then_inc(done["prods"], 1)

            def clamp(b):
                dve.wait_ge(done["norms"], b + 1)
                dve.tensor_scalar(norm_c[:, :], ps_norm[:, 0:HP * DH + HP], TINY2, None,
                                  ALU.max).then_inc(done["clamp"], 1)

            def scores(b):
                dve.wait_ge(done["roots"], b + 1)
                nk, nq = norm_r[:, 0:HP * DH], norm_r[:, HP * DH:HP * DH + HP]
                step(dve, dve.scalar_tensor_tensor(norm_t[:, :], norm_t[:, :], -0.5, norm_c[:, :], ALU.mult, ALU.mult))
                step(dve, dve.scalar_tensor_tensor(norm_r[:, :], norm_t[:, :], 1.5, norm_r[:, :], ALU.add, ALU.mult))
                if b == 0:
                    dve.wait_ge(ch_act, 2)
                if b >= 2:
                    dve.wait_ge(done["exps"], b - 1)
                step(dve, dve.scalar_tensor_tensor(zscale[:, b % 2, :], nq, 8.0, texp_sb[:, :], ALU.mult, ALU.mult))
                dve.wait_ge(done["sim"], b + 1)
                dve.tensor_tensor(z_sb[:, b % 2, :], SIM, nk, ALU.mult).then_inc(sim_read, 1)
                dve.wait_ge(sim_read, b + 1)
                step(dve, dve.tensor_reduce(zm[:, :], z_sb[:, b % 2, :].rearrange("p (h e) -> p h e", h=HP), AX, ALU.max))
                dve.scalar_tensor_tensor(zshift[:, b % 2, :], zm[:, :], -1.0, zscale[:, b % 2, :], ALU.mult,
                                         ALU.mult).then_inc(done["scores"], 1)

            def probs(b):
                dve.wait_ge(done["exps"], b + 1)
                e3 = ez[:, b % 2, :].rearrange("p (h e) -> p h e", h=HP)
                step(dve, dve.reciprocal(zs[:, b % 2, :], zs[:, b % 2, :]))
                if b >= 2:
                    dve.wait_ge(done["union"], b - 1)
                for i in range(2):
                    r = slice(64 * i, 64 * i + 64)
                    dve.tensor_tensor(attn[r, b % 2, :, r], e3[r], zs[r, b % 2, :].rearrange(
                        "p (h e) -> p h e", e=1).to_broadcast((64, HP, DH)), ALU.mult).then_inc(done["probs"], 1)

            def var2(b):
                dve.wait_ge(done["square"], b + 1)
                wide = lambda a, n: a.rearrange("p (a j k) -> p a j k", a=2, k=1).to_broadcast((TOK, 2, 3, n))
                four = lambda t: t.rearrange("p (a j) n -> p a j n", a=2)
                dve.tensor_scalar(rho2[:, 1, :], rho2[:, 0, :], 1.0 / D, EPS, ALU.mult,
                                  ALU.add).then_inc(done["var2"], 1)
                step(dve, dve.tensor_copy(mean2[:, :].rearrange("p (a j) -> p a j", a=2), TOK2[:, :, :, D]))
                dve.tensor_tensor(four(h2[:, NT * b:NT * b + NT, :]), TOK2[:, :, :, 0:D],
                                  wide(mean2[:, :], D), ALU.add).then_inc(h2_read, 1)

            def norm2(b):
                wide = lambda a, n: a.rearrange("p (a j k) -> p a j k", a=2, k=1).to_broadcast((TOK, 2, 3, n))
                four = lambda t: t.rearrange("p (a j) n -> p a j n", a=2)
                dve.wait_ge(done["rho2"], b + 1)
                polish(rho2[:, 2, :], rho2[:, 1, :], rho2[:, 0, :])
                if b >= 2:
                    dve.wait_ge(done["split_lo"], b - 1)
                dve.tensor_tensor(four(x2[:, b % 2])[:, :, :, 1:D], TOK2[:, :, :, 1:D], wide(rho2[:, 2, :], D - 1),
                                  ALU.mult).then_inc(x2_ready, 1)
                dve.tensor_tensor(four(lg[:, b % 2]), TOK2[:, :, :, D + 1:NC2], wide(rho2[:, 2, :], E),
                                  ALU.mult).then_inc(done["norm2"], 1)

            def top2(b):
                l, o, tail = lg[:, b % 2], oh[:, b % 2], xrow[:, b % 2, :, D:ROWF]
                if b == 0:
                    dve.wait_ge(load["br"], 16)
                if b >= 2:
                    dve.wait_ge(sent[b % 2], 2 * RSENT * (b // 2))
                    dve.wait_ge(done["exp_logits"], b - 1)
                if b >= 1:
                    dve.wait_ge(done["shares"], emitted_before("top2", b, "shares"))
                dve.wait_ge(done["norm2"], b + 1)
                bias = br_sb[0:TOK, :].rearrange("p (j e) -> p j e", j=1).to_broadcast((TOK, NT, E))
                step(dve, dve.tensor_tensor(l, l, bias, ALU.add))
                for j in range(NT):
                    last = dve.max(top[:, j, :], l[:, j, :])
                step(dve, last)
                dve.tensor_tensor(tops[:, b % 2], top[:, :, :], top[:, :, 0:1].to_broadcast((TOK, NT, E)),
                                  ALU.subtract).then_inc(lg_ready, 1)
                for j in range(NT):
                    last = dve.max_index(topi[:, j, :], top[:, j, :], l[:, j, :])
                step(dve, last)
                step(dve, dve.tensor_copy(tail[:, :, 0:2], topi[:, :, 0:2]))
                ids = exp_ids[0:TOK, :].rearrange("p (j e) -> p j e", j=1).to_broadcast((TOK, NT, E))
                for c in range(2):
                    last = dve.tensor_tensor(o[:, c], ids, tail[:, :, c:c + 1].to_broadcast((TOK, NT, E)), ALU.is_equal)
                step(dve, last)
                dve.tensor_tensor(mask[:, b % 2], o[:, 0], o[:, 1], ALU.add).then_inc(done["top2"], 1)

            def shares(b):
                tail = xrow[:, b % 2, :, D:ROWF]
                dve.wait_ge(done["exp_logits"], b + 1)
                step(dve, dve.tensor_reduce(sums[:, 0, :], exl[:, b % 2], AX, ALU.add))
                dve.wait_ge(done["top2"], b + 1)
                dve.tensor_reduce(mrow[:, :], mask[:, b % 2].rearrange("p j e -> p e j"), AX, ALU.add)
                step(dve, dve.tensor_scalar(sums[:, 0, :], sums[:, 0, :], WS * WS, None, ALU.mult))
                dve.tensor_tensor(msum[:, b + 1, :], mrow[:, :], msum[:, b, :], ALU.add).then_inc(counted, 1)
                step(dve, dve.reciprocal(tail[:, :, 2], sums[:, 0, :]))
                dve.tensor_tensor(tail[:, :, 3], exl[:, b % 2, :, 1], tail[:, :, 2], ALU.mult).then_inc(done["shares"], 1)

            mid = lambda a, n: a.rearrange("p (e k) -> p e k", k=1).to_broadcast((128, a.shape[1], n))
            last = lambda a, n: a.rearrange("p (e k) -> p e k", e=1).to_broadcast((128, n, a.shape[1]))

            def tabulate(n, lo, hi):
                t = slice(lo, hi)
                p, q = (a[:, 0:(hi - lo) * n].rearrange("p (t g) -> p t g", g=n) for a in (past, past2))
                step(dve, dve.tensor_tensor_scan(ends[:, 0:n], ones[:, 0:n], groups[:, 0:n], 0.0, ALU.mult, ALU.add))
                step(dve, dve.tensor_tensor(skip[:, 0:n], starts[:, 1:n + 1], starts[:, 0:n], ALU.subtract))
                step(dve, dve.scalar_tensor_tensor(skip[:, 0:n], groups[:, 0:n], -float(TILE), skip[:, 0:n],
                                                   ALU.mult, ALU.add))
                step(dve, dve.tensor_tensor(p, mid(tindex[:, t], n), last(ends[:, 0:n], hi - lo), ALU.is_ge))
                dve.tensor_reduce(group[:, lo + 1:hi + 1], p, AX, ALU.add)
                step(dve, dve.tensor_tensor(q, p, last(skip[:, 0:n], hi - lo), ALU.mult))
                step(dve, dve.tensor_reduce(first_row[:, t], q, AX, ALU.add))
                dve.scalar_tensor_tensor(table[:, t, 0], tindex[:, t], float(TILE), first_row[:, t], ALU.mult, ALU.add)
                step(dve, dve.tensor_scalar(et[:, t], group[:, lo + 1:hi + 1], float(E), -float(E), ALU.is_ge, ALU.mult))
                step(dve, dve.tensor_tensor(et[:, t], et[:, t], group[:, lo + 1:hi + 1], ALU.add))
                dve.tensor_scalar(table[:, t, 1], et[:, t], float(E - 1), float(D), ALU.min, ALU.mult)
                step(dve, dve.tensor_tensor(changed[:, t], group[:, lo + 1:hi + 1], group[:, lo:hi], ALU.is_gt))
                dve.tensor_scalar(table[:, t, 2], changed[:, t], float(LANDED), None, ALU.mult).then_inc(table_ready, 1)

            def tabulate_early():
                step(dve, dve.memset(group[:, 0:1], 0.0))
                step(dve, dve.tensor_copy(starts[:, 0:E], ebase[:, :]))
                step(dve, dve.memset(starts[:, E:2 * E + 1], float(E * REGION)))
                step(dve, dve.tensor_tensor(over[:, :, :], mid(cnt[:, :], KT), last(ksteps[:, :], E), ALU.is_ge))
                step(dve, dve.tensor_reduce(groups[:, 0:E], over[:, :, 1:KT], AX, ALU.add))
                tabulate(E, 0, EARLY_TILES)

            def place(b):
                dve.wait_ge(done["rank"], b + 1)
                base = ebase[0:TOK, :].rearrange("p (j e) -> p j e", j=1).to_broadcast((TOK, NT, E))
                if b == EARLY:
                    step(dve, dve.tensor_copy(cnt[:, :], COUNT))
                dve.tensor_tensor(rk[:, :, :], RANK, base, ALU.add).then_inc(rank_read, 1)
                dve.wait_ge(rank_read, b + 1)
                for c in range(2):
                    last = dve.tensor_tensor(rk2[:, c], oh[:, b % 2, c], rk[:, :, :], ALU.mult)
                step(dve, last)
                step(dve, dve.tensor_reduce(posf[:, :, :], rk2[:, :, :, :], AX, ALU.add))
                if b >= 2:
                    dve.wait_ge(sent[b % 2], 2 * RSENT * (b // 2))
                dve.wait_ge(done["shares"], b + 1)
                dve.tensor_copy(pos[:, b % 2], posf[:, :, :]).then_inc(done["place"], 1)
                if b == EARLY:
                    tabulate_early()

            here = dict(qk_split=qk_split, gram_rest=gram_rest, gram_low=gram_low, low_w=low_w, var=var, kappa=kappa, prods=prods, clamp=clamp, var2=var2, scores=scores, probs=probs, norm2=norm2, top2=top2, shares=shares, place=place)
            for name, b in SCHEDULE:
                if name in here:
                    here[name](b)

            dve.wait_ge(count_ps, 1)
            dve.tensor_copy(cnt[:, :], COUNT).then_inc(count_read, 1)
            dve.wait_ge(count_read, 1)
            step(dve, dve.tensor_tensor(over[:, :, :], mid(cnt[:, :], KT), last(ksteps[:, :], E), ALU.is_gt))
            dve.tensor_tensor(pads[:, :], cnt[:, :], ebase[:, :], ALU.add).then_inc(pads_ready, 1)
            step(dve, dve.tensor_reduce(tiles[:, :], over[:, :, :], AX, ALU.add))
            step(dve, dve.tensor_tensor(groups[:, E:2 * E], tiles[:, :], groups[:, 0:E], ALU.subtract))
            step(dve, dve.scalar_tensor_tensor(starts[:, E:2 * E], groups[:, 0:E], float(TILE), ebase[:, :],
                                               ALU.mult, ALU.add))
            tabulate(2 * E, EARLY_TILES, NTILES)

            def weigh(t, i, v):
                u = v % 2
                dve.wait_ge(x_in[v], 16 * i + 16)
                if since(t, XB):
                    dve.wait_ge(added[u], LANDED * (XB // 2 * i + v // 2 - XB // 2 + 1))
                tail = xin[:, v, :, D:ROWF]
                for r in range(BLK):
                    ins = dve.scalar_tensor_tensor(mine[:, u, r], tail[:, r, 0:2], et[:, bass.ds(t, 1)], tail[:, r, 2:4],
                                                   ALU.is_equal, ALU.mult)
                ins.then_inc(weigh1, 1)
                dve.tensor_scalar(dst[:, v], tail[:, :, 4], FAR, None, ALU.add)
                dve.wait_ge(weigh1, t + 1)
                dve.tensor_reduce(cw[:, v, :, 0], mine[:, u], AX, ALU.add).then_inc(weights, 1)

            def low(t, u):
                dve.wait_ge(h_high, t + 1)
                if since(t, 2):
                    dve.wait_ge(y_ps, t - 1)
                dve.scalar_tensor_tensor(hlo[:, u].rearrange("p f n -> p (f n)"), HPS[u], 0.0,
                                         hhi[:, u].rearrange("p f n -> p (f n)"), ALU.max,
                                         ALU.subtract).then_inc(h_low, 1)

            def scale_y(t, u, v):
                dve.wait_ge(y_ps, t + 1)
                dve.tensor_tensor(ysb[:, v], YPS[u].rearrange("p (r n) -> p r n", n=D),
                                  cw[:, v, :, :].to_broadcast((128, BLK, D)), ALU.mult).then_inc(y_sbuf, 1)

            def tile(t, i, v):
                low(t, v % 2)
                if since(t, 1):
                    scale_y(t - 1, (v + 1) % 2, (v - 1) % XB)
                weigh(t + 1, i + (v + 1) // XB, (v + 1) % XB)

            weigh(0, 0, 0)
            over_tiles(dve, tile, 0, NTILES - 1)
            low(NTILES - 1, (NTILES - 1) % 2)
            for t in range(NTILES - 2, NTILES):
                scale_y(t, t % 2, t % XB)

        @block.tensor
        def _(pe):
            def made(ins):
                ins.then_inc(setup_ps, 1)

            pe.wait_ge(consts, 18)
            pe.wait_ge(load["wlin"], 16)
            made(pe.transpose(ps_qk[:, 0, 0:D], wlin_sb[:, :], ident[:, :]))
            pe.wait_ge(setup_sb, 1)
            pe.wait_ge(setup_dve, 4)
            made(pe.matmul(ps_qk[:, 1, 0:KA], lhsT=wlinT[:, :], rhs=vext[:, :], start=True, stop=True))
            pe.wait_ge(load["wr"], 16)
            made(pe.matmul(ps_norm[:, 0:E], lhsT=cmat[:, 0:D], rhs=wr_sb[:, :], start=True, stop=True))
            pe.wait_ge(setup_dve, 6)
            made(pe.matmul(ps_sim[:, 0:KA], lhsT=cmat[:, 0:D], rhs=wc1T[:, :], start=True, stop=True))
            pe.wait_ge(setup_sb, 4)
            made(pe.matmul(ps_tok[0:KA, 0:NC2], lhsT=wc1T[:, :], rhs=cmat[:, :], start=True, stop=True))
            made(pe.matmul(ps_small[0:KA, 0:KA], lhsT=aT[:, :], rhs=aT[:, :], start=True, stop=True))
            for i in range(2):
                made(pe.matmul(ps_qk[0:KA, i, :], lhsT=aT[:, :], rhs=wg_sb[:, HD * i:HD * i + HD], start=True, stop=True))

            def rest(b):
                if b:
                    return
                pe.wait_ge(load["wout"], 16)
                for p in range(HP):
                    last = pe.transpose(ps_small[:, D * p:D * p + D], wout_sb[:, p, :], ident[:, :])
                made(last)
                pe.wait_ge(setup_sb, 10)
                for p in range(HP):
                    last = pe.matmul(UNION[p // 3][:, p % 3, :], lhsT=woutT[:, p, :], rhs=cmat[:, :], start=True, stop=True)
                made(last)
                for p in range(HP):
                    last = pe.matmul(ps_tok2[:, 0, KA * p:KA * p + KA], lhsT=wg_sb[:, 2 * HD + 128 * p:2 * HD + 128 * p + 128],
                                     rhs=aT[:, :], start=True, stop=True)
                made(last)

            def tokens(b):
                pe.wait_ge(smooth, b + 1)
                pe.wait_ge(ch_pool, b + 1)
                if b == 0:
                    pe.wait_ge(setup_sb, 7)
                else:
                    pe.wait_ge(done["gram_rest"], b)
                for j in range(NT):
                    last = pe.matmul(TOKS[:, j, :], lhsT=SR[0:KA, b, TOK * j:TOK * j + TOK], rhs=ik[:, :],
                                     start=True, stop=True)
                last.then_inc(done["tokens"], 1)

            def gram(b):
                pe.wait_ge(done["kappa"], b + 1)
                for j in range(NT):
                    last = pe.matmul(GRAM, lhsT=spT[:, b % 2, j, :], rhs=spT[:, b % 2, j, :],
                                     start=(j == 0), stop=(j == NT - 1))
                last.then_inc(done["gram"], 1)

            def turn(b):
                if b == 0:
                    pe.wait_ge(setup_sb, 12)
                n2 = emitted_before("turn", b, "tokens2")
                if n2:
                    pe.wait_ge(done["norm2"], n2)
                if b >= 1:
                    pe.wait_ge(done["copy_turn"], b)
                for j in range(NT):
                    last = pe.transpose(ps_tok2[0:KA, j // 3, TOK * (j % 3):TOK * (j % 3) + TOK],
                                        spT[:, b % 2, j, :], ident[0:TOK, 0:TOK])
                last.then_inc(done["turn"], 1)

            def qk(b):
                pe.wait_ge(done["gram_low"], b + 1)
                if b == 0:
                    pe.wait_ge(setup_sb, 12)
                    pe.wait_ge(qk_low, 1)
                if b >= 1:
                    pe.wait_ge(done["prods"], 2 * b)
                    pe.wait_ge(done["copy_k"], b)
                nu = emitted_before("qk", b, "union")
                if nu:
                    pe.wait_ge(done["copy_u"], nu)
                for i in range(2):
                    for n, g in enumerate((0, 0, 1)):
                        last = pe.matmul(ps_qk[0:KA, i, :], lhsT=g_sb[:, b % 2, g, :],
                                         rhs=qk_parts[:, n, HD * i:HD * i + HD], start=(n == 0), stop=(n == 2))
                last.then_inc(done["qk"], 1)

            def norms(b):
                pe.wait_ge(done["prods"], 2 * b + 2)
                if b >= 1:
                    pe.wait_ge(done["clamp"], b)
                for p in range(HP):
                    pe.matmul(NQ[:, p:p + 1], lhsT=prod[:, b % 2, 128 * p:128 * p + 128], rhs=ones[0:KA, 0:1],
                              start=True, stop=True)
                kp = prod[:, b % 2, HD:2 * HD].rearrange("k (p i e) -> k i p e", i=2, e=DH)
                for i in range(2):
                    last = pe.matmul(NK[64 * i:64 * i + 64, :], lhsT=ones[0:KA, 0:64], rhs=kp[:, i], start=True, stop=True)
                last.then_inc(done["norms"], 1)

            def sim(b):
                pe.wait_ge(done["copy_k"], b + 1)
                if b >= 1:
                    pe.wait_ge(sim_read, b)
                for h in range(H):
                    i, p = h % 2, h // 2
                    last = pe.matmul(SIM[64 * i:64 * i + 64, DH * p:DH * p + DH], lhsT=qk_w[:, DH * h:DH * h + DH],
                                     rhs=k_sb[:, b % 2, DH * h:DH * h + DH], start=True, stop=True)
                last.then_inc(done["sim"], 1)

            def union(b):
                pe.wait_ge(done["probs"], 2 * b + 2)
                pe.wait_ge(done["prods"], 2 * emitted_before("union", b, "prods"))
                if b >= 1:
                    pe.wait_ge(done["copy_u"], b)
                for p in range(HP):
                    last = pe.matmul(UNION[p // 3][:, p % 3, :], lhsT=attn[:, b % 2, p, :], rhs=wc_out[:, p, :],
                                     start=True, stop=True)
                last.then_inc(done["union"], 1)

            def bank_small(name, b):
                n = emitted_before(name, b, "px")
                if n:
                    pe.wait_ge(done["copy_px"], n)
                n = emitted_before(name, b, "rank")
                if n:
                    pe.wait_ge(rank_read, n)

            def px(b):
                pe.wait_ge(done["copy_u"], b + 1)
                bank_small("px", b)
                for p in range(HP):
                    last = pe.matmul(PX, lhsT=vT[:, p, :], rhs=u_sb[:, b % 2, p, :], start=(p == 0), stop=(p == HP - 1))
                last.then_inc(done["px"], 1)

            def tokens2(b):
                pe.wait_ge(done["copy_px"], b + 1)
                pe.wait_ge(done["copy_turn"], emitted_before("tokens2", b, "turn"))
                if b >= 1:
                    pe.wait_ge(done["norm2"], b)
                    pe.wait_ge(done["square"], b)
                for j in range(NT):
                    last = pe.matmul(TOK2[:, j // 3, j % 3, :], lhsT=SR[:, b, TOK * j:TOK * j + TOK], rhs=R[:, b % 2, :],
                                     start=True, stop=True)
                last.then_inc(done["tokens2"], 1)

            def rank(b):
                pe.wait_ge(done["top2"], b + 1)
                if b >= 1:
                    pe.wait_ge(counted, b)
                bank_small("rank", b)
                if b == EARLY:
                    pe.matmul(COUNT, lhsT=onesb[0:TOK, :], rhs=msum[:, b, :], start=True, stop=True)
                pe.matmul(RANK, lhsT=tri[0:TOK, 0:TOK], rhs=mask[:, b % 2], start=True, stop=False)
                for j in range(NT - 1):
                    pe.matmul(RANK[:, j + 1:NT, :], lhsT=onesb[0:TOK, 0:TOK],
                              rhs=mask[:, b % 2, j:j + 1, :].to_broadcast((TOK, NT - 1 - j, E)), start=False, stop=False)
                pe.matmul(RANK, lhsT=onesb[0:TOK, 0:TOK],
                          rhs=msum[:, b:b + 1, :].to_broadcast((TOK, NT, E)), start=False,
                          stop=True).then_inc(done["rank"], 1)

            here = dict(rest=rest, tokens=tokens, gram=gram, turn=turn, qk=qk, norms=norms, sim=sim, union=union,
                        px=px, tokens2=tokens2, rank=rank)
            for name, b in SCHEDULE:
                if name in here:
                    here[name](b)

            pe.wait_ge(counted, B)
            pe.wait_ge(rank_read, B)
            pe.matmul(COUNT, lhsT=onesb[0:TOK, :], rhs=msum[:, B, :], start=True, stop=True).then_inc(count_ps, 1)
            pe.wait_ge(table_ready, 1)
            pe.wait_ge(done["norm2"], B)
            pe.wait_ge(done["copy_u"], B)
            pe.wait_ge(count_read, 1)
            pe.wait_ge(wlow, len(CHUNKS))

            def turn_x(t, i, v):
                u = v % 2
                pe.wait_ge(x_in[v], 16 * i + 16)
                if since(t, 2):
                    pe.wait_ge(x_sbuf, t - 1)
                for s in range(2):
                    for r in range(BLK):
                        last = pe.transpose(XPS[u][:, TILE * s + 128 * r:TILE * s + 128 * r + 128],
                                            xin16[:, v, r, D * s:D * s + D], ident16[:, :])
                last.then_inc(x_ps, 1)

            expert_at = [pe.alloc_register(f"expert_at{u}") for u in range(2)]

            def chunk(weights, f, at):
                return weights[:, 128 * f:E * F - 128 * (FC - 1 - f)][:, bass.ds(at, 128)]

            def hidden(t, u):
                pe.reg_load(expert_at[u], table[0:1, bass.ds(t, 1), 1:2])
                at = pe.snap(expert_at[u], min_val=0, max_val=(E - 1) * D) * FC
                pe.wait_ge(x_sbuf, t + 1)
                if since(t, 2):
                    pe.wait_ge(h_low, t - 1)
                for f in range(FC):
                    to = HPS[u][:, TILE * f:TILE * f + TILE]
                    high = chunk(w1h, f, at)
                    pe.matmul(to, lhsT=high, rhs=xT[:, u, 0, :], start=True, stop=False)
                    pe.matmul(to, lhsT=high, rhs=xT[:, u, 1, :], start=False, stop=False)
                    last = pe.matmul(to, lhsT=chunk(w1l, f, at), rhs=xT[:, u, 0, :], start=False, stop=True)
                last.then_inc(h_ps, 1)

            def result(t, u):
                at = pe.snap(expert_at[u], min_val=0, max_val=(E - 1) * D)
                pe.wait_ge(h_low, t + 1)
                if since(t, 2):
                    pe.wait_ge(y_sbuf, t - 1)
                for r in range(BLK):
                    to = YPS[u][:, D * r:D * r + D]
                    for f in range(FC):
                        hi, lo = (h[:, u, f, 128 * r:128 * r + 128] for h in (hhi, hlo))
                        pe.matmul(to, lhsT=hi, rhs=chunk(w2h, f, at * FC), start=(f == 0), stop=False)
                        pe.matmul(to, lhsT=hi, rhs=chunk(w2l, f, at * FC), start=False, stop=False)
                        pe.matmul(to, lhsT=lo, rhs=chunk(w2h, f, at * FC), start=False, stop=False)
                    last = pe.matmul(to, lhsT=ones16[0:64, 0:128], rhs=b2h[:, bass.ds(at, D)], start=False, stop=True)
                last.then_inc(y_ps, 1)

            turn_x(0, 0, 0)
            hidden(0, 0)
            turn_x(1, 0, 1)

            def tile(t, i, v):
                turn_x(t + 2, i + (v + 2) // XB, (v + 2) % XB)
                hidden(t + 1, (v + 1) % 2)
                result(t, v % 2)

            over_tiles(pe, tile, 0, EARLY_TILES - XB)
            pe.wait_ge(table_ready, 2)
            over_tiles(pe, tile, EARLY_TILES - XB, NTILES - 2)
            hidden(NTILES - 1, (NTILES - 1) % 2)
            result(NTILES - 2, NTILES % 2)
            result(NTILES - 1, (NTILES - 1) % 2)


_INS = ["x", "L0_tok_W_ve", "L0_tok_b_ve", "L0_tok_W_lin", "L0_tok_b_lin", "L0_attn_gamma", "L0_attn_w_qkv",
        "L0_attn_temperature", "L0_attn_w_out", "L0_ffn_Wr", "L0_ffn_br", "L0_ffn_W1", "L0_ffn_b1",
        "L0_ffn_W2", "L0_ffn_b2"]


def kernel(**inputs):
    import numpy as _np
    import concourse.bacc as _bacc
    from concourse import mybir as _mybir
    from concourse.bass_utils import run_bass_kernel_spmd as _run

    nc = _bacc.Bacc("TRN2", target_bir_lowering=False, num_devices=1)
    arrays, args = {}, []
    for name in _INS:
        a = _np.ascontiguousarray(inputs[name])
        arrays[f"in_{name}"] = a
        args.append(nc.dram_tensor(f"in_{name}", a.shape, _mybir.dt.from_np(a.dtype), kind="ExternalInput").ap())
    out = nc.dram_tensor("out", (B, T, D), F32, kind="ExternalOutput").ap()
    rows = nc.dram_tensor("rows", (ROWS, ROWF), F32).ap()
    audio_tower(nc, *args, out, rows)
    r = _run(nc, [arrays], core_ids=[0])
    return r.results[0]["out"]
```
